# Optimizing a Trainium2 kernel written in Bass

```python
import numpy as np
import jax
import jax.numpy as jnp

def _softmax(x, axis=-1):
    return jax.nn.softmax(x, axis=axis)

def _gelu(x):
    return jax.nn.gelu(x, approximate=True)

def _silu(x):
    return jax.nn.silu(x)

def _sigmoid(x):
    return jax.nn.sigmoid(x)

def _layernorm(x, axis=-1, eps=1e-05):
    m = jnp.mean(x, axis=axis, keepdims=True)
    v = jnp.var(x, axis=axis, keepdims=True)
    return (x - m) / jnp.sqrt(v + eps)

def _scatter_add(tgt, idx, src, axis=0):
    return tgt.at[idx].add(src)

def _segment_sum(src, seg, n):
    return jax.ops.segment_sum(src, seg, n)
kernel_name = 'mk_adaln_ffn_d2_seqx_r8_a7869b'

def setup_inputs(seed: int=0):
    np.random.seed(seed)
    _w = jnp.asarray

    def _rec_inputs():
        import jax
        import jax.numpy as jnp
        _rk = jax.random.key(seed)
        x = 7.22e-05 + 1 * jax.random.normal(jax.random.fold_in(_rk, 1), (8, 256, 128), jnp.float32)
        _lenS = 256 - jax.random.randint(jax.random.fold_in(_rk, 7), (8,), 0, max(1, 256 // 4) + 1, jnp.int32)
        _lenS2 = 256 - jax.random.randint(jax.random.fold_in(_rk, 8), (8,), 0, max(1, 256 // 4) + 1, jnp.int32)
        cond_8 = jax.random.uniform(jax.random.fold_in(_rk, 11), (8, 8), jnp.float32, 0.0, 0.999837)
        return (x, cond_8)
    x, cond_8 = _rec_inputs()

    def _L0_cond_setup():
        import jax, jax.numpy as jnp
        import numpy as np
        key = jax.random.key(seed)
        k1, k2, k3, k4, k5 = jax.random.split(key, 5)
        B, N, T, O, G = (32, 32, 128, 128, 8)
        x = jax.random.normal(k1, (B, N, T), dtype=jnp.float32)
        y = jax.random.uniform(k2, (B, G), dtype=jnp.float32)
        weight = jax.random.normal(k3, (G, O, T), dtype=jnp.float32) * (1.0 / np.sqrt(T))
        mask = jax.random.uniform(k4, (O, T), dtype=jnp.float32)
        bias = jax.random.normal(k5, (O,), dtype=jnp.float32)
        return {'x': x, 'y': y, 'weight': weight, 'mask': mask, 'bias': bias}
    _L0_cond_all = _L0_cond_setup()
    _L0_cond_in = {k: v for k, v in _L0_cond_all.items() if k in ('weight', 'mask', 'bias')}
    del _L0_cond_all

    def _L0_ffn_setup():
        import jax, jax.numpy as jnp
        import numpy as np
        B, S = (4, 64)
        H = 128
        I = 352
        E = 8
        K = 2
        IS = 176
        key = jax.random.key(seed)
        ks = jax.random.split(key, 8)

        def init(k, shape, fan_in):
            return (jax.random.normal(k, shape, jnp.float32) / np.sqrt(fan_in)).astype(jnp.float32)
        return {'hidden_states': jax.random.normal(ks[0], (B, S, H), jnp.float32), 'gate_w': init(ks[1], (H, E), H), 'Wg': init(ks[2], (E, H, I), H), 'Wu': init(ks[3], (E, H, I), H), 'Wd': init(ks[4], (E, I, H), I), 'Sg': init(ks[5], (H, IS), H), 'Su': init(ks[6], (H, IS), H), 'Sd': init(ks[7], (IS, H), IS)}
    _L0_ffn_all = _L0_ffn_setup()
    _L0_ffn_in = {k: v for k, v in _L0_ffn_all.items() if k in ('gate_w', 'Wg', 'Wu', 'Wd', 'Sg', 'Su', 'Sd')}
    del _L0_ffn_all

    def _L1_cond_setup():
        import jax, jax.numpy as jnp
        import numpy as np
        TOP_K = 2
        NUM_MOE_LAYERS = 12

        def _gemma_mlp(x, gate_w, up_w, down_w):
            g = jnp.einsum('bsh,hi->bsi', x, gate_w)
            u = jnp.einsum('bsh,hi->bsi', x, up_w)
            return jnp.einsum('bsi,ih->bsh', jax.nn.gelu(g, approximate=True) * u, down_w)
        key = jax.random.key(seed)
        ks = jax.random.split(key, 8)
        B, S, H, I, E = (32, 32, 128, 512, 8)
        std = 0.02
        return {'x': jax.random.normal(ks[0], (B, S, H), jnp.float32), 'router_logits': jax.random.normal(ks[1], (B, E), jnp.float32), 'skill_gate': jax.random.normal(ks[2], (E, H, I), jnp.float32) * std, 'skill_up': jax.random.normal(ks[3], (E, H, I), jnp.float32) * std, 'skill_down': jax.random.normal(ks[4], (E, I, H), jnp.float32) * std, 'shared_gate': jax.random.normal(ks[5], (H, I), jnp.float32) * std, 'shared_up': jax.random.normal(ks[6], (H, I), jnp.float32) * std, 'shared_down': jax.random.normal(ks[7], (I, H), jnp.float32) * std}
    _L1_cond_all = _L1_cond_setup()
    _L1_cond_in = {k: v for k, v in _L1_cond_all.items() if k in ('skill_gate', 'skill_up', 'skill_down', 'shared_gate', 'shared_up', 'shared_down')}
    del _L1_cond_all

    def _L1_ffn_setup():
        import jax, jax.numpy as jnp
        import numpy as np
        D = 128
        H = 4
        HD = D // H
        E = 8
        FF = 512
        CAP_FACTOR = 1.0

        def _ln(x, g, b, eps=1e-05):
            mu = jnp.mean(x, -1, keepdims=True)
            v = jnp.mean((x - mu) ** 2, -1, keepdims=True)
            return (x - mu) * jax.lax.rsqrt(v + eps) * g + b

        def _mha(x, w, b, ow, ob):
            L, N, _ = x.shape
            qkv = x @ w.T + b
            q, k, v = jnp.split(qkv, 3, axis=-1)
            rh = lambda t: t.reshape(L, N, H, HD).transpose(1, 2, 0, 3)
            q, k, v = (rh(q), rh(k), rh(v))
            scores = jnp.einsum('nhld,nhmd->nhlm', q, k) / np.float32(np.sqrt(HD))
            attn = jax.nn.softmax(scores, axis=-1)
            o = jnp.einsum('nhlm,nhmd->nhld', attn, v).transpose(2, 0, 1, 3).reshape(L, N, D)
            return o @ ow.T + ob

        def _moe(x, wg, w1, b1, w2, b2):
            L, N, _ = x.shape
            S = L * N
            cap = int(CAP_FACTOR * S) // E
            xf = x.reshape(S, D)
            gates = jax.nn.softmax(xf @ wg, axis=-1)
            idx = jnp.argmax(gates, axis=-1)
            mask1 = jax.nn.one_hot(idx, E, dtype=x.dtype)
            loc = jnp.sum((jnp.cumsum(mask1, 0) - 1.0) * mask1, -1).astype(jnp.int32)
            keep = loc < cap
            gate_val = jnp.take_along_axis(gates, idx[:, None], -1)[:, 0]
            slot = jnp.where(keep, idx.astype(jnp.int32) * cap + loc, E * cap)
            disp = jnp.zeros((E * cap, D), x.dtype).at[slot].set(xf, mode='drop')
            disp = disp.reshape(E, cap, D)
            h = jnp.einsum('ecd,edf->ecf', disp, w1) + b1[:, None, :]
            y = (jnp.einsum('ecf,efd->ecd', h, w2) + b2[:, None, :]).reshape(E * cap, D)
            out = jnp.where(keep[:, None], gate_val[:, None] * y[jnp.minimum(slot, E * cap - 1)], 0.0)
            return out.reshape(L, N, D)
        key = jax.random.key(seed)
        ks = jax.random.split(key, 8)
        L, N = (128, 16)
        s = 0.02
        return {'x': jax.random.normal(ks[0], (L, N, D), jnp.float32), 'in_proj_w': jax.random.normal(ks[1], (3 * D, D), jnp.float32) * s, 'in_proj_b': jnp.zeros((3 * D,), jnp.float32), 'out_proj_w': jax.random.normal(ks[2], (D, D), jnp.float32) * s, 'out_proj_b': jnp.zeros((D,), jnp.float32), 'ln1_g': jnp.ones((D,), jnp.float32), 'ln1_b': jnp.zeros((D,), jnp.float32), 'ln2_g': jnp.ones((D,), jnp.float32), 'ln2_b': jnp.zeros((D,), jnp.float32), 'wg': jax.random.normal(ks[3], (D, E), jnp.float32) * s, 'w1': jax.random.normal(ks[4], (E, D, FF), jnp.float32) * s, 'b1': jnp.zeros((E, FF), jnp.float32), 'w2': jax.random.normal(ks[5], (E, FF, D), jnp.float32) * s, 'b2': jnp.zeros((E, D), jnp.float32)}
    _L1_ffn_all = _L1_ffn_setup()
    _L1_ffn_in = {k: v for k, v in _L1_ffn_all.items() if k in ('in_proj_w', 'in_proj_b', 'out_proj_w', 'out_proj_b', 'ln1_g', 'ln1_b', 'ln2_g', 'ln2_b', 'wg', 'w1', 'b1', 'w2', 'b2')}
    del _L1_ffn_all
    return {'x': x, 'cond_8': cond_8, 'L0_cond_weight': _L0_cond_in['weight'], 'L0_cond_mask': _L0_cond_in['mask'], 'L0_cond_bias': _L0_cond_in['bias'], 'L0_ffn_gate_w': _L0_ffn_in['gate_w'], 'L0_ffn_Wg': _L0_ffn_in['Wg'], 'L0_ffn_Wu': _L0_ffn_in['Wu'], 'L0_ffn_Wd': _L0_ffn_in['Wd'], 'L0_ffn_Sg': _L0_ffn_in['Sg'], 'L0_ffn_Su': _L0_ffn_in['Su'], 'L0_ffn_Sd': _L0_ffn_in['Sd'], 'L1_cond_skill_gate': _L1_cond_in['skill_gate'], 'L1_cond_skill_up': _L1_cond_in['skill_up'], 'L1_cond_skill_down': _L1_cond_in['skill_down'], 'L1_cond_shared_gate': _L1_cond_in['shared_gate'], 'L1_cond_shared_up': _L1_cond_in['shared_up'], 'L1_cond_shared_down': _L1_cond_in['shared_down'], 'L1_ffn_in_proj_w': _L1_ffn_in['in_proj_w'], 'L1_ffn_in_proj_b': _L1_ffn_in['in_proj_b'], 'L1_ffn_out_proj_w': _L1_ffn_in['out_proj_w'], 'L1_ffn_out_proj_b': _L1_ffn_in['out_proj_b'], 'L1_ffn_ln1_g': _L1_ffn_in['ln1_g'], 'L1_ffn_ln1_b': _L1_ffn_in['ln1_b'], 'L1_ffn_ln2_g': _L1_ffn_in['ln2_g'], 'L1_ffn_ln2_b': _L1_ffn_in['ln2_b'], 'L1_ffn_wg': _L1_ffn_in['wg'], 'L1_ffn_w1': _L1_ffn_in['w1'], 'L1_ffn_b1': _L1_ffn_in['b1'], 'L1_ffn_w2': _L1_ffn_in['w2'], 'L1_ffn_b2': _L1_ffn_in['b2']}

def reference(x, cond_8, L0_cond_weight, L0_cond_mask, L0_cond_bias, L0_ffn_gate_w, L0_ffn_Wg, L0_ffn_Wu, L0_ffn_Wd, L0_ffn_Sg, L0_ffn_Su, L0_ffn_Sd, L1_cond_skill_gate, L1_cond_skill_up, L1_cond_skill_down, L1_cond_shared_gate, L1_cond_shared_up, L1_cond_shared_down, L1_ffn_in_proj_w, L1_ffn_in_proj_b, L1_ffn_out_proj_w, L1_ffn_out_proj_b, L1_ffn_ln1_g, L1_ffn_ln1_b, L1_ffn_ln2_g, L1_ffn_ln2_b, L1_ffn_wg, L1_ffn_w1, L1_ffn_b1, L1_ffn_w2, L1_ffn_b2):
    import jax
    import jax.numpy as jnp

    def _L0_cond_ref(x, y, weight, mask, bias):
        import jax, jax.numpy as jnp
        import numpy as np
        masked_w = weight * mask[None, :, :]
        w_bot = jnp.einsum('bg,got->bot', y, masked_w)
        return jnp.einsum('bnt,bot->bno', x, w_bot) + bias

    def _L0_ffn_ref(hidden_states, gate_w, Wg, Wu, Wd, Sg, Su, Sd):
        import jax, jax.numpy as jnp
        import numpy as np
        B, S = (4, 64)
        H = 128
        I = 352
        E = 8
        K = 2
        IS = 176
        b, s, h = hidden_states.shape
        x = hidden_states.reshape(-1, h)
        T = x.shape[0]
        logits = x @ gate_w
        top_v, top_i = jax.lax.top_k(logits, K)
        top_p = jax.nn.softmax(top_v, axis=-1)
        combine = jnp.zeros((T, E), x.dtype).at[jnp.arange(T)[:, None], top_i].add(top_p)
        g = jnp.einsum('th,ehi->tei', x, Wg)
        u = jnp.einsum('th,ehi->tei', x, Wu)
        d = jnp.einsum('tei,eih->teh', jax.nn.silu(g) * u, Wd)
        expert_out = jnp.einsum('te,teh->th', combine, d)
        shared = jax.nn.silu(x @ Sg) * (x @ Su) @ Sd
        return (expert_out + shared).reshape(b, s, h)

    def _L1_cond_ref(x, router_logits, skill_gate, skill_up, skill_down, shared_gate, shared_up, shared_down):
        import jax, jax.numpy as jnp
        import numpy as np
        TOP_K = 2
        NUM_MOE_LAYERS = 12

        def _gemma_mlp(x, gate_w, up_w, down_w):
            g = jnp.einsum('bsh,hi->bsi', x, gate_w)
            u = jnp.einsum('bsh,hi->bsi', x, up_w)
            return jnp.einsum('bsi,ih->bsh', jax.nn.gelu(g, approximate=True) * u, down_w)
        B = x.shape[0]
        E = skill_gate.shape[0]
        rw = jax.nn.softmax(router_logits.astype(jnp.float32), axis=-1)
        w, sel = jax.lax.top_k(rw, TOP_K)
        w = w / w.sum(axis=-1, keepdims=True)
        w = w.astype(x.dtype)
        scale = 1.0 / NUM_MOE_LAYERS
        w = scale * w + (1.0 - scale) * jax.lax.stop_gradient(w)
        dense_w = jnp.zeros((B, E), x.dtype).at[jnp.arange(B)[:, None], sel].add(w)

        def step(acc, params):
            g, u, d, we = params
            return (acc + we[:, None, None] * _gemma_mlp(x, g, u, d), None)
        out, _ = jax.lax.scan(step, jnp.zeros_like(x), (skill_gate, skill_up, skill_down, dense_w.T))
        out = out + _gemma_mlp(x, shared_gate, shared_up, shared_down)
        return out

    def _L1_ffn_ref(x, in_proj_w, in_proj_b, out_proj_w, out_proj_b, ln1_g, ln1_b, ln2_g, ln2_b, wg, w1, b1, w2, b2):
        import jax, jax.numpy as jnp
        import numpy as np
        D = 128
        H = 4
        HD = D // H
        E = 8
        FF = 512
        CAP_FACTOR = 1.0

        def _ln(x, g, b, eps=1e-05):
            mu = jnp.mean(x, -1, keepdims=True)
            v = jnp.mean((x - mu) ** 2, -1, keepdims=True)
            return (x - mu) * jax.lax.rsqrt(v + eps) * g + b

        def _mha(x, w, b, ow, ob):
            L, N, _ = x.shape
            qkv = x @ w.T + b
            q, k, v = jnp.split(qkv, 3, axis=-1)
            rh = lambda t: t.reshape(L, N, H, HD).transpose(1, 2, 0, 3)
            q, k, v = (rh(q), rh(k), rh(v))
            scores = jnp.einsum('nhld,nhmd->nhlm', q, k) / np.float32(np.sqrt(HD))
            attn = jax.nn.softmax(scores, axis=-1)
            o = jnp.einsum('nhlm,nhmd->nhld', attn, v).transpose(2, 0, 1, 3).reshape(L, N, D)
            return o @ ow.T + ob

        def _moe(x, wg, w1, b1, w2, b2):
            L, N, _ = x.shape
            S = L * N
            cap = int(CAP_FACTOR * S) // E
            xf = x.reshape(S, D)
            gates = jax.nn.softmax(xf @ wg, axis=-1)
            idx = jnp.argmax(gates, axis=-1)
            mask1 = jax.nn.one_hot(idx, E, dtype=x.dtype)
            loc = jnp.sum((jnp.cumsum(mask1, 0) - 1.0) * mask1, -1).astype(jnp.int32)
            keep = loc < cap
            gate_val = jnp.take_along_axis(gates, idx[:, None], -1)[:, 0]
            slot = jnp.where(keep, idx.astype(jnp.int32) * cap + loc, E * cap)
            disp = jnp.zeros((E * cap, D), x.dtype).at[slot].set(xf, mode='drop')
            disp = disp.reshape(E, cap, D)
            h = jnp.einsum('ecd,edf->ecf', disp, w1) + b1[:, None, :]
            y = (jnp.einsum('ecf,efd->ecd', h, w2) + b2[:, None, :]).reshape(E * cap, D)
            out = jnp.where(keep[:, None], gate_val[:, None] * y[jnp.minimum(slot, E * cap - 1)], 0.0)
            return out.reshape(L, N, D)
        y1 = _ln(x + _mha(x, in_proj_w, in_proj_b, out_proj_w, out_proj_b), ln1_g, ln1_b)
        y2 = _ln(y1 + _moe(y1, wg, w1, b1, w2, b2), ln2_g, ln2_b)
        return y2
    x = x + _L0_ffn_ref(_L0_cond_ref(x, cond_8, L0_cond_weight, L0_cond_mask, L0_cond_bias), L0_ffn_gate_w, L0_ffn_Wg, L0_ffn_Wu, L0_ffn_Wd, L0_ffn_Sg, L0_ffn_Su, L0_ffn_Sd)
    x = x + _L1_ffn_ref(_L1_cond_ref(x, cond_8, L1_cond_skill_gate, L1_cond_skill_up, L1_cond_skill_down, L1_cond_shared_gate, L1_cond_shared_up, L1_cond_shared_down), L1_ffn_in_proj_w, L1_ffn_in_proj_b, L1_ffn_out_proj_w, L1_ffn_out_proj_b, L1_ffn_ln1_g, L1_ffn_ln1_b, L1_ffn_ln2_g, L1_ffn_ln2_b, L1_ffn_wg, L1_ffn_w1, L1_ffn_b1, L1_ffn_w2, L1_ffn_b2)
    return x

_drawn_inputs = setup_inputs


def setup_inputs(seed=0):
    import zlib

    import numpy as np

    out = dict(_drawn_inputs(seed))
    spreads = {'L1_ffn_in_proj_b': (0.0, 0.1),
     'L1_ffn_out_proj_b': (0.0, 0.1),
     'L1_ffn_ln1_g': (1.0, 0.2),
     'L1_ffn_ln1_b': (0.0, 0.1),
     'L1_ffn_ln2_g': (1.0, 0.2),
     'L1_ffn_ln2_b': (0.0, 0.1),
     'L1_ffn_b1': (0.0, 0.8),
     'L1_ffn_b2': (0.0, 0.8)}
    factors = {'L1_ffn_in_proj_w': 8.0, 'L1_ffn_wg': 7.707, 'L1_ffn_w1': 8.0, 'L1_ffn_w2': 8.0}
    for name, (base, spread) in spreads.items():
        noise = np.random.default_rng([zlib.crc32(name.encode()), seed]).standard_normal(out[name].shape)
        drawn = base * np.exp(spread * noise) if base else spread * noise
        out[name] = jnp.asarray(drawn.astype(out[name].dtype))
    for name, factor in factors.items():
        out[name] = (out[name] * factor).astype(out[name].dtype)
    return out
```

```python
from contextlib import ExitStack

import concourse.bass as bass
from concourse import mybir
import numpy as np

ALU = mybir.AluOpType
ACT = mybir.ActivationFunctionType
AX = mybir.AxisListType
F32 = mybir.dt.float32
F16 = mybir.dt.float16
BF16 = mybir.dt.bfloat16
I32 = mybir.dt.int32
U32 = mybir.dt.uint32

P = 128
B, N, D = 8, 256, 128
T = B * N
NT = T // P
E = 8
F0 = 352
FS = 176
SC = FS // 2
F1 = 512
C1 = F1 // P
C2 = 512 // P
H, HD = 4, 32
G, GN = 16, 16
CAP = T // E
SLOT_TILES = 2 * T // P + E
BIG = 3.0e38
EPS = 1e-5
SKILL_SCALE = 1.0 / 12.0
BLK = 4
NB = NT // BLK

CONST = {}
_at = 0
for _name, _width in (("ident", P), ("iota", P), ("before", P), ("row_before", P), ("row_same", P),
                      ("row_same_before", P), ("mask", P), ("token", NT), ("tile_start", SLOT_TILES),
                      ("restart", E * G), ("ones", P), ("eye8", E * E), ("own_group", G), ("repeat8", P)):
    CONST[_name] = (_at, _at + _width)
    _at += _width
CONST_W = _at


def shape_constants():
    k = np.arange(P)[:, None]
    m = np.arange(P)[None, :]
    c = np.zeros((P, CONST_W), np.float32)

    def put(name, a):
        c[:, CONST[name][0]:CONST[name][1]] = a

    put("ident", k == m)
    put("iota", m + 0 * k)
    put("before", k < m)
    put("row_before", k // GN < m // GN)
    put("row_same", k // GN == m // GN)
    put("row_same_before", (k // GN == m // GN) & (k < m))
    put("mask", np.where((k - m) % GN == 0, 0.0, -1.0e30))
    put("token", k + P * np.arange(NT)[None, :])
    put("tile_start", P * np.arange(SLOT_TILES)[None, :] + 0 * k)
    put("restart", (np.arange(E * G)[None, :] % G != 0) + 0 * k)
    put("ones", 1.0)
    put("eye8", np.eye(E).reshape(1, -1) + 0 * k)
    put("own_group", k // E == np.arange(G)[None, :])
    put("repeat8", (k < E) & (m % E == k))
    return c


def block_kernel(nc, xT_d, x_d, cond_d, cw_d, cmask_d, cbias_d, vecs_d, const_d, gate_d, wgu_d, wd_d,
                 sgu_d, sd_d, wexp_d, wsh_d, w1_d, w2_d, b1_d, b2_d, wqkv_d, wo_d, bqkv_d, wg_d, out_d):
    with ExitStack() as ctx:
        def sb(name, shape, dt=F32):
            return ctx.enter_context(nc.sbuf_tensor(name, shape, dt))

        def sem(name):
            return ctx.enter_context(nc.semaphore(name))

        bank = [ctx.enter_context(nc.psum_tensor(f"bank{i}", [P, 512], F32)) for i in range(8)]

        h0_rows = nc.dram_tensor("h0_rows", [T, D], F32, kind="Internal").ap()
        y_rows = nc.dram_tensor("y_rows", [SLOT_TILES * P, D], F32, kind="Internal").ap()
        x1_rows = nc.dram_tensor("x1_rows", [T, D], F32, kind="Internal").ap()

        xT = sb("xT", [P, T])
        y_bc = sb("y_bc", [P, B * E])
        cw = sb("cw", [P, 2, E, P])
        cmask = sb("cmask", [P, P])
        cbias = sb("cbias", [P, 1])
        vecs = sb("vecs", [P, 7, P])
        cbias_bc, bv_bc, bo_bc, g1_bc, n1_bc, g2_bc, n2_bc = (vecs[:, i, :] for i in range(7))
        const = sb("const", [P, CONST_W])
        gate_w = sb("gate_w", [P, E])
        wgu = sb("wgu", [P, E * 2 * F0])
        wd = sb("wd", [P, E, 3, D])
        sgu = sb("sgu", [P, 2 * FS])
        sd = sb("sd", [SC, 2, D])
        wk = [sb(f"wk{k}", [P, 3 * F1]) for k in range(2)]
        wsh = sb("wsh", [P, 3 * F1])
        w12in = sb("w12in", [P, 2, E, C2, P])
        b1 = sb("b1", [P, E, C2])
        b2 = sb("b2", [E, D])
        wqkv = sb("wqkv", [P, 3 * D])
        wo = sb("wo", [P, D])
        bqkv = sb("bqkv", [P, 3])
        wg = sb("wg", [P, E])

        def K(name):
            return const[:, CONST[name][0]:CONST[name][1]]

        wbt = sb("wbt", [P, B, P])
        h0T = sb("h0T", [P, T])
        h0r = sb("h0r", [P, NT, D])
        xs = sb("xs", [P, NT, D])
        lg = sb("lg", [P, NT, E])
        lgb = sb("lgb", [P, NT, E])
        oh = [sb(f"oh{k}", [P, NT, E]) for k in range(2)]
        mtop = [sb(f"mtop{k}", [P, NT]) for k in range(2)]
        itop = [sb(f"itop{k}", [P, NT]) for k in range(2)]
        t8 = sb("t8", [P, NT, E])
        taken = sb("taken", [P, NT, E], BF16)
        before_b = sb("before_b", [P, P], BF16)
        ones_b = sb("ones_b", [P, P], BF16)
        dlt = sb("dlt", [P, NT])
        edl = sb("edl", [P, NT])
        sdl = sb("sdl", [P, NT])
        pk = sb("pk", [P, 2, NT])
        tot = sb("tot", [P, E, NT])
        incl = sb("incl", [P, E, NT])
        excl = sb("excl", [P, E, NT])
        cnt = sb("cnt", [P, 6, E])
        Q = sb("Q", [P, NT, E])
        pos = sb("pos", [P, 2, NT])
        lo = sb("lo", [P, 2 * NT])
        hi = sb("hi", [P, 2 * NT])
        lo_i = sb("lo_i", [P, 2 * NT], U32)
        hi_i = sb("hi_i", [P, 2 * NT], U32)
        cnt_i = sb("cnt_i", [P, E], I32)
        pos_u = sb("pos_u", [P, 2, NT], U32)
        prod = sb("prod", [P, 2, E, D])
        ohlo = prod[:].rearrange("p a e d -> p (a e d)").bitcast(F16).rearrange("p (i s) -> p i s", s=P)
        ohhi = sb("ohhi", [P, 2 * NT, SLOT_TILES], F16)
        slot_tok = sb("slot_tok", [P, SLOT_TILES], U32)
        cmp = sb("cmp", [P, SLOT_TILES, E])
        ecnt = sb("ecnt", [P, SLOT_TILES])
        eslot = sb("eslot", [P, SLOT_TILES], I32)
        sgl = sb("sgl", [SC, 2, 512])
        acts = sb("acts", [P, 4, 512])
        sact = acts[0:SC].rearrange("p (a c) n -> p a c n", a=2)
        xg = sb("xg", [P, 4, D])
        xgT = sb("xgT", [P, 2, P])
        hidT = prod[:].rearrange("p a e d -> p (a e d)")[:, 0:6 * P].rearrange("p (a n) -> p a n", a=2)
        slu = prod[:].rearrange("p a e d -> p (a e d)")[:, 6 * P:6 * P + 2 * F0].rearrange("p (a n) -> p a n", a=2)
        hid = sb("hid", [P, 2, 3 * P])
        ysb = sb("ysb", [P, 4, D])
        yg = sb("yg", [P, 2, 2, 2, D])
        cd = sb("cd", [P, B, E])
        ce = sb("ce", [P, B, E])
        rw = sb("rw", [P, B, E])
        rwb = sb("rwb", [P, B, E])
        c8 = sb("c8", [P, B, E])
        coh = sb("coh", [P, B, E])
        cs = sb("cs", [P, 8, B])
        cwt = sb("cwt", [P, 2, B])
        cix = sb("cix", [P, 2, B], I32)
        half1 = sb("half1", [P, 2, D])
        x1t = sb("x1t", [P, 2, 2, D])
        x1T = sb("x1T", [P, 2, N])
        gl = acts[:, 0:2]
        hb = acts[:, 2:4]
        zT = xT
        W12 = wbt[:].rearrange("p b d -> p (b d)")
        b1z = sb("b1z", [P, E, C2, E])
        c_e = sb("c_e", [E, D])
        c_ge = sb("c_ge", [P, D])
        qT = h0T
        bq_s = sb("bq_s", [P, 1])
        kz = w12in[:, :, :, :, :].rearrange("p a e c d -> p (a e c d)").rearrange(
            "p (g h k) -> p g h k", g=G, h=H)
        mask_b = sb("mask_b", [P, H, P], BF16)
        ident_b = sb("ident_b", [P, P], BF16)
        nmax = sb("nmax", [P, 2, H])
        pr = gl.rearrange("p a (h k) -> p a h k", h=H)
        den = sb("den", [P, 2, H])
        rden = sb("rden", [P, 2, H])
        prT = hb
        vv = sb("vv", [P, 3, D])
        att = sb("att", [P, 2, D])
        attT = sb("attT", [P, 2, P])
        res = sb("res", [P, 2, D])
        st1 = sb("st1", [P, 2, 6])
        mv1 = sb("mv1", [P, 2, 2])
        rs1 = sb("rs1", [P, 2, 1])
        var_e = sb("var_e", [P, 1])
        newton = sb("newton", [P, 1])
        nrm = sb("nrm", [P, 2, D])
        nrg = sb("nrg", [P, 2, D])
        y1 = h0r
        y1T = cw[:, :, :, :].rearrange("p a e d -> p (a e) d")
        x1g = wgu[:, 0:T].rearrange("p (g d) -> p g d", g=G)
        cblk = wgu[:, T:2 * T].rearrange("p (g d) -> p g d", g=G)
        lg1 = lg
        e1 = lgb
        oh1 = oh[0]
        oh1b = sb("oh1b", [P, G, E], BF16)
        rowm = {n: sb(n + "_b", [P, P], BF16) for n in ("row_before", "row_same", "row_same_before")}
        tsum = sb("tsum", [P, E])
        tsum_b = sb("tsum_b", [P, G, E], BF16)
        exb = sb("exb", [P, G, E], BF16)
        gk = sb("gk", [P, G, E])
        sm1 = sb("sm1", [P, 6, G])
        gkT = sb("gkT", [P, P])
        base = xs
        msum = sb("msum", [P, 2, D])
        fin = wk[0][:, 0:4 * D].rearrange("p (r d) -> p r d", r=4)

        s_xT, s_cond, s_const, s_gate, s_sh, s_exp0, s_fold, s_wsh, s_attw = (
            sem(n) for n in ("xT_in", "cond_in", "const_in", "gate_in", "shared_in", "experts_in",
                             "fold_in", "gemma_shared_in", "attention_in"))
        s_dve = sem("dve_chain")
        s_wb, s_h0p, s_r0p, s_h0, s_h0r, s_h0st, s_lgp = (
            sem(n) for n in ("cond_weights", "h0T_product", "h0_rows_product", "h0T_ready",
                             "h0_rows_ready", "h0_rows_stored", "logits_product"))
        s_castb, s_taken, s_pre, s_dlt, s_edl, s_onehot, s_tab, s_slots, s_pos = (
            sem(n) for n in ("constants_cast", "taken_ready", "prefix_product", "gap_ready",
                             "gap_exp", "onehots_ready", "slot_table_product", "slots_ready",
                             "positions_ready"))
        s_cd, s_ce, s_cr = sem("cond_gap_ready"), sem("cond_exp"), sem("cond_router_ready")
        s_b1z, s_w12p, s_w12, s_cp, s_c8, s_c2p, s_cge = (
            sem(n) for n in ("b1_spread", "w12_product", "w12_ready", "c_product", "c_ready",
                             "c_repeat_product", "c_repeat_ready"))
        s_sgp, s_ssl, s_sact, s_sdp, s_xs = (
            sem(n) for n in ("shared_gu", "shared_silu", "shared_act", "shared_down", "xs_ready"))
        s_hpad = sem("hid_padding")
        s_xg = [sem(f"xg_in{i}") for i in range(4)]
        s_X, s_xe, s_G, s_sl, s_hm, s_H, s_he, s_D, s_ye = (
            sem(n) for n in ("xg_turned", "xgT_ready", "gu_product", "silu_ready", "hid_ready",
                             "hid_turned", "hidT_ready", "down_product", "y_ready"))
        s_yst = [sem(f"y_stored{i}") for i in range(4)]
        s_yg = [sem(f"yg_in{i}") for i in range(2)]
        s_half, s_x1, s_x1st, s_x1p, s_x1T = (
            sem(n) for n in ("x1_half", "x1_ready", "x1_stored", "x1_turned", "x1T_ready"))
        s_x1h = sem("x1_half_rows")
        s_wk = [sem(f"skill_in{k}") for k in range(2)]
        s_gu1, s_gl, s_m1, s_dn, s_z = (
            sem(n) for n in ("gemma_gu", "gelu_ready", "gemma_hid", "gemma_down", "z_ready"))
        s_kz0, s_bq, s_qkp, s_qk, s_kk, s_ka = (
            sem(n) for n in ("kz_zeroed", "bq_scaled", "qk_product", "q_ready", "keys_ready_vector", "keys_ready_scalar"))
        s_S, s_V, s_nm, s_vv, s_pr, s_rd, s_PT, s_pe, s_O, s_att = (
            sem(n) for n in ("scores_product", "v_product", "score_max", "v_ready", "probs_ready",
                             "rden_ready", "probs_turned", "probsT_ready", "o_product", "att_ready"))
        s_AT, s_ae, s_Y, s_res, s_y1, s_YT, s_yT = (
            sem(n) for n in ("att_turned", "attT_ready", "proj_product", "residual_ready",
                             "y1_ready", "y1_turned", "y1T_ready"))
        s_nr1, s_ng1 = sem("norm1_scaled"), sem("norm1_gained")
        s_l1, s_gap1, s_e1, s_oh1, s_loc, s_gk, s_gkp, s_gkT, s_bp, s_base = (
            sem(n) for n in ("moe_logits", "moe_gap", "moe_exp", "moe_onehot", "moe_location",
                             "moe_gates", "gates_turned", "gatesT_ready", "bias_product",
                             "base_ready"))
        s_x1g, s_cblk, s_ym, s_prod, s_fn, s_fo = (
            sem(n) for n in ("x1_grouped_in", "cblk_ready", "moe_product", "moe_weighted",
                             "norm2_scaled", "final_ready"))
        s_fst = [sem(f"out_stored{i}") for i in range(4)]

        group = lambda ap, g: ap[:, P * g:P * g + P]

        block = ctx.enter_context(nc.Block())

        @block.sync
        def _(sp):
            sp.dma_start(y_bc[:], cond_d.rearrange("b e -> (b e)").partition_broadcast(P)).then_inc(s_cond, 16)
            sp.dma_start(cw[:, 0], cw_d).then_inc(s_cond, 16)
            sp.dma_start(cmask[:], cmask_d).then_inc(s_cond, 16)
            sp.dma_start(cbias[:], cbias_d).then_inc(s_cond, 16)
            sp.dma_start(vecs[:], vecs_d.partition_broadcast(P)).then_inc(s_cond, 16)
            sp.dma_start(xT[:], xT_d).then_inc(s_xT, 16)
            sp.dma_start(gate_w[:], gate_d).then_inc(s_gate, 16)
            sp.dma_start(const[:], const_d).then_inc(s_const, 16)
            sp.dma_start(w12in[:, 0], w1_d).then_inc(s_fold, 16)
            sp.dma_start(w12in[:, 1], w2_d).then_inc(s_fold, 16)
            sp.dma_start(b1[:], b1_d).then_inc(s_fold, 16)
            sp.dma_start(b2[:], b2_d).then_inc(s_fold, 16)
            sp.dma_start(sgu[:], sgu_d).then_inc(s_sh, 16)
            sp.dma_start(sd[:], sd_d).then_inc(s_sh, 16)
            sp.dma_start(xs[:], x_d.rearrange("(t p) d -> p t d", p=P)).then_inc(s_sh, 16)
            for blk in range(NB):
                sp.wait_ge(s_h0r, blk + 1)
                sp.dma_start(h0_rows[512 * blk:512 * blk + 512, :].rearrange("(t p) d -> p t d", p=P),
                             h0r[:, BLK * blk:BLK * blk + BLK, :]).then_inc(s_h0st, 16)
            sp.dma_start(wgu[:], wgu_d).then_inc(s_exp0, 16)
            sp.dma_start(wd[:], wd_d).then_inc(s_exp0, 16)
            sp.dma_start(wsh[:], wsh_d).then_inc(s_wsh, 16)
            sp.dma_start(wqkv[:], wqkv_d).then_inc(s_attw, 16)
            sp.dma_start(wo[:], wo_d).then_inc(s_attw, 16)
            sp.dma_start(bqkv[:], bqkv_d).then_inc(s_attw, 16)
            sp.dma_start(wg[:], wg_d).then_inc(s_attw, 16)
            sp.wait_ge(s_cr, 1)
            for k in range(2):
                e = sp.value_load(cix[0:1, k, 0:1], min_val=0, max_val=E - 1)
                sp.dma_start(wk[k][:], wexp_d[bass.ds(e, 1), :, :].rearrange("a p n -> (a p) n")).then_inc(s_wk[k], 16)
            with sp.Fori(0, SLOT_TILES // 4) as jj:
                for r in range(4):
                    sp.wait_ge(s_ye, jj * 4 + r + 1)
                    sp.dma_start(y_rows[bass.ds((jj * 4 + r) * P, P), :], ysb[:, r, :]).then_inc(s_yst[r], 16)

            def store_x1(b, par):
                sp.wait_ge(s_x1, b + 1)
                sp.dma_start(x1_rows[bass.ds(b * N, N), :].rearrange("(t p) d -> p t d", p=P),
                             x1t[:, par]).then_inc(s_x1st, 16)

            def load_skill(b, k):
                sp.wait_ge(s_dn, b * 6 - 6 + 2 * (k + 1))
                e = sp.value_load(cix[0:1, k, bass.ds(b, 1)], min_val=0, max_val=E - 1)
                sp.dma_start(wk[k][:], wexp_d[bass.ds(e, 1), :, :].rearrange("a p n -> (a p) n")).then_inc(s_wk[k], 16)

            store_x1(0, 0)
            with sp.Fori(0, B // 2 - 1) as bp:
                for u in range(2):
                    load_skill(bp * 2 + u + 1, 0)
                    store_x1(bp * 2 + u + 1, (u + 1) % 2)
                    load_skill(bp * 2 + u + 1, 1)
            load_skill(B - 1, 0)
            store_x1(B - 1, 1)
            load_skill(B - 1, 1)
            sp.wait_ge(s_x1st, 16 * B)
            for l in range(B):
                sp.dma_start(x1g[GN * l:GN * l + GN, :, :],
                             x1_rows[N * l:N * l + N, :].rearrange("(g n) d -> n g d", n=GN)).then_inc(s_x1g, 16)
            for g in range(G):
                sp.wait_ge(s_fo, g + 1)
                sp.dma_start(out_d[:, GN * g:GN * g + GN, :], fin[:, g % 4, :]).then_inc(s_fst[g % 4], 16)
            for r in range(4):
                sp.wait_ge(s_fst[r], 16 * (G // 4))

        @block.gpsimd
        def _(pool):
            nc.gpsimd.memset(hid[:], 0.0).then_inc(s_hpad, 1)
            pool.wait_ge(s_const, 16)
            nc.gpsimd.tensor_copy(before_b[:], K("before"))
            nc.gpsimd.tensor_copy(ones_b[:], K("ones"))
            nc.gpsimd.tensor_copy(ident_b[:], K("ident"))
            nc.gpsimd.tensor_copy(mask_b[:], K("mask").unsqueeze(1).broadcast_to([P, H, P]))
            for n in rowm:
                nc.gpsimd.tensor_copy(rowm[n][:], K(n))
            pool.wait_ge(s_fold, 64)
            nc.gpsimd.tensor_tensor(b1z[:], b1[:].unsqueeze(3).broadcast_to([P, E, C2, E]),
                                    K("eye8").rearrange("p (e f) -> p e f", e=E).unsqueeze(2)
                                    .broadcast_to([P, E, C2, E]), ALU.mult).then_inc(s_b1z, 1)
            pool.wait_ge(s_h0st, 16 * NB)
            pool.wait_ge(s_slots, 1)
            for j in range(SLOT_TILES):
                if j >= 4:
                    pool.wait_ge(s_X, j - 3)
                nc.gpsimd.indirect_dma_start(
                    out=xg[:, j % 4, :], out_offset=None, in_=h0_rows,
                    in_offset=bass.IndirectOffsetOnAxis(ap=slot_tok[:, j:j + 1], axis=0)).then_inc(s_xg[j % 4], 16)
                if j == 3:
                    pool.wait_ge(s_w12p, 1)
                    pool.wait_ge(s_cp, 1)
                if 4 <= j < 4 + G:
                    nc.gpsimd.memset(kz[:, j - 4], 0.0).then_inc(s_kz0, 1)
            for r in range(4):
                pool.wait_ge(s_yst[r], 16 * (SLOT_TILES // 4))
            pool.wait_ge(s_pos, 1)
            for b in range(B):
                if b >= 2:
                    pool.wait_ge(s_x1, b - 1)
                for i in range(2):
                    for k in range(2):
                        nc.gpsimd.indirect_dma_start(
                            out=yg[:, b % 2, i, k, :], out_offset=None, in_=y_rows,
                            in_offset=bass.IndirectOffsetOnAxis(ap=pos_u[:, k, 2 * b + i:2 * b + i + 1], axis=0)
                        ).then_inc(s_yg[b % 2], 16)
                if b == 2:
                    pool.wait_ge(s_cge, 1)
                    nc.gpsimd.tensor_tensor(cblk, c_ge[:].unsqueeze(1).broadcast_to([P, G, D]),
                                            K("own_group").unsqueeze(2).broadcast_to([P, G, D]),
                                            ALU.mult).then_inc(s_cblk, 1)
            for g in range(G):
                pool.wait_ge(s_nr1, g + 1)
                nc.gpsimd.tensor_tensor(nrg[:, g % 2], nrm[:, g % 2], g1_bc, ALU.mult).then_inc(s_ng1, 1)
                pool.wait_ge(s_ng1, g + 1)
                nc.gpsimd.tensor_tensor(y1[:, g], nrg[:, g % 2], n1_bc, ALU.add).then_inc(s_y1, 1)

        @block.scalar
        def _(act):
            act.wait_ge(s_cond, 80)
            for blk in range(NB):
                act.wait_ge(s_h0p, blk + 1)
                nc.scalar.activation(h0T[:, 512 * blk:512 * blk + 512], bank[blk % 2][:], ACT.Identity,
                                     bias=cbias[:]).then_inc(s_h0, 1)
            act.wait_ge(s_cd, 1)
            nc.scalar.activation(ce[:], cd[:], ACT.Exp).then_inc(s_ce, 1)
            act.wait_ge(s_w12p, 1)
            for i in range(2):
                nc.scalar.activation(W12[:, 512 * i:512 * i + 512], bank[5 + i][:], ACT.Copy).then_inc(s_w12, 1)
            act.wait_ge(s_dlt, 1)
            nc.scalar.activation(edl[:], dlt[:], ACT.Exp).then_inc(s_edl, 1)
            act.wait_ge(s_c2p, 1)
            nc.scalar.activation(c_ge[:], bank[7][:, 128:256], ACT.Copy).then_inc(s_cge, 1)
            for n in range(2 * NB):
                act.wait_ge(s_sgp, n + 1)
                if n >= 2:
                    act.wait_ge(s_sact, n - 1)
                nc.scalar.activation(sgl[:, n % 2], bank[2 * (n % 2)][0:SC, :], ACT.Silu).then_inc(s_ssl, 1)

            def silu(j, r, ring):
                act.wait_ge(s_G, j + 1)
                if ring:
                    act.wait_ge(s_hm, j - 1)
                nc.scalar.activation(slu[:, r], bank[2 * r][:, 0:F0], ACT.Silu).then_inc(s_sl, 1)

            def hidT_copy(j, r, ring):
                act.wait_ge(s_H, j + 1)
                if ring:
                    act.wait_ge(s_D, j - 1)
                nc.scalar.activation(hidT[:, r], bank[4 + r][:, 0:3 * P], ACT.Copy).then_inc(s_he, 1)

            silu(0, 0, False)
            silu(1, 1, False)
            hidT_copy(0, 0, False)
            silu(2, 0, True)
            hidT_copy(1, 1, False)
            silu(3, 1, True)
            hidT_copy(2, 0, True)
            with act.Fori(1, SLOT_TILES // 4) as jj:
                for u in range(4):
                    silu(jj * 4 + u, u % 2, True)
                    hidT_copy(jj * 4 + (u - 1), (u + 1) % 2, True)
            hidT_copy(SLOT_TILES - 1, 1, True)

            def x1T_copy(b, par):
                act.wait_ge(s_x1p, b + 1)
                nc.scalar.activation(x1T[:, par], bank[6 + par][:, 0:N], ACT.Copy).then_inc(s_x1T, 1)

            def gelu(b, hh, ring):
                act.wait_ge(s_gu1, b * 6 + (hh + 1))
                if ring:
                    act.wait_ge(s_m1, b * 6 + (hh - 1))
                nc.scalar.activation(gl[:, hh % 2], bank[hh % 2][:], ACT.Gelu_apprx_tanh).then_inc(s_gl, 1)

            def z_copy(b):
                act.wait_ge(s_dn, b * 6 + 6)
                nc.scalar.activation(zT[:].rearrange("p (g l n) -> p g l n", g=G, l=B)[:, :, bass.ds(b, 1), :].rearrange("p g a n -> p g (a n)"),
                                     bank[4][:, 0:N].rearrange("p (g n) -> p g n", g=G), ACT.Copy).then_inc(s_z, 1)

            def act_row(b, par, first=False, last=False):
                for hh in range(6):
                    gelu(b, hh, not (first and hh < 2))
                    if hh == 0 and not first:
                        z_copy(b - 1)
                    if hh == 4 and not last:
                        x1T_copy(b + 1, 1 - par)

            x1T_copy(0, 0)
            act_row(0, 0, first=True)
            act_row(1, 1)
            with act.Fori(1, B // 2 - 1) as bp:
                for u in range(2):
                    act_row(bp * 2 + u, u)
            act_row(B - 2, 0)
            act_row(B - 1, 1, last=True)
            z_copy(B - 1)

            act.wait_ge(s_attw, 64)
            act.wait_ge(s_bq, 1)
            for blk in range(NB):
                act.wait_ge(s_qkp, blk + 1)
                nc.scalar.activation(qT[:, 512 * blk:512 * blk + 512], bank[2 * (blk % 2)][:], ACT.Identity,
                                     bias=bq_s[:], scale=HD ** -0.5).then_inc(s_qk, 1)
                act.wait_ge(s_kz0, G)
                for h in range(2):
                    a = HD * h
                    nc.scalar.activation(
                        kz[a:a + HD, BLK * blk:BLK * blk + BLK, h, :],
                        bank[2 * (blk % 2) + 1][a:a + HD, :].rearrange("p (g k) -> p g k", g=BLK),
                        ACT.Identity, bias=bqkv[a:a + HD, 1:2]).then_inc(s_ka, 1)
            for i in range(G + 4):
                if i < G:
                    act.wait_ge(s_nm, i + 1)
                    if i >= 2:
                        act.wait_ge(s_PT, i - 1)
                        act.wait_ge(s_rd, i - 1)
                    for h in range(H):
                        nc.scalar.activation(pr[:, i % 2, h], bank[i % 2][:, P * h:P * h + P], ACT.Exp,
                                             bias=nmax[:, i % 2, h:h + 1],
                                             accum_out=den[:, i % 2, h:h + 1]).then_inc(s_pr, 1)
                g = i - 3
                if 0 <= g < G:
                    act.wait_ge(s_AT, g + 1)
                    if g >= 2:
                        act.wait_ge(s_Y, g - 1)
                    nc.scalar.activation(attT[:, g % 2], bank[6][:, 0:P],
                                         ACT.Copy).then_inc(s_ae, 1)
                g = i - 4
                if 0 <= g < G:
                    act.wait_ge(s_YT, g + 1)
                    nc.scalar.activation(y1T[:, g], bank[7][:, 0:P],
                                         ACT.Copy).then_inc(s_yT, 1)
            act.wait_ge(s_gap1, 1)
            nc.scalar.activation(e1[:], t8[:], ACT.Exp).then_inc(s_e1, 1)
            act.wait_ge(s_gkp, 1)
            nc.scalar.activation(gkT[:], bank[5][:, 0:P], ACT.Copy).then_inc(s_gkT, 1)

        @block.tensor
        def _(pe):
            ident = K("ident")
            mm = nc.tensor.matmul
            pe.wait_ge(s_xT, 16)

            def logits(blk):
                pe.wait_ge(s_h0, blk + 1)
                for t in range(BLK * blk, BLK * blk + BLK):
                    last = mm(bank[4][:, E * t:E * t + E], h0T[:, P * t:P * t + P], gate_w[:], start=True, stop=True)
                last.then_inc(s_lgp, 1)

            for blk in range(NB):
                pe.wait_ge(s_wb, 2 * blk + 2)
                if blk >= 2:
                    pe.wait_ge(s_h0, blk - 1)
                for i in range(2):
                    b = 2 * blk + i
                    last = mm(bank[blk % 2][:, N * i:N * i + N], wbt[:, b, :], xT[:, N * b:N * b + N],
                              start=True, stop=True)
                last.then_inc(s_h0p, 1)
                if blk >= 2:
                    pe.wait_ge(s_h0r, blk - 1)
                for i in range(BLK):
                    t = BLK * blk + i
                    last = mm(bank[2 + blk % 2][:, P * i:P * i + P], xT[:, P * t:P * t + P], wbt[:, t // 2, :],
                              start=True, stop=True)
                last.then_inc(s_r0p, 1)
                if blk == 0:
                    pe.wait_ge(s_gate, 16)
                else:
                    logits(blk - 1)
            logits(NB - 1)

            pe.wait_ge(s_fold, 64)
            for e in range(E):
                for c in range(C2):
                    last = mm(bank[5 + e // 4][:, P * (e % 4):P * (e % 4) + P], w12in[:, 0, e, c], w12in[:, 1, e, c],
                              start=(c == 0), stop=(c == C2 - 1))
            last.then_inc(s_w12p, 1)
            pe.wait_ge(s_b1z, 1)
            for e in range(E):
                for c in range(C2):
                    last = mm(bank[7][0:E, 0:D], b1z[:, e, c], w12in[:, 1, e, c],
                              start=(e == 0 and c == 0), stop=(e == E - 1 and c == C2 - 1))
            last.then_inc(s_cp, 1)

            pe.wait_ge(s_taken, 1)
            mm(bank[4][:, 128:256], before_b[:], taken[:].rearrange("p t e -> p (t e)"), start=True, stop=True)
            mm(bank[4][:, 256:384], ones_b[:], taken[:].rearrange("p t e -> p (t e)"),
               start=True, stop=True).then_inc(s_pre, 1)
            pe.wait_ge(s_c8, 1)
            mm(bank[7][:, 128:256], K("repeat8")[0:E], c_e[:], start=True, stop=True).then_inc(s_c2p, 1)

            def shared_gu(n):
                blk, c = n // 2, n % 2
                if n >= 2:
                    pe.wait_ge(s_sact, n - 1)
                for i in range(2):
                    last = mm(bank[2 * c + i][0:SC, :], sgu[:, FS * i + SC * c:FS * i + SC * c + SC],
                              h0T[:, 512 * blk:512 * blk + 512], start=True, stop=True)
                last.then_inc(s_sgp, 1)

            def shared_down(blk):
                pe.wait_ge(s_sact, 2 * blk + 2)
                if blk >= 2:
                    pe.wait_ge(s_xs, blk - 1)
                for i in range(BLK):
                    for c in range(2):
                        last = mm(bank[5 + blk % 2][:, P * i:P * i + P], sact[:, blk % 2, c, P * i:P * i + P],
                                  sd[:, c], start=(c == 0), stop=(c == 1))
                last.then_inc(s_sdp, 1)

            pe.wait_ge(s_sh, 48)
            pe.wait_ge(s_h0r, NB)
            shared_gu(0)
            shared_gu(1)
            pe.wait_ge(s_onehot, 1)
            for i in range(2 * NT):
                last = mm(bank[4][:, 384:384 + SLOT_TILES], ohlo[:, i, :], ohhi[:, i], start=(i == 0), stop=(i == 2 * NT - 1))
            last.then_inc(s_tab, 1)
            pe.wait_ge(s_w12, 2)
            for n in range(2, 2 * NB):
                shared_gu(n)
                if n % 2:
                    shared_down(n // 2 - 1)
            shared_down(NB - 1)

            def turn_x(j, r4, ring):
                pe.wait_ge(s_xg[r4], (j // 4 + 1) * 16 if isinstance(j, int) else 16 * 0 + turn_x.count)
                if ring:
                    pe.wait_ge(s_xe, j)
                pe.transpose(bank[6][:, 0:P], xg[:, r4], ident).then_inc(s_X, 1)

            def gate_up(j, r, ring):
                e = pe.value_load(eslot[0:1, j:j + 1] if isinstance(j, int) else eslot[0:1, bass.ds(j, 1)],
                                  min_val=0, max_val=E - 1)
                pe.wait_ge(s_xe, j + 1)
                if ring:
                    pe.wait_ge(s_hm, j - 1)
                mm(bank[2 * r][:, 0:F0], xgT[:, r], wgu[:, bass.ds(e * (2 * F0), F0)], start=True, stop=True)
                mm(bank[2 * r + 1][:, 0:F0], xgT[:, r], wgu[:, bass.ds(e * (2 * F0) + F0, F0)],
                   start=True, stop=True).then_inc(s_G, 1)

            def turn_hid(j, r, ring):
                pe.wait_ge(s_hm, j + 1)
                if ring:
                    pe.wait_ge(s_he, j - 1)
                for c in range(3):
                    last = pe.transpose(bank[4 + r][:, P * c:P * c + P], hid[:, r, P * c:P * c + P], ident)
                last.then_inc(s_H, 1)

            def down(j, r, ring):
                e = pe.value_load(eslot[0:1, j:j + 1] if isinstance(j, int) else eslot[0:1, bass.ds(j, 1)],
                                  min_val=0, max_val=E - 1)
                pe.wait_ge(s_he, j + 1)
                if ring:
                    pe.wait_ge(s_ye, j)
                for c in range(3):
                    last = mm(bank[7][:, 0:P], hidT[:, r, P * c:P * c + P],
                              wd[:, bass.ds(e, 1), c, :].rearrange("p a d -> p (a d)"), start=(c == 0), stop=(c == 2))
                last.then_inc(s_D, 1)

            pe.wait_ge(s_exp0, 32)
            pe.wait_ge(s_slots, 1)
            pe.wait_ge(s_xs, NB)
            turn_x(0, 0, False)
            for j in range(4):
                gate_up(j, j % 2, j >= 2)
                turn_x(j + 1, (j + 1) % 4, True)
                if j >= 1:
                    turn_hid(j - 1, (j - 1) % 2, j >= 3)
                if j >= 2:
                    down(j - 2, j % 2, j >= 3)
            with pe.Fori(1, SLOT_TILES // 4 - 1) as jj:
                for u in range(4):
                    j = jj * 4 + u
                    turn_x.count = (jj + (2 if u == 3 else 1)) * 16
                    gate_up(j, u % 2, True)
                    turn_x(j + 1, (u + 1) % 4, True)
                    turn_hid(j - 1, (u + 1) % 2, True)
                    down(j - 2, u % 2, True)
            for j in range(SLOT_TILES - 4, SLOT_TILES + 2):
                if j < SLOT_TILES:
                    gate_up(j, j % 2, True)
                if j + 1 < SLOT_TILES:
                    turn_x(j + 1, (j + 1) % 4, True)
                if j - 1 < SLOT_TILES:
                    turn_hid(j - 1, (j - 1) % 2, True)
                down(j - 2, j % 2, True)

            def turn_x1(b, par):
                pe.wait_ge(s_x1, b + 1)
                for i in range(2):
                    last = pe.transpose(bank[6 + par][:, P * i:P * i + P], x1t[:, par, i], ident)
                last.then_inc(s_x1p, 1)

            def weights(k):
                return wk[k] if k < 2 else wsh

            def gemma_gu(b, par, hh, ring):
                k, q = hh // 2, hh % 2
                if q == 0 and k < 2:
                    pe.wait_ge(s_wk[k], (b + 1) * 16)
                if hh == 0:
                    pe.wait_ge(s_x1T, b + 1)
                if ring:
                    pe.wait_ge(s_m1, b * 6 + (hh - 1))
                w = weights(k)
                for i in range(2):
                    for c in range(2):
                        a = F1 * i + P * (2 * q + c)
                        last = mm(bank[2 * i + hh % 2][:, N * c:N * c + N], w[:, a:a + P], x1T[:, par],
                                  start=True, stop=True)
                last.then_inc(s_gu1, 1)

            def gemma_down(b, hh, first):
                k, q = hh // 2, hh % 2
                pe.wait_ge(s_m1, b * 6 + (hh + 1))
                if hh == 0 and not first:
                    pe.wait_ge(s_z, b)
                w = weights(k)
                for c in range(2):
                    a = 2 * F1 + P * (2 * q + c)
                    last = mm(bank[4][:, 0:N], w[:, a:a + P], hb[:, hh % 2, N * c:N * c + N],
                              start=(hh == 0 and c == 0), stop=(hh == 5 and c == 1), skip_group_check=True)
                last.then_inc(s_dn, 1)

            def pe_row(b, par, first=False, last=False):
                for hh in range(6):
                    gemma_gu(b, par, hh, not (first and hh < 2))
                    if hh > 0:
                        gemma_down(b, hh - 1, first)
                    elif not first:
                        gemma_down(b - 1, 5, False)
                    if hh == 4 and not last:
                        turn_x1(b + 1, 1 - par)

            pe.wait_ge(s_wsh, 16)
            turn_x1(0, 0)
            pe_row(0, 0, first=True)
            pe_row(1, 1)
            with pe.Fori(1, B // 2 - 1) as bp:
                for u in range(2):
                    pe_row(bp * 2 + u, u)
            pe_row(B - 2, 0)
            pe_row(B - 1, 1, last=True)
            gemma_down(B - 1, 5, False)

            pe.wait_ge(s_attw, 64)
            pe.wait_ge(s_z, B)
            for blk in range(NB):
                if blk >= 2:
                    pe.wait_ge(s_qk, blk - 1)
                    pe.wait_ge(s_kk, 2 * (blk - 1))
                    pe.wait_ge(s_ka, 2 * (blk - 1))
                for i in range(2):
                    last = mm(bank[2 * (blk % 2) + i][:], wqkv[:, D * i:D * i + D], zT[:, 512 * blk:512 * blk + 512],
                              start=True, stop=True)
                last.then_inc(s_qkp, 1)
            pe.wait_ge(s_qk, NB)
            pe.wait_ge(s_kk, 2 * NB)
            pe.wait_ge(s_ka, 2 * NB)
            for i in range(G + 4 + 1):
                g = i
                if g < G:
                    if g >= 2:
                        pe.wait_ge(s_pr, H * (g - 1))
                    mm(bank[g % 2][:], group(qT, g), kz[:, g].rearrange("p h k -> p (h k)"), start=True, stop=False)
                    mm(bank[g % 2][:], ident_b[:], mask_b[:].rearrange("p h k -> p (h k)"),
                       start=False, stop=True).then_inc(s_S, 1)
                    if g >= 1:
                        pe.wait_ge(s_vv, g)
                    mm(bank[2][:, 0:P], group(zT, g), wqkv[:, 2 * D:3 * D],
                       start=True, stop=True).then_inc(s_V, 1)
                g = i - 1
                if 0 <= g < G:
                    pe.wait_ge(s_pr, H * (g + 1))
                    if g >= 1:
                        pe.wait_ge(s_pe, g)
                    for h in range(H):
                        last = pe.transpose(bank[5][:, P * h:P * h + P], pr[:, g % 2, h], ident)
                    last.then_inc(s_PT, 1)
                g = i - 2
                if 0 <= g < G:
                    pe.wait_ge(s_pe, g + 1)
                    pe.wait_ge(s_vv, g + 1)
                    if g >= 1:
                        pe.wait_ge(s_att, g)
                    for h in range(H):
                        last = mm(bank[3][:, HD * h:HD * h + HD], prT[:, g % 2, P * h:P * h + P], vv[:, g % 3, HD * h:HD * h + HD],
                                  start=True, stop=True)
                    last.then_inc(s_O, 1)
                g = i - 3
                if 0 <= g < G:
                    pe.wait_ge(s_att, g + 1)
                    if g >= 1:
                        pe.wait_ge(s_ae, g)
                    pe.transpose(bank[6][:, 0:P], att[:, g % 2], ident).then_inc(s_AT, 1)
                    pe.wait_ge(s_ae, g + 1)
                    if g >= 1:
                        pe.wait_ge(s_res, g)
                    o = bank[4][:, 0:P]
                    mm(o, group(zT, g), ident, start=True, stop=False)
                    mm(o, attT[:, g % 2], wo[:], start=False, stop=True).then_inc(s_Y, 1)
                g = i - 4
                if 0 <= g < G:
                    pe.wait_ge(s_y1, g + 1)
                    if g >= 1:
                        pe.wait_ge(s_yT, g)
                    pe.transpose(bank[7][:, 0:P], y1[:, g], ident).then_inc(s_YT, 1)
            pe.wait_ge(s_yT, G)
            for g in range(G):
                last = mm(bank[2][:, E * g:E * g + E], y1T[:, g], wg[:], start=True, stop=True)
            last.then_inc(s_l1, 1)

            pe.wait_ge(s_oh1, 1)
            flat = lambda t: t[:].rearrange("p g e -> p (g e)")
            mm(bank[7][:, 0:P], rowm["row_before"][:], flat(tsum_b), start=True, stop=False)
            mm(bank[7][:, 0:P], rowm["row_same"][:], flat(exb), start=False, stop=False)
            mm(bank[7][:, 0:P], rowm["row_same_before"][:], flat(oh1b), start=False, stop=True).then_inc(s_loc, 1)
            pe.wait_ge(s_gk, 1)
            pe.transpose(bank[5][:, 0:P], flat(gk), ident).then_inc(s_gkp, 1)
            pe.wait_ge(s_gkT, 1)
            pe.wait_ge(s_cblk, 1)
            for blk in range(NB):
                mm(bank[blk][:], gkT[:], cblk[:, BLK * blk:BLK * blk + BLK].rearrange("p g d -> p (g d)"),
                   start=True, stop=True).then_inc(s_bp, 1)
            for g in range(G):
                if g >= 2:
                    pe.wait_ge(s_prod, g - 1)
                else:
                    pe.wait_ge(s_base, NB)
                for i in range(2):
                    last = mm(bank[4 + 2 * (g % 2) + i][:], y1T[:, g], W12[:, 512 * i:512 * i + 512], start=True, stop=True)
                last.then_inc(s_ym, 1)

        @block.vector
        def _(dve):
            v = nc.vector
            chain = [0]

            def link(ins):
                chain[0] += 1
                ins.then_inc(s_dve, 1)
                dve.wait_ge(s_dve, chain[0])

            def row(ap, n):
                return ap.unsqueeze(1).broadcast_to([P, n, ap.shape[-1]])

            def col(ap, n=E):
                return ap.unsqueeze(2).broadcast_to([P, ap.shape[-1], n])

            def first_max(vals, n, top, index, onehot, tmp):
                link(v.tensor_reduce(top, vals, AX.X, ALU.max))
                link(v.tensor_tensor(tmp, vals, col(top), ALU.is_lt))
                link(v.scalar_tensor_tensor(out=tmp, in0=tmp, scalar=float(E), in1=row(K("iota")[:, 0:E], n),
                                            op0=ALU.mult, op1=ALU.add))
                link(v.tensor_reduce(index, tmp, AX.X, ALU.min))
                link(v.tensor_tensor(onehot, row(K("iota")[:, 0:E], n), col(index), ALU.is_equal))

            def rsqrt(out, var):
                link(v.tensor_scalar(var_e[:], var, EPS, None, ALU.add))
                link(v.tensor_scalar(out.bitcast(I32), var_e[:].bitcast(I32), 1, None, ALU.logical_shift_right))
                link(v.tensor_scalar(out.bitcast(I32), out.bitcast(I32), -1.0, float(0x5f3759df), ALU.mult, ALU.add))
                for _ in range(3):
                    link(v.tensor_tensor(newton[:], out, out, ALU.mult))
                    link(v.scalar_tensor_tensor(out=newton[:], in0=newton[:], scalar=-0.5, in1=var_e[:],
                                                op0=ALU.mult, op1=ALU.mult))
                    link(v.scalar_tensor_tensor(out=out, in0=newton[:], scalar=1.5, in1=out, op0=ALU.add, op1=ALU.mult))

            dve.wait_ge(s_cond, 80)
            link(v.tensor_tensor(cw[:, 1], cw[:, 0], row(cmask[:], E), ALU.mult))
            for half in range(2):
                for e in range(E):
                    for b in range(4 * half, 4 * half + 4):
                        y = y_bc[:, E * b + e:E * b + e + 1]
                        if e == 0:
                            ins = v.tensor_scalar(wbt[:, b], cw[:, 1, e], y, None, ALU.mult)
                        else:
                            dve.wait_ge(s_dve, chain[0] - 3)
                            ins = v.scalar_tensor_tensor(out=wbt[:, b], in0=cw[:, 1, e], scalar=y, in1=wbt[:, b],
                                                         op0=ALU.mult, op1=ALU.add)
                        chain[0] += 1
                        ins.then_inc(s_dve, 1)
                for b in range(4):
                    dve.wait_ge(s_dve, chain[0] - 3 + b)
                    dve.sem_inc(s_wb, 1)
            yv = y_bc[:].rearrange("p (b e) -> p b e", b=B)
            link(v.tensor_reduce(cs[:, 0], yv, AX.X, ALU.max))
            v.tensor_tensor(cd[:], yv, col(cs[:, 0]), ALU.subtract).then_inc(s_cd, 1)
            for blk in range(NB):
                dve.wait_ge(s_r0p, blk + 1)
                v.tensor_tensor(h0r[:, BLK * blk:BLK * blk + BLK], bank[2 + blk % 2][:].rearrange("p (t d) -> p t d", t=BLK),
                                row(cbias_bc, BLK), ALU.add).then_inc(s_h0r, 1)
            dve.wait_ge(s_lgp, NB)
            dve.wait_ge(s_const, 16)
            link(v.tensor_copy(lg[:], bank[4][:, 0:NT * E].rearrange("p (t e) -> p t e", t=NT)))
            first_max(lg[:], NT, mtop[0][:], itop[0][:], oh[0][:], t8[:])
            link(v.scalar_tensor_tensor(out=lgb[:], in0=oh[0][:], scalar=-BIG, in1=lg[:], op0=ALU.mult, op1=ALU.add))
            first_max(lgb[:], NT, mtop[1][:], itop[1][:], oh[1][:], t8[:])
            v.tensor_tensor(taken[:], oh[0][:], oh[1][:], ALU.add).then_inc(s_taken, 1)
            v.tensor_tensor(dlt[:], mtop[1][:], mtop[0][:], ALU.subtract).then_inc(s_dlt, 1)
            dve.wait_ge(s_cp, 1)
            v.tensor_tensor(c_e[:], bank[7][0:E, 0:D], b2[:], ALU.add).then_inc(s_c8, 1)
            dve.wait_ge(s_pre, 1)
            link(v.tensor_copy(tot[:].rearrange("p e t -> p t e"), bank[4][:, 256:384].rearrange("p (t e) -> p t e", t=NT)))
            link(v.tensor_tensor_scan(incl[:].rearrange("p e t -> p (e t)"), K("restart"),
                                      tot[:].rearrange("p e t -> p (e t)"), 0.0, ALU.mult, ALU.add))
            link(v.tensor_scalar(cnt[:, 0], incl[:, :, NT - 1], float(P - 1), None, ALU.add))
            link(v.tensor_copy(cnt_i[:], cnt[:, 0]))
            link(v.tensor_scalar(cnt_i[:], cnt_i[:], -P, None, ALU.bitwise_and))
            link(v.tensor_copy(cnt[:, 2], cnt_i[:]))
            link(v.tensor_tensor_scan(cnt[:, 3], K("ones")[:, 0:E], cnt[:, 2], 0.0, ALU.mult, ALU.add))
            link(v.tensor_tensor(cnt[:, 4], cnt[:, 3], cnt[:, 2], ALU.subtract))
            link(v.tensor_tensor(excl[:], incl[:], tot[:], ALU.subtract))
            link(v.tensor_tensor(Q[:], bank[4][:, 128:256].rearrange("p (t e) -> p t e", t=NT),
                                 excl[:].rearrange("p e t -> p t e"), ALU.add))
            link(v.tensor_tensor(Q[:], Q[:], row(cnt[:, 4], NT), ALU.add))
            for k in range(2):
                link(v.tensor_tensor(t8[:], oh[k][:], Q[:], ALU.mult))
                link(v.tensor_reduce(pos[:, k], t8[:], AX.X, ALU.add))
            link(v.tensor_copy(pos_u[:], pos[:]))
            flat_pos = pos_u[:].rearrange("p k t -> p (k t)")
            v.tensor_scalar(lo_i[:], flat_pos, P - 1, None, ALU.bitwise_and)
            link(v.tensor_scalar(hi_i[:], flat_pos, P.bit_length() - 1, None, ALU.logical_shift_right))
            v.tensor_copy(lo[:], lo_i[:])
            link(v.tensor_copy(hi[:], hi_i[:]))
            v.tensor_tensor(ohlo, row(K("iota"), 2 * NT), col(lo[:], P), ALU.is_equal)
            link(v.tensor_tensor(ohhi[:], row(K("iota")[:, 0:SLOT_TILES], 2 * NT), col(hi[:], SLOT_TILES), ALU.is_equal))
            link(v.tensor_tensor(ohhi[:].rearrange("p (k t) s -> p k t s", k=2), ohhi[:].rearrange("p (k t) s -> p k t s", k=2),
                                 K("token").unsqueeze(1).unsqueeze(3).broadcast_to([P, 2, NT, SLOT_TILES]), ALU.mult))
            dve.sem_inc(s_onehot, 1)
            dve.sem_inc(s_pos, 1)
            link(v.tensor_tensor(cmp[:], row(cnt[:, 3], SLOT_TILES), col(K("tile_start")), ALU.is_le))
            link(v.tensor_reduce(ecnt[:], cmp[:], AX.X, ALU.add))
            link(v.tensor_scalar(ecnt[:], ecnt[:], float(E - 1), None, ALU.min))
            link(v.tensor_copy(eslot[:], ecnt[:]))
            dve.wait_ge(s_tab, 1)
            v.tensor_copy(slot_tok[:], bank[4][:, 384:384 + SLOT_TILES]).then_inc(s_slots, 1)
            dve.wait_ge(s_edl, 1)
            link(v.tensor_scalar(sdl[:], edl[:], 1.0, None, ALU.add))
            link(v.reciprocal(pk[:, 0], sdl[:]))
            link(v.tensor_tensor(pk[:, 1], edl[:], pk[:, 0], ALU.mult))
            dve.wait_ge(s_ce, 1)
            link(v.tensor_reduce(cs[:, 1], ce[:], AX.X, ALU.add))
            link(v.reciprocal(cs[:, 2], cs[:, 1]))
            link(v.tensor_tensor(rw[:], ce[:], col(cs[:, 2]), ALU.mult))
            first_max(rw[:], B, cs[:, 3], cs[:, 4], coh[:], c8[:])
            link(v.tensor_copy(cix[:, 0], cs[:, 4]))
            link(v.scalar_tensor_tensor(out=rwb[:], in0=coh[:], scalar=-BIG, in1=rw[:], op0=ALU.mult, op1=ALU.add))
            first_max(rwb[:], B, cs[:, 5], cs[:, 4], coh[:], c8[:])
            link(v.tensor_copy(cix[:, 1], cs[:, 4]))
            link(v.tensor_tensor(cs[:, 6], cs[:, 3], cs[:, 5], ALU.add))
            link(v.reciprocal(cs[:, 7], cs[:, 6]))
            for k, m in enumerate((3, 5)):
                link(v.tensor_tensor(cs[:, m], cs[:, m], cs[:, 7], ALU.mult))
                link(v.tensor_scalar(cs[:, 6], cs[:, m], SKILL_SCALE, None, ALU.mult))
                link(v.scalar_tensor_tensor(out=cwt[:, k], in0=cs[:, m], scalar=1.0 - SKILL_SCALE, in1=cs[:, 6],
                                            op0=ALU.mult, op1=ALU.add))
            dve.sem_inc(s_cr, 1)

            def shared_xs(blk):
                dve.wait_ge(s_sdp, blk + 1)
                t = xs[:, BLK * blk:BLK * blk + BLK]
                v.tensor_tensor(t, bank[5 + blk % 2][:].rearrange("p (t d) -> p t d", t=BLK), t, ALU.add).then_inc(s_xs, 1)

            dve.wait_ge(s_sh, 48)
            for n in range(2 * NB):
                dve.wait_ge(s_ssl, n + 1)
                if n >= 4:
                    dve.wait_ge(s_sdp, n // 2 - 1)
                v.tensor_tensor(sact[:, (n // 2) % 2, n % 2], sgl[:, n % 2], bank[2 * (n % 2) + 1][0:SC, :],
                                ALU.mult).then_inc(s_sact, 1)
                if n % 2 and n > 1:
                    shared_xs(n // 2 - 1)
            shared_xs(NB - 1)

            def xgT_copy(j, r, ring):
                dve.wait_ge(s_X, j + 1)
                if ring:
                    dve.wait_ge(s_G, j - 1)
                v.tensor_copy(xgT[:, r], bank[6][:, 0:P]).then_inc(s_xe, 1)

            def hidden(j, r, ring):
                dve.wait_ge(s_sl, j + 1)
                if ring:
                    dve.wait_ge(s_H, j - 1)
                v.tensor_tensor(hid[:, r, 0:F0], slu[:, r], bank[2 * r + 1][:, 0:F0], ALU.mult).then_inc(s_hm, 1)

            def y_copy(j, r4, stored):
                dve.wait_ge(s_D, j + 1)
                if stored is not None:
                    dve.wait_ge(s_yst[r4], stored)
                v.tensor_copy(ysb[:, r4], bank[7][:, 0:P]).then_inc(s_ye, 1)

            dve.wait_ge(s_hpad, 1)
            xgT_copy(0, 0, False)
            for j in range(4):
                xgT_copy(j + 1, (j + 1) % 2, j >= 1)
                hidden(j, j % 2, j >= 2)
                if j >= 2:
                    y_copy(j - 2, j - 2, None)
            for j in range(4, 6):
                xgT_copy(j + 1, (j + 1) % 2, True)
                hidden(j, j % 2, True)
                y_copy(j - 2, j - 2, None)
            with dve.Fori(1, (SLOT_TILES - 4) // 4) as jj:
                for u in range(4):
                    j = jj * 4 + (u + 2)
                    xgT_copy(j + 1, (u + 1) % 2, True)
                    hidden(j, u % 2, True)
                    y_copy(j - 2, u, jj * 16)
            for j in range(SLOT_TILES - 2, SLOT_TILES + 2):
                if j + 1 < SLOT_TILES:
                    xgT_copy(j + 1, (j + 1) % 2, True)
                if j < SLOT_TILES:
                    hidden(j, j % 2, True)
                y_copy(j - 2, (j - 2) % 4, 16 * ((j - 2) // 4))

            def x1_row(b, par, stored):
                dve.wait_ge(s_yg[par], stored["gathered"])
                for i in range(2):
                    t = b * 2 + i
                    v.scalar_tensor_tensor(out=half1[:, i], in0=yg[:, par, i, 0], scalar=stored["p"](0, t),
                                           in1=stored["xs"](t), op0=ALU.mult, op1=ALU.add).then_inc(s_half, 1)
                if stored["old"] is not None:
                    dve.wait_ge(s_x1p, stored["old"])
                    dve.wait_ge(s_x1st, stored["old"] * 16)
                for i in range(2):
                    t = b * 2 + i
                    dve.wait_ge(s_half, b * 2 + i + 1)
                    ins = v.scalar_tensor_tensor(out=x1t[:, par, i], in0=yg[:, par, i, 1], scalar=stored["p"](1, t),
                                                 in1=half1[:, i], op0=ALU.mult, op1=ALU.add)
                    ins.then_inc(s_x1h, 1)
                dve.wait_ge(s_x1h, b * 2 + 2)
                dve.sem_inc(s_x1, 1)

            def row_args(b, gathered, old):
                if isinstance(b, int):
                    return dict(gathered=gathered, old=old, p=lambda k, t: pk[:, k, t:t + 1], xs=lambda t: xs[:, t])
                return dict(gathered=gathered, old=old, p=lambda k, t: pk[:, k, bass.ds(t, 1)],
                            xs=lambda t: xs[:, bass.ds(t, 1), :].rearrange("p a d -> p (a d)"))

            def gemma_hid(b, hh, ring):
                k = hh // 2
                dve.wait_ge(s_gl, b * 6 + (hh + 1))
                if ring:
                    dve.wait_ge(s_dn, b * 6 + (hh - 1))
                if k < 2:
                    w = cwt[:, k, b:b + 1] if isinstance(b, int) else cwt[:, k, bass.ds(b, 1)]
                    ins = v.scalar_tensor_tensor(out=hb[:, hh % 2], in0=gl[:, hh % 2], scalar=w,
                                                 in1=bank[2 + hh % 2][:], op0=ALU.mult, op1=ALU.mult)
                else:
                    ins = v.tensor_tensor(hb[:, hh % 2], gl[:, hh % 2], bank[2 + hh % 2][:], ALU.mult)
                ins.then_inc(s_m1, 1)

            def dve_row(b, par, gathered, old, first=False, last=False):
                for hh in range(6):
                    gemma_hid(b, hh, not (first and hh < 2))
                    if hh == 2 and not last:
                        x1_row(b + 1, 1 - par, row_args(b, gathered, old))

            x1_row(0, 0, row_args(0, 64, None))
            dve_row(0, 0, 64, None, first=True)
            dve_row(1, 1, 128, 1)
            with dve.Fori(1, B // 2 - 1) as bp:
                dve_row(bp * 2, 0, bp * 64 + 64, bp * 2)
                dve_row(bp * 2 + 1, 1, bp * 64 + 128, bp * 2 + 1)
            dve_row(B - 2, 0, 64 * (B // 2), B - 2)
            dve_row(B - 1, 1, None, None, last=True)

            dve.wait_ge(s_attw, 64)
            v.tensor_scalar(bq_s[:], bqkv[:, 0:1], HD ** -0.5, None, ALU.mult).then_inc(s_bq, 1)
            for blk in range(NB):
                dve.wait_ge(s_qkp, blk + 1)
                dve.wait_ge(s_kz0, G)
                for h in range(2, 4):
                    a = HD * h
                    v.tensor_scalar(
                        kz[a:a + HD, BLK * blk:BLK * blk + BLK, h, :],
                        bank[2 * (blk % 2) + 1][a:a + HD, :].rearrange("p (g k) -> p g k", g=BLK),
                        bqkv[a:a + HD, 1:2], None, ALU.add).then_inc(s_kk, 1)
            for i in range(G + 4):
                g = i
                if g < G:
                    dve.wait_ge(s_S, g + 1)
                    if g >= 2:
                        dve.wait_ge(s_pr, H * (g - 1))
                    v.tensor_reduce(nmax[:, g % 2], bank[g % 2][:].rearrange("p (h k) -> p h k", h=H), AX.X, ALU.max,
                                    negate=True).then_inc(s_nm, 1)
                    dve.wait_ge(s_V, g + 1)
                    if g >= 3:
                        dve.wait_ge(s_O, g - 2)
                    v.tensor_tensor(vv[:, g % 3], bank[2][:, 0:P], bv_bc, ALU.add).then_inc(s_vv, 1)
                g = i - 1
                if 0 <= g < G:
                    dve.wait_ge(s_pr, H * (g + 1))
                    if g >= 2:
                        dve.wait_ge(s_att, g - 1)
                    v.reciprocal(rden[:, g % 2], den[:, g % 2]).then_inc(s_rd, 1)
                    dve.wait_ge(s_PT, g + 1)
                    if g >= 2:
                        dve.wait_ge(s_O, g - 1)
                    v.tensor_copy(prT[:, g % 2], bank[5][:]).then_inc(s_pe, 1)
                g = i - 2
                if 0 <= g < G:
                    dve.wait_ge(s_O, g + 1)
                    dve.wait_ge(s_rd, g + 1)
                    if g >= 2:
                        dve.wait_ge(s_AT, g - 1)
                    v.tensor_tensor(att[:, g % 2].rearrange("p (h d) -> p h d", h=H),
                                    bank[3][:, 0:P].rearrange("p (h d) -> p h d", h=H),
                                    col(rden[:, g % 2], HD), ALU.mult).then_inc(s_att, 1)
                g = i - 3
                if 0 <= g < G:
                    dve.wait_ge(s_Y, g + 1)
                    link(v.tensor_tensor(res[:, g % 2], bank[4][:, 0:P], bo_bc, ALU.add))
                    dve.sem_inc(s_res, 1)
                    link(v.bn_stats(st1[:, g % 2], res[:, g % 2]))
                    link(v.bn_aggr(mv1[:, g % 2], st1[:, g % 2]))
                    rsqrt(rs1[:, g % 2], mv1[:, g % 2, 1:2])
                    if g >= 2:
                        dve.wait_ge(s_ng1, g - 1)
                    v.tensor_scalar(nrm[:, g % 2], res[:, g % 2], mv1[:, g % 2, 0:1], rs1[:, g % 2], ALU.subtract,
                                    ALU.mult).then_inc(s_nr1, 1)

            dve.wait_ge(s_l1, 1)
            link(v.tensor_copy(lg1[:], bank[2][:, 0:P].rearrange("p (g e) -> p g e", g=G)))
            link(v.tensor_reduce(sm1[:, 0], lg1[:], AX.X, ALU.max))
            v.tensor_tensor(t8[:], lg1[:], col(sm1[:, 0]), ALU.subtract).then_inc(s_gap1, 1)
            dve.wait_ge(s_e1, 1)
            first_max(e1[:], G, sm1[:, 1], sm1[:, 2], oh1[:], Q[:])
            link(v.tensor_copy(oh1b[:], oh1[:]))
            by_e = oh1[:].rearrange("p g e -> p e g")
            link(v.tensor_copy(tot[:], by_e))
            link(v.tensor_tensor_scan(incl[:].rearrange("p e t -> p (e t)"), K("restart"),
                                      tot[:].rearrange("p e t -> p (e t)"), 0.0, ALU.mult, ALU.add))
            link(v.tensor_tensor(exb[:].rearrange("p g e -> p e g"), incl[:], tot[:], ALU.subtract))
            link(v.tensor_copy(tsum_b[:], row(incl[:, :, G - 1], G)))
            dve.sem_inc(s_oh1, 1)
            link(v.tensor_reduce(sm1[:, 3], e1[:], AX.X, ALU.add))
            link(v.reciprocal(sm1[:, 4], sm1[:, 3]))
            link(v.tensor_tensor(sm1[:, 4], sm1[:, 4], sm1[:, 1], ALU.mult))
            dve.wait_ge(s_loc, 1)
            link(v.tensor_tensor(t8[:], bank[7][:, 0:P].rearrange("p (g e) -> p g e", g=G), oh1[:], ALU.mult))
            link(v.tensor_reduce(sm1[:, 5], t8[:], AX.X, ALU.add))
            link(v.tensor_scalar(sm1[:, 5], sm1[:, 5], float(CAP), None, ALU.is_lt))
            link(v.tensor_tensor(sm1[:, 4], sm1[:, 4], sm1[:, 5], ALU.mult))
            v.tensor_tensor(gk[:], oh1[:], col(sm1[:, 4]), ALU.mult).then_inc(s_gk, 1)
            for blk in range(NB):
                dve.wait_ge(s_bp, blk + 1)
                v.tensor_tensor(base[:, BLK * blk:BLK * blk + BLK], bank[blk][:].rearrange("p (g d) -> p g d", g=BLK),
                                y1[:, BLK * blk:BLK * blk + BLK], ALU.add).then_inc(s_base, 1)
            dve.wait_ge(s_gk, 1)
            dve.wait_ge(s_x1g, 16 * B)
            for g in range(G):
                dve.wait_ge(s_ym, g + 1)
                if g == 0:
                    dve.wait_ge(s_base, NB)
                for i in range(2):
                    ins = v.tensor_tensor(prod[:, g % 2, 4 * i:4 * i + 4], bank[4 + 2 * (g % 2) + i][:].rearrange("p (e d) -> p e d", e=4),
                                          col(gk[:, g, 4 * i:4 * i + 4], D), ALU.mult)
                link(ins)
                dve.sem_inc(s_prod, 1)
                link(v.tensor_reduce(msum[:, g % 2], prod[:, g % 2].rearrange("p e d -> p d e"), AX.X, ALU.add))
                link(v.tensor_tensor(res[:, g % 2], msum[:, g % 2], base[:, g], ALU.add))
                link(v.bn_stats(st1[:, g % 2], res[:, g % 2]))
                link(v.bn_aggr(mv1[:, g % 2], st1[:, g % 2]))
                rsqrt(rs1[:, g % 2], mv1[:, g % 2, 1:2])
                link(v.tensor_scalar(nrm[:, g % 2], res[:, g % 2], mv1[:, g % 2, 0:1], rs1[:, g % 2], ALU.subtract, ALU.mult))
                link(v.tensor_tensor(nrg[:, g % 2], nrm[:, g % 2], g2_bc, ALU.mult))
                link(v.tensor_tensor(nrg[:, g % 2], nrg[:, g % 2], n2_bc, ALU.add))
                if g >= 4:
                    dve.wait_ge(s_fst[g % 4], 16 * (g // 4))
                v.tensor_tensor(fin[:, g % 4], nrg[:, g % 2], x1g[:, g], ALU.add).then_inc(s_fo, 1)


def kernel(**a):
    import concourse.bacc as bacc
    from concourse.bass_utils import run_bass_kernel_spmd

    a = {k: np.asarray(v) for k, v in a.items()}
    x = a["x"].reshape(T, D)

    def chunked(w, p=P):
        w = w.reshape(*w.shape[:-2], w.shape[-2] // p, p, w.shape[-1])
        return np.moveaxis(w, -2, 0)

    wd = np.zeros((P, E, 3, D), np.float32)
    wd[:, :, 0:2] = chunked(a["L0_ffn_Wd"][:, 0:2 * P])
    wd[0:F0 - 2 * P, :, 2] = np.moveaxis(a["L0_ffn_Wd"][:, 2 * P:], 1, 0)

    def gemma(gate, up, down):
        d = np.moveaxis(down.reshape(-1, C1, P, D), 2, 1).reshape(-1, P, C1 * D)
        return np.concatenate([gate.reshape(-1, D, F1), up.reshape(-1, D, F1), d], axis=2)

    c = {k[3:]: v for k, v in a.items() if k.startswith("L1_")}
    ins = {
        "xT": x.T,
        "x_rows": x,
        "cond": a["cond_8"],
        "cw": a["L0_cond_weight"].transpose(2, 0, 1),
        "cmask": a["L0_cond_mask"].T,
        "cbias": a["L0_cond_bias"].reshape(D, 1),
        "vecs": np.stack([a["L0_cond_bias"], c["ffn_in_proj_b"][2 * D:], c["ffn_out_proj_b"], c["ffn_ln1_g"],
                          c["ffn_ln1_b"], c["ffn_ln2_g"], c["ffn_ln2_b"]]),
        "consts": shape_constants(),
        "gate_w": a["L0_ffn_gate_w"],
        "wgu": np.moveaxis(np.concatenate([a["L0_ffn_Wg"], a["L0_ffn_Wu"]], axis=2), 1, 0).reshape(D, E * 2 * F0),
        "wd": wd,
        "sgu": np.concatenate([a["L0_ffn_Sg"], a["L0_ffn_Su"]], axis=1),
        "sd": chunked(a["L0_ffn_Sd"], SC),
        "wexp": gemma(c["cond_skill_gate"], c["cond_skill_up"], c["cond_skill_down"]),
        "wsh": gemma(c["cond_shared_gate"], c["cond_shared_up"], c["cond_shared_down"])[0],
        "w1": chunked(c["ffn_w1"].transpose(0, 2, 1)),
        "w2": chunked(c["ffn_w2"]),
        "b1": c["ffn_b1"].reshape(E, C2, P).transpose(2, 0, 1),
        "b2": c["ffn_b2"],
        "wqkv": c["ffn_in_proj_w"].T,
        "wo": c["ffn_out_proj_w"].T,
        "bqkv": c["ffn_in_proj_b"].reshape(3, D).T,
        "wg": c["ffn_wg"],
    }
    nc = bacc.Bacc("TRN2", target_bir_lowering=False, num_devices=1)
    arrays, args = {}, []
    for name, v in ins.items():
        v = np.ascontiguousarray(v)
        arrays[f"in_{name}"] = v
        args.append(nc.dram_tensor(f"in_{name}", v.shape, mybir.dt.from_np(v.dtype), kind="ExternalInput").ap())
    args.append(nc.dram_tensor("out", [B, N, D], F32, kind="ExternalOutput").ap())
    block_kernel(nc, *args)
    r = run_bass_kernel_spmd(nc, [arrays], core_ids=[0])
    return r.results[0]["out"]
```

```python
from contextlib import ExitStack

import concourse.bass as bass
from concourse import mybir
import numpy as np

ALU = mybir.AluOpType
ACT = mybir.ActivationFunctionType
AX = mybir.AxisListType
F32 = mybir.dt.float32
F16 = mybir.dt.float16
BF16 = mybir.dt.bfloat16
I32 = mybir.dt.int32
U32 = mybir.dt.uint32

P = 128
B, N, D = 8, 256, 128
T = B * N
NT = T // P
E = 8
F0 = 352
FS = 176
SC = FS // 2
F1 = 512
C1 = F1 // P
C2 = 512 // P
H, HD = 4, 32
G, GN = 16, 16
CAP = T // E
SLOT_TILES = 2 * T // P + E
BIG = 3.0e38
EPS = 1e-5
SKILL_SCALE = 1.0 / 12.0
BLK = 4
NB = NT // BLK

CONST = {}
_at = 0
for _name, _width in (("ident", P), ("iota", P), ("before", P), ("row_before", P), ("row_same", P),
                      ("row_same_before", P), ("mask", P), ("token", NT), ("tile_start", SLOT_TILES),
                      ("restart", E * G), ("ones", P), ("eye8", E * E), ("own_group", G), ("repeat8", P)):
    CONST[_name] = (_at, _at + _width)
    _at += _width
CONST_W = _at


def shape_constants():
    k = np.arange(P)[:, None]
    m = np.arange(P)[None, :]
    c = np.zeros((P, CONST_W), np.float32)

    def put(name, a):
        c[:, CONST[name][0]:CONST[name][1]] = a

    put("ident", k == m)
    put("iota", m + 0 * k)
    put("before", k < m)
    put("row_before", k // GN < m // GN)
    put("row_same", k // GN == m // GN)
    put("row_same_before", (k // GN == m // GN) & (k < m))
    put("mask", np.where((k - m) % GN == 0, 0.0, -1.0e30))
    put("token", k + P * np.arange(NT)[None, :])
    put("tile_start", P * np.arange(SLOT_TILES)[None, :] + 0 * k)
    put("restart", (np.arange(E * G)[None, :] % G != 0) + 0 * k)
    put("ones", 1.0)
    put("eye8", np.eye(E).reshape(1, -1) + 0 * k)
    put("own_group", k // E == np.arange(G)[None, :])
    put("repeat8", (k < E) & (m % E == k))
    return c


def block_kernel(nc, xT_d, x_d, cond_d, cw_d, cmask_d, cbias_d, vecs_d, const_d, gate_d, wgu_d, wd_d,
                 sgu_d, sd_d, wexp_d, wsh_d, w1_d, w2_d, b1_d, b2_d, wqkv_d, wo_d, bqkv_d, wg_d, cols1_d, out_d):
    with ExitStack() as ctx:
        def sb(name, shape, dt=F32):
            return ctx.enter_context(nc.sbuf_tensor(name, shape, dt))

        def sem(name):
            return ctx.enter_context(nc.semaphore(name))

        bank = [ctx.enter_context(nc.psum_tensor(f"bank{i}", [P, 512], F32)) for i in range(8)]

        h0_rows = nc.dram_tensor("h0_rows", [T, D], F32, kind="Internal").ap()
        y_rows = nc.dram_tensor("y_rows", [SLOT_TILES * P, D], F32, kind="Internal").ap()
        x1_rows = nc.dram_tensor("x1_rows", [T, D], F32, kind="Internal").ap()

        xT = sb("xT", [P, T])
        y_bc = sb("y_bc", [P, B * E])
        cw = sb("cw", [P, 2, E, P])
        cmask = sb("cmask", [P, P])
        cbias = sb("cbias", [P, 1])
        vecs = sb("vecs", [P, 7, P])
        cbias_bc, bv_bc, bo_bc, g1_bc, n1_bc, g2_bc, n2_bc = (vecs[:, i, :] for i in range(7))
        const = sb("const", [P, CONST_W])
        gate_w = sb("gate_w", [P, E])
        wgu = sb("wgu", [P, E * 2 * F0])
        wd = sb("wd", [P, E, 3, D])
        sgu = sb("sgu", [P, 2 * FS])
        sd = sb("sd", [SC, 2, D])
        wk = [sb(f"wk{k}", [P, 3 * F1]) for k in range(2)]
        wsh = sb("wsh", [P, 3 * F1])
        w12in = sb("w12in", [P, 2, E, C2, P])
        b1 = sb("b1", [P, E, C2])
        b2T = sb("b2T", [P, E])
        wqkv = sb("wqkv", [P, 3 * D])
        wo = sb("wo", [P, D])
        bqkv = sb("bqkv", [P, 3])
        wg = sb("wg", [P, E])

        def K(name):
            return const[:, CONST[name][0]:CONST[name][1]]

        wbt = sb("wbt", [P, B, P])
        h0T = sb("h0T", [P, T])
        h0r = sb("h0r", [P, NT, D])
        xs = sb("xs", [P, NT, D])
        lg = sb("lg", [P, NT, E])
        lgb = sb("lgb", [P, NT, E])
        oh = [sb(f"oh{k}", [P, NT, E]) for k in range(2)]
        mtop = [sb(f"mtop{k}", [P, NT]) for k in range(2)]
        itop = [sb(f"itop{k}", [P, NT]) for k in range(2)]
        t8 = sb("t8", [P, NT, E])
        taken = sb("taken", [P, NT, E], BF16)
        before_b = sb("before_b", [P, P], BF16)
        ones_b = sb("ones_b", [P, P], BF16)
        dlt = sb("dlt", [P, NT])
        edl = sb("edl", [P, NT])
        sdl = sb("sdl", [P, NT])
        pk = sb("pk", [P, 2, NT])
        tot = sb("tot", [P, E, NT])
        incl = sb("incl", [P, E, NT])
        excl = sb("excl", [P, E, NT])
        cnt = sb("cnt", [P, 6, E])
        Q = sb("Q", [P, NT, E])
        pos = sb("pos", [P, 2, NT])
        lo = sb("lo", [P, 2 * NT])
        hi = sb("hi", [P, 2 * NT])
        lo_i = sb("lo_i", [P, 2 * NT], U32)
        hi_i = sb("hi_i", [P, 2 * NT], U32)
        cnt_i = sb("cnt_i", [P, E], I32)
        pos_u = sb("pos_u", [P, 2, NT], U32)
        prod = sb("prod", [P, 2, E, D])
        ohlo = prod[:].rearrange("p a e d -> p (a e d)").bitcast(F16).rearrange("p (i s) -> p i s", s=P)
        ohhi = sb("ohhi", [P, 2 * NT, SLOT_TILES], F16)
        slot_tok = sb("slot_tok", [P, SLOT_TILES], U32)
        cmp = sb("cmp", [P, SLOT_TILES, E])
        ecnt = sb("ecnt", [P, SLOT_TILES])
        eslot = sb("eslot", [P, SLOT_TILES], I32)
        sgl = sb("sgl", [SC, 2, 512])
        sul = cw[0:SC, 0].rearrange("p e d -> p (e d)").rearrange("p (a n) -> p a n", a=2)
        sdn = h0r[:, 0:2 * BLK]
        acts = sb("acts", [P, 4, 512])
        sact = acts[0:SC].rearrange("p (a c) n -> p a c n", a=2)
        xg = sb("xg", [P, 4, D])
        xgT = sb("xgT", [P, 2, P])
        hidT = prod[:].rearrange("p a e d -> p (a e d)")[:, 0:6 * P].rearrange("p (a n) -> p a n", a=2)
        slu = prod[:].rearrange("p a e d -> p (a e d)")[:, 6 * P:6 * P + 2 * F0].rearrange("p (a n) -> p a n", a=2)
        hid = sb("hid", [P, 2, 3 * P])
        ysb = sb("ysb", [P, 4, D])
        yg = sb("yg", [P, 2, 2, 2, D])
        cd = sb("cd", [P, B, E])
        ce = sb("ce", [P, B, E])
        rw = sb("rw", [P, B, E])
        rwb = sb("rwb", [P, B, E])
        c8 = sb("c8", [P, B, E])
        coh = sb("coh", [P, B, E])
        cs = sb("cs", [P, 8, B])
        cwt = sb("cwt", [P, 2, B])
        cix = sb("cix", [P, 2, B], I32)
        cols1 = sb("cols1", [P, 2])
        half1 = sb("half1", [P, 2, D])
        x1t = sb("x1t", [P, 2, 2, D])
        x1T = sb("x1T", [P, 2, N])
        gl = acts[:, 0:2]
        hb = acts[:, 2:4]
        zT = xT
        W12 = wbt[:].rearrange("p b d -> p (b d)")
        c_rep = sb("c_rep", [P, G, E])
        c_ge = sb("c_ge", [P, D])
        qT = h0T
        bq_s = sb("bq_s", [P, 1])
        kz = w12in[:, :, :, :, :].rearrange("p a e c d -> p (a e c d)").rearrange(
            "p (g h k) -> p g h k", g=G, h=H)
        mask_b = sb("mask_b", [P, H, P], BF16)
        ident_b = sb("ident_b", [P, P], BF16)
        nmax = sb("nmax", [P, 2, H])
        pr = gl.rearrange("p a (h k) -> p a h k", h=H)
        den = sb("den", [P, 2, H])
        rden = sb("rden", [P, 2, H])
        prT = hb
        vv = xs

        def batches(buffer):
            return buffer.rearrange("p (a j d) -> p a j d", a=2, j=BLK)

        att = batches(wk[0][:, 0:1024])
        attT = wk[1][:, 0:1024].rearrange("p (a n) -> p a n", a=2)
        res = batches(wsh[:, 0:1024])
        prod_flat = prod[:].rearrange("p a e d -> p (a e d)")
        nrm = batches(prod_flat[:, 0:1024])
        nrg = batches(prod_flat[:, 1024:2048])
        part = prod_flat.rearrange("p (a e d) -> p a e d", a=4, e=E // 2)
        st1 = sb("st1", [P, 2, BLK, 6])
        mv1 = sb("mv1", [P, 2, BLK, 2])
        var_e = sb("var_e", [P, 2, BLK])
        rs1 = sb("rs1", [P, 2, BLK])
        newton = sb("newton", [P, 2, BLK])
        half_var = sb("half_var", [P, 2, BLK])
        warm = sb("warm", [P, 1])
        shift1 = sb("shift1", [P, 2, BLK])
        y1 = h0r
        y1T = cw[:, :, :, :].rearrange("p a e d -> p (a e) d")
        x1g = wgu[:, 0:T].rearrange("p (g d) -> p g d", g=G)
        cblk = wgu[:, T:2 * T].rearrange("p (g d) -> p g d", g=G)
        lg1 = lg
        e1 = lgb
        oh1 = oh[0]
        oh1b = sb("oh1b", [P, G, E], BF16)
        rowm = {n: sb(n + "_b", [P, P], BF16) for n in ("row_before", "row_same", "row_same_before")}
        tsum = sb("tsum", [P, E])
        tsum_b = sb("tsum_b", [P, G, E], BF16)
        exb = sb("exb", [P, G, E], BF16)
        gk = sb("gk", [P, G, E])
        sm1 = sb("sm1", [P, 6, G])
        gkT = sb("gkT", [P, P])
        base = xs
        macc = batches(acts[:, 0:2].rearrange("p a n -> p (a n)"))
        fin = batches(acts[:, 2:4].rearrange("p a n -> p (a n)"))
        nrm2 = att
        nrg2 = batches(wk[1][:, 0:1024])

        s_xT, s_cond, s_const, s_gate, s_sh, s_exp0, s_fold, s_wsh, s_attw = (
            sem(n) for n in ("xT_in", "cond_in", "const_in", "gate_in", "shared_in", "experts_in",
                             "fold_in", "gemma_shared_in", "attention_in"))
        s_dve = sem("dve_chain")
        s_wb, s_h0p, s_r0p, s_h0, s_h0r, s_h0st, s_lgp = (
            sem(n) for n in ("cond_weights", "h0T_product", "h0_rows_product", "h0T_ready",
                             "h0_rows_ready", "h0_rows_stored", "logits_product"))
        s_ssu, s_sde = sem("shared_up_copied"), sem("shared_down_copied")
        s_pool = sem("pool_chain")
        s_castb, s_taken, s_pre, s_dlt, s_edl, s_onehot, s_tab, s_slots, s_pos = (
            sem(n) for n in ("constants_cast", "taken_ready", "prefix_product", "gap_ready",
                             "gap_exp", "onehots_ready", "slot_table_product", "slots_ready",
                             "positions_ready"))
        s_cd, s_ce, s_cr = sem("cond_gap_ready"), sem("cond_exp"), sem("cond_router_ready")
        s_w12p, s_w12, s_cp, s_c8, s_c2p, s_cge = (
            sem(n) for n in ("w12_product", "w12_ready", "c_product", "c_ready",
                             "c_repeat_product", "c_repeat_ready"))
        s_sgp, s_ssl, s_sact, s_sdp, s_xs = (
            sem(n) for n in ("shared_gu", "shared_silu", "shared_act", "shared_down", "xs_ready"))
        s_hpad = sem("hid_padding")
        s_xg = [sem(f"xg_in{i}") for i in range(4)]
        s_X, s_xe, s_G, s_sl, s_hm, s_H, s_he, s_D, s_ye = (
            sem(n) for n in ("xg_turned", "xgT_ready", "gu_product", "silu_ready", "hid_ready",
                             "hid_turned", "hidT_ready", "down_product", "y_ready"))
        s_yst = [sem(f"y_stored{i}") for i in range(4)]
        s_yg = [sem(f"yg_in{i}") for i in range(2)]
        s_half, s_x1, s_x1st, s_x1p, s_x1T = (
            sem(n) for n in ("x1_half", "x1_ready", "x1_stored", "x1_turned", "x1T_ready"))
        s_x1h = sem("x1_half_rows")
        s_wk = [sem(f"skill_in{k}") for k in range(2)]
        s_gu1, s_gl, s_m1, s_dn, s_z = (
            sem(n) for n in ("gemma_gu", "gelu_ready", "gemma_hid", "gemma_down", "z_ready"))
        s_kz0, s_bq, s_qkp, s_qk, s_kk, s_ka = (
            sem(n) for n in ("kz_zeroed", "bq_scaled", "qk_product", "q_ready", "keys_ready_vector", "keys_ready_scalar"))
        s_S, s_V, s_nm, s_vv, s_pr, s_rd, s_PT, s_pe, s_O, s_att = (
            sem(n) for n in ("scores_product", "v_product", "score_max", "v_ready", "probs_ready",
                             "rden_ready", "probs_turned", "probsT_ready", "o_product", "att_ready"))
        s_AT, s_ae, s_Y, s_res, s_y1, s_YT, s_yT = (
            sem(n) for n in ("att_turned", "attT_ready", "proj_product", "residual_ready",
                             "y1_ready", "y1_turned", "y1T_ready"))
        s_seed, s_rs1, s_rs1v, s_nr1, s_xb, s_acc, s_seed2, s_rs2, s_rs2v, s_nr2, s_fov = (
            sem(n) for n in ("norm1_seed", "norm1_scale_ready", "norm1_last_scale_ready", "norm1_scaled",
                             "x1_plus_bias", "moe_accumulated", "norm2_seed", "norm2_scale_ready",
                             "norm2_last_scale_ready", "norm2_scaled", "last_final_ready"))
        s_l1, s_gap1, s_e1, s_oh1, s_loc, s_gk, s_gkp, s_gkT, s_bp, s_base = (
            sem(n) for n in ("moe_logits", "moe_gap", "moe_exp", "moe_onehot", "moe_location",
                             "moe_gates", "gates_turned", "gatesT_ready", "bias_product",
                             "base_ready"))
        s_x1g, s_cblk, s_ym, s_fo, s_lgc, s_part, s_psum = (
            sem(n) for n in ("x1_grouped_in", "cblk_ready", "moe_product", "final_ready",
                             "moe_logits_copied", "moe_parts_ready", "moe_parts_summed"))
        s_fst = [sem(f"out_stored{i}") for i in range(2)]

        group = lambda ap, g: ap[:, P * g:P * g + P]

        block = ctx.enter_context(nc.Block())

        @block.sync
        def _(sp):
            sp.dma_start(y_bc[:], cond_d.rearrange("b e -> (b e)").partition_broadcast(P)).then_inc(s_cond, 16)
            sp.dma_start(cw[:, 0], cw_d).then_inc(s_cond, 16)
            sp.dma_start(cmask[:], cmask_d).then_inc(s_cond, 16)
            sp.dma_start(cbias[:], cbias_d).then_inc(s_cond, 16)
            sp.dma_start(vecs[:], vecs_d.partition_broadcast(P)).then_inc(s_cond, 16)
            sp.dma_start(xT[:], xT_d).then_inc(s_xT, 16)
            sp.dma_start(gate_w[:], gate_d).then_inc(s_gate, 16)
            sp.dma_start(const[:], const_d).then_inc(s_const, 16)
            sp.dma_start(sgu[:], sgu_d).then_inc(s_sh, 16)
            sp.dma_start(sd[:], sd_d).then_inc(s_sh, 16)
            sp.dma_start(xs[:], x_d.rearrange("(t p) d -> p t d", p=P)).then_inc(s_sh, 16)
            sp.dma_start(wgu[:], wgu_d).then_inc(s_exp0, 16)
            sp.dma_start(wd[:], wd_d).then_inc(s_exp0, 16)
            for blk in range(NB):
                sp.wait_ge(s_h0r, blk + 1)
                sp.dma_start(h0_rows[512 * blk:512 * blk + 512, :].rearrange("(t p) d -> p t d", p=P),
                             h0r[:, BLK * blk:BLK * blk + BLK, :]).then_inc(s_h0st, 16)
            sp.dma_start(w12in[:, 0], w1_d).then_inc(s_fold, 16)
            sp.dma_start(w12in[:, 1], w2_d).then_inc(s_fold, 16)
            sp.dma_start(b1[:], b1_d).then_inc(s_fold, 16)
            sp.dma_start(b2T[:], b2_d).then_inc(s_fold, 16)
            sp.dma_start(wsh[:], wsh_d).then_inc(s_wsh, 16)
            sp.dma_start(wqkv[:], wqkv_d).then_inc(s_attw, 16)
            sp.dma_start(wo[:], wo_d).then_inc(s_attw, 16)
            sp.dma_start(bqkv[:], bqkv_d).then_inc(s_attw, 16)
            sp.dma_start(wg[:], wg_d).then_inc(s_attw, 16)
            sp.dma_start(cols1[:], cols1_d).then_inc(s_attw, 16)
            sp.wait_ge(s_cr, 1)
            for k in range(2):
                e = sp.value_load(cix[0:1, k, 0:1], min_val=0, max_val=E - 1)
                sp.dma_start(wk[k][:], wexp_d[bass.ds(e, 1), :, :].rearrange("a p n -> (a p) n")).then_inc(s_wk[k], 16)
            with sp.Fori(0, SLOT_TILES // 4) as jj:
                for r in range(4):
                    sp.wait_ge(s_ye, jj * 4 + r + 1)
                    sp.dma_start(y_rows[bass.ds((jj * 4 + r) * P, P), :], ysb[:, r, :]).then_inc(s_yst[r], 16)

            def store_x1(b, par):
                sp.wait_ge(s_x1, b + 1)
                sp.dma_start(x1_rows[bass.ds(b * N, N), :].rearrange("(t p) d -> p t d", p=P),
                             x1t[:, par]).then_inc(s_x1st, 16)

            def load_skill(b, k):
                sp.wait_ge(s_dn, b * 6 - 6 + 2 * (k + 1))
                e = sp.value_load(cix[0:1, k, bass.ds(b, 1)], min_val=0, max_val=E - 1)
                sp.dma_start(wk[k][:], wexp_d[bass.ds(e, 1), :, :].rearrange("a p n -> (a p) n")).then_inc(s_wk[k], 16)

            store_x1(0, 0)
            with sp.Fori(0, B // 2 - 1) as bp:
                for u in range(2):
                    load_skill(bp * 2 + u + 1, 0)
                    store_x1(bp * 2 + u + 1, (u + 1) % 2)
                    load_skill(bp * 2 + u + 1, 1)
            load_skill(B - 1, 0)
            store_x1(B - 1, 1)
            load_skill(B - 1, 1)
            sp.wait_ge(s_x1st, 16 * B)
            for l in range(B):
                sp.dma_start(x1g[GN * l:GN * l + GN, :, :],
                             x1_rows[N * l:N * l + N, :].rearrange("(g n) d -> n g d", n=GN)).then_inc(s_x1g, 16)
            for q in range(NB):
                if q < NB - 1:
                    sp.wait_ge(s_fo, q + 1)
                else:
                    sp.wait_ge(s_fov, 1)
                for j in range(BLK):
                    g = BLK * q + j
                    sp.dma_start(out_d[:, GN * g:GN * g + GN, :], fin[:, q % 2, j, :]).then_inc(s_fst[q % 2], 16)
            for r in range(2):
                sp.wait_ge(s_fst[r], 16 * G // 2)

        @block.gpsimd
        def _(pool):
            nc.gpsimd.memset(hid[:], 0.0).then_inc(s_hpad, 1)
            pool.wait_ge(s_const, 16)
            nc.gpsimd.tensor_copy(before_b[:], K("before")).then_inc(s_castb, 1)
            nc.gpsimd.tensor_copy(ones_b[:], K("ones")).then_inc(s_castb, 1)
            nc.gpsimd.tensor_copy(ident_b[:], K("ident")).then_inc(s_castb, 1)
            nc.gpsimd.tensor_copy(mask_b[:], K("mask").unsqueeze(1).broadcast_to([P, H, P])).then_inc(s_castb, 1)
            for n in rowm:
                nc.gpsimd.tensor_copy(rowm[n][:], K(n)).then_inc(s_castb, 1)
            pool.wait_ge(s_sh, 48)

            def shared_xs(blk):
                pool.wait_ge(s_sde, blk + 1)
                t = xs[:, BLK * blk:BLK * blk + BLK]
                nc.gpsimd.tensor_tensor(t, sdn[:, BLK * (blk % 2):BLK * (blk % 2) + BLK], t, ALU.add).then_inc(s_xs, 1)

            for n in range(2 * NB):
                pool.wait_ge(s_ssl, n + 1)
                pool.wait_ge(s_ssu, n + 1)
                if n >= 4:
                    pool.wait_ge(s_sdp, n // 2 - 1)
                nc.gpsimd.tensor_tensor(sact[:, (n // 2) % 2, n % 2], sgl[:, n % 2], sul[:, n % 2], ALU.mult).then_inc(s_sact, 1)
                if n % 2 and n > 1:
                    shared_xs(n // 2 - 1)
            pool.wait_ge(s_h0st, 16 * NB)
            pool.wait_ge(s_slots, 1)
            for j in range(SLOT_TILES):
                if j >= 4:
                    pool.wait_ge(s_X, j - 3)
                nc.gpsimd.indirect_dma_start(
                    out=xg[:, j % 4, :], out_offset=None, in_=h0_rows,
                    in_offset=bass.IndirectOffsetOnAxis(ap=slot_tok[:, j:j + 1], axis=0)).then_inc(s_xg[j % 4], 16)
                if j == 3:
                    shared_xs(NB - 1)
            for r in range(4):
                pool.wait_ge(s_yst[r], 16 * (SLOT_TILES // 4))
            pool.wait_ge(s_pos, 1)
            for b in range(B):
                if b >= 2:
                    pool.wait_ge(s_x1, b - 1)
                for i in range(2):
                    for k in range(2):
                        nc.gpsimd.indirect_dma_start(
                            out=yg[:, b % 2, i, k, :], out_offset=None, in_=y_rows,
                            in_offset=bass.IndirectOffsetOnAxis(ap=pos_u[:, k, 2 * b + i:2 * b + i + 1], axis=0)
                        ).then_inc(s_yg[b % 2], 16)
                if b == 1:
                    pool.wait_ge(s_w12p, 2)
                    pool.wait_ge(s_cp, 1)
                if b >= 1 and b < 5:
                    for g in range(BLK * (b - 1), BLK * b):
                        nc.gpsimd.memset(kz[:, g], 0.0).then_inc(s_kz0, 1)
                if b == 5:
                    pool.wait_ge(s_cge, 1)
                    nc.gpsimd.tensor_tensor(cblk, c_ge[:].unsqueeze(1).broadcast_to([P, G, D]),
                                            K("own_group").unsqueeze(2).broadcast_to([P, G, D]),
                                            ALU.mult).then_inc(s_cblk, 1)
            chain = [0]

            def link(ins):
                chain[0] += 1
                ins.then_inc(s_pool, 1)
                pool.wait_ge(s_pool, chain[0])

            def newton_steps(q):
                w, z, v = rs1[:, q % 2], newton[:, q % 2], var_e[:, q % 2]
                for _ in range(3):
                    link(nc.gpsimd.tensor_tensor(z, w, w, ALU.mult))
                    link(nc.gpsimd.tensor_tensor(z, z, v, ALU.mult))
                    link(nc.gpsimd.tensor_scalar(z, z, -0.5, 1.5, ALU.mult, ALU.add))
                    link(nc.gpsimd.tensor_tensor(w, w, z, ALU.mult))

            def rows(vec):
                return vec.unsqueeze(1).broadcast_to([P, BLK, D])

            def scale_and_shift(q):
                newton_steps(q)
                link(nc.gpsimd.tensor_tensor(shift1[:, q % 2], mv1[:, q % 2, :, 0], rs1[:, q % 2], ALU.mult))
                return nc.gpsimd.tensor_scalar(shift1[:, q % 2], shift1[:, q % 2], -1.0, None, ALU.mult)

            for q in range(NB):
                if q < NB - 1:
                    pool.wait_ge(s_seed, q + 1)
                    scale_and_shift(q).then_inc(s_rs1, 1)
                pool.wait_ge(s_nr1, BLK * (q + 1))
                link(nc.gpsimd.tensor_tensor(nrg[:, q % 2], nrm[:, q % 2], rows(g1_bc), ALU.mult))
                nc.gpsimd.tensor_tensor(y1[:, BLK * q:BLK * q + BLK], nrg[:, q % 2], rows(n1_bc), ALU.add).then_inc(s_y1, 1)
                if q == 0:
                    pool.wait_ge(s_x1g, 16 * B)
                    nc.gpsimd.tensor_tensor(x1g, x1g, n2_bc.unsqueeze(1).broadcast_to([P, G, D]), ALU.add).then_inc(s_xb, 1)
            for g in range(G):
                pool.wait_ge(s_part, E // 2 * (g + 1))
                t = part[:, g % 4]
                link(nc.gpsimd.tensor_tensor(t[:, 0:2], t[:, 0:2], t[:, 2:4], ALU.add))
                nc.gpsimd.tensor_tensor(t[:, 0], t[:, 0], t[:, 1], ALU.add).then_inc(s_psum, 1)
                if g % BLK == 1 and g > BLK:
                    q = g // BLK - 1
                    pool.wait_ge(s_seed2, q + 1)
                    scale_and_shift(q).then_inc(s_rs2, 1)
                if g % BLK == 3 and g > BLK:
                    q = g // BLK - 1
                    pool.wait_ge(s_nr2, BLK * (q + 1))
                    link(nc.gpsimd.tensor_tensor(nrg2[:, q % 2], nrm2[:, q % 2], rows(g2_bc), ALU.mult))
                    if q == 0:
                        pool.wait_ge(s_xb, 1)
                    if q >= 2:
                        pool.wait_ge(s_fst[q % 2], 16 * BLK * (q // 2))
                    nc.gpsimd.tensor_tensor(fin[:, q % 2], nrg2[:, q % 2], x1g[:, BLK * q:BLK * q + BLK], ALU.add).then_inc(s_fo, 1)

        @block.scalar
        def _(act):
            act.wait_ge(s_cond, 80)
            for blk in range(NB):
                act.wait_ge(s_h0p, blk + 1)
                nc.scalar.activation(h0T[:, 512 * blk:512 * blk + 512], bank[blk % 2][:], ACT.Identity,
                                     bias=cbias[:]).then_inc(s_h0, 1)
            act.wait_ge(s_cd, 1)
            nc.scalar.activation(ce[:], cd[:], ACT.Exp).then_inc(s_ce, 1)
            def shared_down_copy(blk):
                act.wait_ge(s_sdp, blk + 1)
                if blk >= 2:
                    act.wait_ge(s_xs, blk - 1)
                nc.scalar.activation(sdn[:, BLK * (blk % 2):BLK * (blk % 2) + BLK],
                                     bank[5][:].rearrange("p (t d) -> p t d", t=BLK), ACT.Copy).then_inc(s_sde, 1)

            for n in range(2 * NB):
                act.wait_ge(s_sgp, n + 1)
                if n >= 2:
                    act.wait_ge(s_sact, n - 1)
                nc.scalar.activation(sgl[:, n % 2], bank[n % 2][0:SC, :], ACT.Silu).then_inc(s_ssl, 1)
                nc.scalar.activation(sul[:, n % 2], bank[2 + n % 2][0:SC, :], ACT.Copy).then_inc(s_ssu, 1)
                if n == 3:
                    act.wait_ge(s_h0st, 16 * NB)
                if n % 2 and n > 1:
                    shared_down_copy(n // 2 - 1)
            act.wait_ge(s_dlt, 1)
            nc.scalar.activation(edl[:], dlt[:], ACT.Exp).then_inc(s_edl, 1)
            shared_down_copy(NB - 1)
            nc.scalar.activation(warm[:], cbias[:], ACT.Silu)
            act.wait_ge(s_w12p, 1)
            nc.scalar.activation(W12[:, 0:512], bank[2][:], ACT.Copy).then_inc(s_w12, 1)

            def silu(j, r, ring):
                act.wait_ge(s_G, j + 1)
                if ring:
                    act.wait_ge(s_hm, j - 1)
                nc.scalar.activation(slu[:, r], bank[2 * r][:, 0:F0], ACT.Silu).then_inc(s_sl, 1)

            def hidT_copy(j, r, ring):
                act.wait_ge(s_H, j + 1)
                if ring:
                    act.wait_ge(s_D, j - 1)
                nc.scalar.activation(hidT[:, r], bank[4 + r][:, 0:3 * P], ACT.Copy).then_inc(s_he, 1)

            silu(0, 0, False)
            silu(1, 1, False)
            hidT_copy(0, 0, False)
            silu(2, 0, True)
            hidT_copy(1, 1, False)
            silu(3, 1, True)
            hidT_copy(2, 0, True)
            with act.Fori(1, SLOT_TILES // 4) as jj:
                for u in range(4):
                    silu(jj * 4 + u, u % 2, True)
                    hidT_copy(jj * 4 + (u - 1), (u + 1) % 2, True)
            hidT_copy(SLOT_TILES - 1, 1, True)

            def x1T_copy(b, par):
                act.wait_ge(s_x1p, b + 1)
                nc.scalar.activation(x1T[:, par], bank[6 + par][:, 0:N], ACT.Copy).then_inc(s_x1T, 1)

            def gelu(b, hh, ring):
                act.wait_ge(s_gu1, b * 6 + (hh + 1))
                if ring:
                    act.wait_ge(s_m1, b * 6 + (hh - 1))
                nc.scalar.activation(gl[:, hh % 2], bank[hh % 2][:], ACT.Gelu_apprx_tanh).then_inc(s_gl, 1)

            def z_copy(b):
                act.wait_ge(s_dn, b * 6 + 6)
                nc.scalar.activation(zT[:].rearrange("p (g l n) -> p g l n", g=G, l=B)[:, :, bass.ds(b, 1), :].rearrange("p g a n -> p g (a n)"),
                                     bank[4][:, 0:N].rearrange("p (g n) -> p g n", g=G), ACT.Copy).then_inc(s_z, 1)

            def act_row(b, par, first=False, last=False):
                for hh in range(6):
                    gelu(b, hh, not (first and hh < 2))
                    if hh == 0 and not first:
                        z_copy(b - 1)
                    if hh == 4 and not last:
                        x1T_copy(b + 1, 1 - par)

            act.wait_ge(s_w12p, 2)
            nc.scalar.activation(W12[:, 512:1024], bank[3][:], ACT.Copy).then_inc(s_w12, 1)
            nc.scalar.activation(warm[:], cbias[:], ACT.Gelu_apprx_tanh)
            x1T_copy(0, 0)
            act.wait_ge(s_c2p, 1)
            nc.scalar.activation(c_ge[:], bank[5][:, 0:P], ACT.Copy).then_inc(s_cge, 1)
            act_row(0, 0, first=True)
            act_row(1, 1)
            with act.Fori(1, B // 2 - 1) as bp:
                for u in range(2):
                    act_row(bp * 2 + u, u)
            act_row(B - 2, 0)
            act_row(B - 1, 1, last=True)
            z_copy(B - 1)

            act.wait_ge(s_attw, 80)
            act.wait_ge(s_bq, 1)
            for blk in range(NB):
                act.wait_ge(s_qkp, blk + 1)
                nc.scalar.activation(qT[:, 512 * blk:512 * blk + 512], bank[2 * (blk % 2)][:], ACT.Identity,
                                     bias=bq_s[:], scale=HD ** -0.5).then_inc(s_qk, 1)
                act.wait_ge(s_kz0, G)
                for h in range(2):
                    a = HD * h
                    nc.scalar.activation(
                        kz[a:a + HD, BLK * blk:BLK * blk + BLK, h, :],
                        bank[2 * (blk % 2) + 1][a:a + HD, :].rearrange("p (g k) -> p g k", g=BLK),
                        ACT.Identity, bias=bqkv[a:a + HD, 1:2]).then_inc(s_ka, 1)
            for i in range(G + 7):
                if i < G:
                    act.wait_ge(s_nm, i + 1)
                    if i >= 2:
                        act.wait_ge(s_PT, i - 1)
                        act.wait_ge(s_rd, i - 1)
                    for h in range(H):
                        nc.scalar.activation(pr[:, i % 2, h], bank[i % 2][:, P * h:P * h + P], ACT.Exp,
                                             bias=nmax[:, i % 2, h:h + 1],
                                             accum_out=den[:, i % 2, h:h + 1]).then_inc(s_pr, 1)
                if i % BLK == 2 and i >= 6 and (i - 6) // BLK < NB:
                    q = (i - 6) // BLK
                    act.wait_ge(s_AT, q + 1)
                    if q >= 2:
                        act.wait_ge(s_Y, q - 1)
                    nc.scalar.activation(attT[:, q % 2], bank[5][:], ACT.Copy).then_inc(s_ae, 1)
                if i % BLK == 0 and i >= 8:
                    q = (i - 8) // BLK
                    if q < NB - 1:
                        act.wait_ge(s_rs1, q + 1)
                    else:
                        act.wait_ge(s_rs1v, 1)
                    if q >= 2:
                        act.wait_ge(s_YT, q - 1)
                        act.wait_ge(s_y1, q - 1)
                    for j in range(BLK):
                        nc.scalar.activation(nrm[:, q % 2, j], res[:, q % 2, j], ACT.Identity,
                                             bias=shift1[:, q % 2, j:j + 1], scale=rs1[:, q % 2, j:j + 1]).then_inc(s_nr1, 1)
                if i % BLK == 1 and i >= 9:
                    q = (i - 9) // BLK
                    act.wait_ge(s_YT, q + 1)
                    nc.scalar.activation(y1T[:, BLK * q:BLK * q + BLK], bank[7][:].rearrange("p (g k) -> p g k", g=BLK),
                                         ACT.Identity, bias=cols1[:, 1:2], scale=cols1[:, 0:1]).then_inc(s_yT, 1)
            act.wait_ge(s_gap1, 1)
            nc.scalar.activation(e1[:], t8[:], ACT.Exp).then_inc(s_e1, 1)
            act.wait_ge(s_gkp, 1)
            nc.scalar.activation(gkT[:], bank[5][:, 0:P], ACT.Copy).then_inc(s_gkT, 1)

            def normalise2(q):
                if q < NB - 1:
                    act.wait_ge(s_rs2, q + 1)
                else:
                    act.wait_ge(s_rs2v, 1)
                if q >= 2:
                    act.wait_ge(s_fo, q - 1)
                for j in range(BLK):
                    nc.scalar.activation(nrm2[:, q % 2, j], macc[:, q % 2, j], ACT.Identity,
                                         bias=shift1[:, q % 2, j:j + 1], scale=rs1[:, q % 2, j:j + 1]).then_inc(s_nr2, 1)

            act.wait_ge(s_y1, NB)
            act.wait_ge(s_gk, 1)
            for g in range(G):
                act.wait_ge(s_ym, g + 1)
                if g >= 4:
                    act.wait_ge(s_acc, g - 3)
                for e in range(E // 2):
                    nc.scalar.activation(part[:, g % 4, e], bank[2 * (g % 4) + 1][:, D * e:D * e + D], ACT.Copy,
                                         scale=gk[:, g, E // 2 + e:E // 2 + e + 1]).then_inc(s_part, 1)
                if g % BLK == 3 and g > BLK:
                    normalise2(g // BLK - 1)
            normalise2(NB - 1)

        @block.tensor
        def _(pe):
            ident = K("ident")
            mm = nc.tensor.matmul
            pe.wait_ge(s_xT, 16)

            def logits(blk):
                pe.wait_ge(s_h0, blk + 1)
                for t in range(BLK * blk, BLK * blk + BLK):
                    last = mm(bank[4][:, E * t:E * t + E], h0T[:, P * t:P * t + P], gate_w[:], start=True, stop=True)
                last.then_inc(s_lgp, 1)

            for blk in range(NB):
                pe.wait_ge(s_wb, blk + 1)
                if blk >= 2:
                    pe.wait_ge(s_h0, blk - 1)
                for i in range(2):
                    b = 2 * blk + i
                    last = mm(bank[blk % 2][:, N * i:N * i + N], wbt[:, b, :], xT[:, N * b:N * b + N],
                              start=True, stop=True)
                last.then_inc(s_h0p, 1)
                if blk == 1:
                    pe.wait_ge(s_gate, 16)
                if blk >= 1:
                    logits(blk - 1)
                if blk >= 2:
                    pe.wait_ge(s_h0r, blk - 1)
                for i in range(BLK):
                    t = BLK * blk + i
                    last = mm(bank[2 + blk % 2][:, P * i:P * i + P], xT[:, P * t:P * t + P], wbt[:, t // 2, :],
                              start=True, stop=True)
                last.then_inc(s_r0p, 1)
            logits(NB - 1)

            def prefixes():
                pe.wait_ge(s_castb, 4 + len(rowm))
                pe.wait_ge(s_taken, 1)
                mm(bank[4][:, 128:256], before_b[:], taken[:].rearrange("p t e -> p (t e)"), start=True, stop=True)
                mm(bank[4][:, 256:384], ones_b[:], taken[:].rearrange("p t e -> p (t e)"),
                   start=True, stop=True).then_inc(s_pre, 1)

            def shared_gu(n):
                blk, c = n // 2, n % 2
                if n >= 2:
                    pe.wait_ge(s_ssl, n - 1)
                    pe.wait_ge(s_ssu, n - 1)
                for i in range(2):
                    last = mm(bank[2 * i + c][0:SC, :], sgu[:, FS * i + SC * c:FS * i + SC * c + SC],
                              h0T[:, 512 * blk:512 * blk + 512], start=True, stop=True)
                last.then_inc(s_sgp, 1)

            def shared_down(blk):
                pe.wait_ge(s_sact, 2 * blk + 2)
                if blk >= 1:
                    pe.wait_ge(s_sde, blk)
                for i in range(BLK):
                    for c in range(2):
                        last = mm(bank[5][:, P * i:P * i + P], sact[:, blk % 2, c, P * i:P * i + P],
                                  sd[:, c], start=(c == 0), stop=(c == 1))
                last.then_inc(s_sdp, 1)

            def slot_table():
                pe.wait_ge(s_onehot, 1)
                for i in range(2 * NT):
                    last = mm(bank[4][:, 384:384 + SLOT_TILES], ohlo[:, i, :], ohhi[:, i], start=(i == 0), stop=(i == 2 * NT - 1))
                last.then_inc(s_tab, 1)

            pe.wait_ge(s_sh, 48)
            pe.wait_ge(s_h0r, NB)
            for n in range(2 * NB):
                shared_gu(n)
                if n == 1:
                    prefixes()
                if n % 2 and n > 1:
                    shared_down(n // 2 - 1)
            slot_table()
            shared_down(NB - 1)

            def turn_x(j, r4, ring):
                pe.wait_ge(s_xg[r4], (j // 4 + 1) * 16 if isinstance(j, int) else 16 * 0 + turn_x.count)
                if ring:
                    pe.wait_ge(s_xe, j)
                pe.transpose(bank[6][:, 0:P], xg[:, r4], ident).then_inc(s_X, 1)

            def expert_of(j):
                return pe.value_load(eslot[0:1, j:j + 1] if isinstance(j, int) else eslot[0:1, bass.ds(j, 1)],
                                     min_val=0, max_val=E - 1)

            def gate_up(j, r, ring, e):
                pe.wait_ge(s_xe, j + 1)
                if ring:
                    pe.wait_ge(s_hm, j - 1)
                mm(bank[2 * r][:, 0:F0], xgT[:, r], wgu[:, bass.ds(e * (2 * F0), F0)], start=True, stop=True)
                mm(bank[2 * r + 1][:, 0:F0], xgT[:, r], wgu[:, bass.ds(e * (2 * F0) + F0, F0)],
                   start=True, stop=True).then_inc(s_G, 1)

            def turn_hid(j, r, ring):
                pe.wait_ge(s_hm, j + 1)
                if ring:
                    pe.wait_ge(s_he, j - 1)
                for c in range(3):
                    last = pe.transpose(bank[4 + r][:, P * c:P * c + P], hid[:, r, P * c:P * c + P], ident)
                last.then_inc(s_H, 1)

            def down(j, r, ring, e):
                pe.wait_ge(s_he, j + 1)
                if ring:
                    pe.wait_ge(s_ye, j)
                for c in range(3):
                    last = mm(bank[7][:, 0:P], hidT[:, r, P * c:P * c + P],
                              wd[:, bass.ds(e, 1), c, :].rearrange("p a d -> p (a d)"), start=(c == 0), stop=(c == 2))
                last.then_inc(s_D, 1)

            def fold(half):
                for e in range(4 * half, 4 * half + 4):
                    for c in range(C2):
                        last = mm(bank[2 + half][:, P * (e % 4):P * (e % 4) + P], w12in[:, 0, e, c],
                                  w12in[:, 1, e, c], start=(c == 0), stop=(c == C2 - 1))
                last.then_inc(s_w12p, 1)

            pe.wait_ge(s_ssl, 2 * NB)
            pe.wait_ge(s_ssu, 2 * NB)
            pe.wait_ge(s_fold, 64)
            fold(0)
            pe.wait_ge(s_exp0, 32)
            pe.wait_ge(s_slots, 1)
            turn_x(0, 0, False)
            for j in range(4):
                e = expert_of(j)
                d = expert_of(j - 3) if j >= 3 else None
                if j == 1:
                    pe.wait_ge(s_w12, 1)
                if j == 2:
                    pe.wait_ge(s_sde, NB)
                if j >= 2:
                    turn_hid(j - 2, j % 2, False)
                if j >= 3:
                    down(j - 3, (j - 3) % 2, False, d)
                gate_up(j, j % 2, j >= 2, e)
                turn_x(j + 1, (j + 1) % 4, True)
            with pe.Fori(1, SLOT_TILES // 4 - 1) as jj:
                for u in range(4):
                    j = jj * 4 + u
                    turn_x.count = (jj + (2 if u == 3 else 1)) * 16
                    e, d = expert_of(j), expert_of(jj * 4 + (u - 3))
                    turn_hid(jj * 4 + (u - 2), u % 2, True)
                    down(jj * 4 + (u - 3), (u + 1) % 2, True, d)
                    gate_up(j, u % 2, True, e)
                    turn_x(j + 1, (u + 1) % 4, True)
            for j in range(SLOT_TILES - 4, SLOT_TILES + 3):
                e = expert_of(j) if j < SLOT_TILES else None
                d = expert_of(j - 3)
                if j - 2 < SLOT_TILES:
                    turn_hid(j - 2, j % 2, True)
                down(j - 3, (j - 3) % 2, True, d)
                if j < SLOT_TILES:
                    gate_up(j, j % 2, True, e)
                if j + 1 < SLOT_TILES:
                    turn_x(j + 1, (j + 1) % 4, True)

            fold(1)
            for e in range(E):
                for c in range(C2):
                    last = mm(bank[5][:, e:e + 1], w12in[:, 1, e, c], b1[:, e, c:c + 1], start=(c == 0), stop=(c == C2 - 1))
            last.then_inc(s_cp, 1)

            def turn_x1(b, par):
                pe.wait_ge(s_x1, b + 1)
                for i in range(2):
                    last = pe.transpose(bank[6 + par][:, P * i:P * i + P], x1t[:, par, i], ident)
                last.then_inc(s_x1p, 1)

            def weights(k):
                return wk[k] if k < 2 else wsh

            def gemma_gu(b, par, hh, ring):
                k, q = hh // 2, hh % 2
                if q == 0 and k < 2:
                    pe.wait_ge(s_wk[k], (b + 1) * 16)
                if hh == 0:
                    pe.wait_ge(s_x1T, b + 1)
                if ring:
                    pe.wait_ge(s_m1, b * 6 + (hh - 1))
                w = weights(k)
                for i in range(2):
                    for c in range(2):
                        a = F1 * i + P * (2 * q + c)
                        last = mm(bank[2 * i + hh % 2][:, N * c:N * c + N], w[:, a:a + P], x1T[:, par],
                                  start=True, stop=True)
                last.then_inc(s_gu1, 1)

            def gemma_down(b, hh, first):
                k, q = hh // 2, hh % 2
                pe.wait_ge(s_m1, b * 6 + (hh + 1))
                if hh == 0 and not first:
                    pe.wait_ge(s_z, b)
                w = weights(k)
                for c in range(2):
                    a = 2 * F1 + P * (2 * q + c)
                    last = mm(bank[4][:, 0:N], w[:, a:a + P], hb[:, hh % 2, N * c:N * c + N],
                              start=(hh == 0 and c == 0), stop=(hh == 5 and c == 1), skip_group_check=True)
                last.then_inc(s_dn, 1)

            def pe_row(b, par, first=False, last=False):
                for hh in range(6):
                    gemma_gu(b, par, hh, not (first and hh < 2))
                    if hh > 0:
                        gemma_down(b, hh - 1, first)
                    elif not first:
                        gemma_down(b - 1, 5, False)
                    if hh == 4 and not last:
                        turn_x1(b + 1, 1 - par)

            pe.wait_ge(s_wsh, 16)
            turn_x1(0, 0)
            pe.wait_ge(s_c8, 1)
            mm(bank[5][:, 0:P], c_rep[:].rearrange("p g e -> p (g e)"), ident, start=True, stop=True).then_inc(s_c2p, 1)
            pe.wait_ge(s_w12, 2)
            pe_row(0, 0, first=True)
            pe_row(1, 1)
            with pe.Fori(1, B // 2 - 1) as bp:
                for u in range(2):
                    pe_row(bp * 2 + u, u)
            pe_row(B - 2, 0)
            pe_row(B - 1, 1, last=True)
            gemma_down(B - 1, 5, False)

            pe.wait_ge(s_attw, 80)
            pe.wait_ge(s_z, B)
            for blk in range(NB):
                if blk >= 2:
                    pe.wait_ge(s_qk, blk - 1)
                    pe.wait_ge(s_kk, 2 * (blk - 1))
                    pe.wait_ge(s_ka, 2 * (blk - 1))
                    pe.wait_ge(s_vv, blk - 1)
                for i in range(2):
                    last = mm(bank[2 * (blk % 2) + i][:], wqkv[:, D * i:D * i + D], zT[:, 512 * blk:512 * blk + 512],
                              start=True, stop=True)
                last.then_inc(s_qkp, 1)
                for j in range(BLK):
                    last = mm(bank[4 + blk % 2][:, P * j:P * j + P], group(zT, BLK * blk + j), wqkv[:, 2 * D:3 * D],
                              start=True, stop=True)
                last.then_inc(s_V, 1)
            pe.wait_ge(s_qk, NB)
            pe.wait_ge(s_kk, 2 * NB)
            pe.wait_ge(s_ka, 2 * NB)
            pe.wait_ge(s_vv, NB)
            for i in range(G + 7):
                g = i
                if g < G:
                    if g >= 2:
                        pe.wait_ge(s_pr, H * (g - 1))
                    mm(bank[g % 2][:], group(qT, g), kz[:, g].rearrange("p h k -> p (h k)"), start=True, stop=False)
                    mm(bank[g % 2][:], ident_b[:], mask_b[:].rearrange("p h k -> p (h k)"),
                       start=False, stop=True).then_inc(s_S, 1)
                g = i - 1
                if 0 <= g < G:
                    pe.wait_ge(s_pr, H * (g + 1))
                    if g >= 2:
                        pe.wait_ge(s_pe, g - 1)
                    for h in range(H):
                        last = pe.transpose(bank[2 + g % 2][:, P * h:P * h + P], pr[:, g % 2, h], ident)
                    last.then_inc(s_PT, 1)
                g = i - 2
                if 0 <= g < G:
                    pe.wait_ge(s_pe, g + 1)
                    if g >= 1:
                        pe.wait_ge(s_att, g)
                    for h in range(H):
                        last = mm(bank[4][:, HD * h:HD * h + HD], prT[:, g % 2, P * h:P * h + P], vv[:, g, HD * h:HD * h + HD],
                                  start=True, stop=True)
                    last.then_inc(s_O, 1)
                if i % BLK == 2 and i >= 6 and (i - 6) // BLK < NB:
                    q = (i - 6) // BLK
                    pe.wait_ge(s_att, BLK * (q + 1))
                    if q >= 1:
                        pe.wait_ge(s_ae, q)
                    for j in range(BLK):
                        last = pe.transpose(bank[5][:, P * j:P * j + P], att[:, q % 2, j], ident)
                    last.then_inc(s_AT, 1)
                if i % BLK == 3 and i >= 7:
                    q = (i - 7) // BLK
                    pe.wait_ge(s_ae, q + 1)
                    if q >= 1:
                        pe.wait_ge(s_res, q)
                    for j in range(BLK):
                        o = bank[6][:, P * j:P * j + P]
                        mm(o, group(zT, BLK * q + j), ident, start=True, stop=False)
                        last = mm(o, attT[:, q % 2, P * j:P * j + P], wo[:], start=False, stop=True)
                    last.then_inc(s_Y, 1)
                if i % BLK == 1 and i >= 9:
                    q = (i - 9) // BLK
                    pe.wait_ge(s_nr1, BLK * (q + 1))
                    if q >= 1:
                        pe.wait_ge(s_lgc, q)
                    for j in range(BLK):
                        last = pe.transpose(bank[7][:, P * j:P * j + P], nrm[:, q % 2, j], ident)
                    last.then_inc(s_YT, 1)
                if i % BLK == 2 and i >= 10:
                    q = (i - 10) // BLK
                    pe.wait_ge(s_yT, q + 1)
                    for g in range(BLK * q, BLK * q + BLK):
                        last = mm(bank[7][:, E * (g % BLK):E * (g % BLK) + E], y1T[:, g], wg[:], start=True, stop=True)
                    last.then_inc(s_l1, 1)

            def moe_product(g):
                for i in range(2):
                    last = mm(bank[2 * (g % 4) + i][:], y1T[:, g], W12[:, 512 * i:512 * i + 512], start=True, stop=True)
                last.then_inc(s_ym, 1)

            moe_product(0)
            moe_product(1)
            pe.wait_ge(s_oh1, 1)
            flat = lambda t: t[:].rearrange("p g e -> p (g e)")
            mm(bank[6][:, 0:P], rowm["row_before"][:], flat(tsum_b), start=True, stop=False)
            mm(bank[6][:, 0:P], rowm["row_same"][:], flat(exb), start=False, stop=False)
            mm(bank[6][:, 0:P], rowm["row_same_before"][:], flat(oh1b), start=False, stop=True).then_inc(s_loc, 1)
            pe.wait_ge(s_gk, 1)
            pe.transpose(bank[5][:, 0:P], flat(gk), ident).then_inc(s_gkp, 1)
            pe.wait_ge(s_gkT, 1)
            pe.wait_ge(s_cblk, 1)
            for blk in range(NB):
                mm(bank[4 + blk][:], gkT[:], cblk[:, BLK * blk:BLK * blk + BLK].rearrange("p g d -> p (g d)"),
                   start=True, stop=True).then_inc(s_bp, 1)
            pe.wait_ge(s_base, NB)
            for g in range(2, G):
                if g >= 4:
                    pe.wait_ge(s_acc, g - 3)
                    pe.wait_ge(s_part, E // 2 * (g - 3))
                moe_product(g)

        @block.vector
        def _(dve):
            v = nc.vector
            chain = [0]

            def link(ins):
                chain[0] += 1
                ins.then_inc(s_dve, 1)
                dve.wait_ge(s_dve, chain[0])

            def row(ap, n):
                return ap.unsqueeze(1).broadcast_to([P, n, ap.shape[-1]])

            def col(ap, n=E):
                return ap.unsqueeze(2).broadcast_to([P, ap.shape[-1], n])

            def first_max(vals, n, top, index, onehot, tmp):
                link(v.tensor_reduce(top, vals, AX.X, ALU.max))
                link(v.tensor_tensor(tmp, vals, col(top), ALU.is_lt))
                link(v.scalar_tensor_tensor(out=tmp, in0=tmp, scalar=float(E), in1=row(K("iota")[:, 0:E], n),
                                            op0=ALU.mult, op1=ALU.add))
                link(v.tensor_reduce(index, tmp, AX.X, ALU.min))
                link(v.tensor_tensor(onehot, row(K("iota")[:, 0:E], n), col(index), ALU.is_equal))

            def moments(src, q):
                for j in range(BLK):
                    ins = v.bn_stats(st1[:, q % 2, j], src[:, q % 2, j])
                link(ins)
                for j in range(BLK):
                    ins = v.bn_aggr(mv1[:, q % 2, j], st1[:, q % 2, j])
                link(ins)
                w, u = rs1[:, q % 2], var_e[:, q % 2]
                link(v.tensor_scalar(u, mv1[:, q % 2, :, 1], EPS, None, ALU.add))
                link(v.tensor_scalar(w.bitcast(I32), u.bitcast(I32), 1, None, ALU.logical_shift_right))
                return v.tensor_scalar(w.bitcast(I32), w.bitcast(I32), -1.0, float(0x5f3759df), ALU.mult, ALU.add)

            def last_scale_and_shift(q):
                w, z, h = rs1[:, q % 2], newton[:, q % 2], half_var[:, q % 2]
                link(v.tensor_scalar(h, var_e[:, q % 2], -0.5, None, ALU.mult))
                for _ in range(3):
                    link(v.tensor_tensor(z, w, w, ALU.mult))
                    link(v.tensor_tensor(z, z, h, ALU.mult))
                    link(v.scalar_tensor_tensor(out=w, in0=z, scalar=1.5, in1=w, op0=ALU.add, op1=ALU.mult))
                return v.scalar_tensor_tensor(out=shift1[:, q % 2], in0=mv1[:, q % 2, :, 0], scalar=-1.0, in1=w,
                                              op0=ALU.mult, op1=ALU.mult)

            dve.wait_ge(s_cond, 80)
            link(v.tensor_tensor(cw[:, 1], cw[:, 0], row(cmask[:], E), ALU.mult))
            for blk in range(NB):
                for e in range(E):
                    for b in (2 * blk, 2 * blk + 1):
                        y = y_bc[:, E * b + e:E * b + e + 1]
                        if e == 0:
                            ins = v.tensor_scalar(wbt[:, b], cw[:, 1, e], y, None, ALU.mult)
                        else:
                            dve.wait_ge(s_dve, chain[0] - 1)
                            ins = v.scalar_tensor_tensor(out=wbt[:, b], in0=cw[:, 1, e], scalar=y, in1=wbt[:, b],
                                                         op0=ALU.mult, op1=ALU.add)
                        chain[0] += 1
                        ins.then_inc(s_dve, 1)
                dve.wait_ge(s_dve, chain[0])
                dve.sem_inc(s_wb, 1)
            yv = y_bc[:].rearrange("p (b e) -> p b e", b=B)
            link(v.tensor_reduce(cs[:, 0], yv, AX.X, ALU.max))
            v.tensor_tensor(cd[:], yv, col(cs[:, 0]), ALU.subtract).then_inc(s_cd, 1)
            for blk in range(NB):
                dve.wait_ge(s_r0p, blk + 1)
                v.tensor_tensor(h0r[:, BLK * blk:BLK * blk + BLK], bank[2 + blk % 2][:].rearrange("p (t d) -> p t d", t=BLK),
                                row(cbias_bc, BLK), ALU.add).then_inc(s_h0r, 1)
            dve.wait_ge(s_lgp, NB)
            dve.wait_ge(s_const, 16)
            link(v.tensor_copy(lg[:], bank[4][:, 0:NT * E].rearrange("p (t e) -> p t e", t=NT)))
            first_max(lg[:], NT, mtop[0][:], itop[0][:], oh[0][:], t8[:])
            link(v.scalar_tensor_tensor(out=lgb[:], in0=oh[0][:], scalar=-BIG, in1=lg[:], op0=ALU.mult, op1=ALU.add))
            first_max(lgb[:], NT, mtop[1][:], itop[1][:], oh[1][:], t8[:])
            v.tensor_tensor(taken[:], oh[0][:], oh[1][:], ALU.add).then_inc(s_taken, 1)
            v.tensor_tensor(dlt[:], mtop[1][:], mtop[0][:], ALU.subtract).then_inc(s_dlt, 1)
            dve.wait_ge(s_pre, 1)
            link(v.tensor_copy(tot[:].rearrange("p e t -> p t e"), bank[4][:, 256:384].rearrange("p (t e) -> p t e", t=NT)))
            link(v.tensor_tensor_scan(incl[:].rearrange("p e t -> p (e t)"), K("restart"),
                                      tot[:].rearrange("p e t -> p (e t)"), 0.0, ALU.mult, ALU.add))
            link(v.tensor_scalar(cnt[:, 0], incl[:, :, NT - 1], float(P - 1), None, ALU.add))
            link(v.tensor_copy(cnt_i[:], cnt[:, 0]))
            link(v.tensor_scalar(cnt_i[:], cnt_i[:], -P, None, ALU.bitwise_and))
            link(v.tensor_copy(cnt[:, 2], cnt_i[:]))
            link(v.tensor_tensor_scan(cnt[:, 3], K("ones")[:, 0:E], cnt[:, 2], 0.0, ALU.mult, ALU.add))
            link(v.tensor_tensor(cnt[:, 4], cnt[:, 3], cnt[:, 2], ALU.subtract))
            link(v.tensor_tensor(excl[:], incl[:], tot[:], ALU.subtract))
            link(v.tensor_tensor(Q[:], bank[4][:, 128:256].rearrange("p (t e) -> p t e", t=NT),
                                 excl[:].rearrange("p e t -> p t e"), ALU.add))
            link(v.tensor_tensor(Q[:], Q[:], row(cnt[:, 4], NT), ALU.add))
            for k in range(2):
                link(v.tensor_tensor(t8[:], oh[k][:], Q[:], ALU.mult))
                link(v.tensor_reduce(pos[:, k], t8[:], AX.X, ALU.add))
            link(v.tensor_copy(pos_u[:], pos[:]))
            flat_pos = pos_u[:].rearrange("p k t -> p (k t)")
            v.tensor_scalar(lo_i[:], flat_pos, P - 1, None, ALU.bitwise_and)
            link(v.tensor_scalar(hi_i[:], flat_pos, P.bit_length() - 1, None, ALU.logical_shift_right))
            v.tensor_copy(lo[:], lo_i[:])
            link(v.tensor_copy(hi[:], hi_i[:]))
            v.tensor_tensor(ohlo, row(K("iota"), 2 * NT), col(lo[:], P), ALU.is_equal)
            link(v.tensor_tensor(ohhi[:], row(K("iota")[:, 0:SLOT_TILES], 2 * NT), col(hi[:], SLOT_TILES), ALU.is_equal))
            link(v.tensor_tensor(ohhi[:].rearrange("p (k t) s -> p k t s", k=2), ohhi[:].rearrange("p (k t) s -> p k t s", k=2),
                                 K("token").unsqueeze(1).unsqueeze(3).broadcast_to([P, 2, NT, SLOT_TILES]), ALU.mult))
            dve.sem_inc(s_onehot, 1)
            dve.sem_inc(s_pos, 1)
            link(v.tensor_tensor(cmp[:], row(cnt[:, 3], SLOT_TILES), col(K("tile_start")), ALU.is_le))
            link(v.tensor_reduce(ecnt[:], cmp[:], AX.X, ALU.add))
            link(v.tensor_scalar(ecnt[:], ecnt[:], float(E - 1), None, ALU.min))
            link(v.tensor_copy(eslot[:], ecnt[:]))
            dve.wait_ge(s_tab, 1)
            v.tensor_copy(slot_tok[:], bank[4][:, 384:384 + SLOT_TILES]).then_inc(s_slots, 1)

            def token_weights():
                dve.wait_ge(s_edl, 1)
                link(v.tensor_scalar(sdl[:], edl[:], 1.0, None, ALU.add))
                link(v.reciprocal(pk[:, 0], sdl[:]))
                link(v.tensor_tensor(pk[:, 1], edl[:], pk[:, 0], ALU.mult))

            def row_softmax():
                dve.wait_ge(s_ce, 1)
                link(v.tensor_reduce(cs[:, 1], ce[:], AX.X, ALU.add))
                link(v.reciprocal(cs[:, 2], cs[:, 1]))
                link(v.tensor_tensor(rw[:], ce[:], col(cs[:, 2]), ALU.mult))

            def row_first_expert():
                first_max(rw[:], B, cs[:, 3], cs[:, 4], coh[:], c8[:])
                link(v.tensor_copy(cix[:, 0], cs[:, 4]))
                link(v.scalar_tensor_tensor(out=rwb[:], in0=coh[:], scalar=-BIG, in1=rw[:], op0=ALU.mult, op1=ALU.add))

            def row_second_expert():
                first_max(rwb[:], B, cs[:, 5], cs[:, 4], coh[:], c8[:])
                link(v.tensor_copy(cix[:, 1], cs[:, 4]))
                dve.sem_inc(s_cr, 1)

            def row_weights():
                link(v.tensor_tensor(cs[:, 6], cs[:, 3], cs[:, 5], ALU.add))
                link(v.reciprocal(cs[:, 7], cs[:, 6]))
                for k, m in enumerate((3, 5)):
                    link(v.tensor_tensor(cs[:, m], cs[:, m], cs[:, 7], ALU.mult))
                    link(v.tensor_scalar(cs[:, 6], cs[:, m], SKILL_SCALE, None, ALU.mult))
                    link(v.scalar_tensor_tensor(out=cwt[:, k], in0=cs[:, m], scalar=1.0 - SKILL_SCALE, in1=cs[:, 6],
                                                op0=ALU.mult, op1=ALU.add))

            def xgT_copy(j, r, ring):
                dve.wait_ge(s_X, j + 1)
                if ring:
                    dve.wait_ge(s_G, j - 1)
                v.tensor_copy(xgT[:, r], bank[6][:, 0:P]).then_inc(s_xe, 1)

            def hidden(j, r, ring):
                dve.wait_ge(s_sl, j + 1)
                if ring:
                    dve.wait_ge(s_H, j - 1)
                v.tensor_tensor(hid[:, r, 0:F0], slu[:, r], bank[2 * r + 1][:, 0:F0], ALU.mult).then_inc(s_hm, 1)

            def y_copy(j, r4, stored):
                dve.wait_ge(s_D, j + 1)
                if stored is not None:
                    dve.wait_ge(s_yst[r4], stored)
                v.tensor_copy(ysb[:, r4], bank[7][:, 0:P]).then_inc(s_ye, 1)

            row_softmax()
            dve.wait_ge(s_hpad, 1)
            xgT_copy(0, 0, False)
            for j in range(4):
                xgT_copy(j + 1, (j + 1) % 2, j >= 1)
                hidden(j, j % 2, j >= 2)
                if j >= 2:
                    y_copy(j - 2, j - 2, None)
                (row_first_expert, row_second_expert, row_weights, token_weights)[j]()
            for j in range(4, 6):
                xgT_copy(j + 1, (j + 1) % 2, True)
                hidden(j, j % 2, True)
                y_copy(j - 2, j - 2, None)
            with dve.Fori(1, (SLOT_TILES - 4) // 4) as jj:
                for u in range(4):
                    j = jj * 4 + (u + 2)
                    xgT_copy(j + 1, (u + 1) % 2, True)
                    hidden(j, u % 2, True)
                    y_copy(j - 2, u, jj * 16)
            for j in range(SLOT_TILES - 2, SLOT_TILES + 2):
                if j + 1 < SLOT_TILES:
                    xgT_copy(j + 1, (j + 1) % 2, True)
                if j < SLOT_TILES:
                    hidden(j, j % 2, True)
                y_copy(j - 2, (j - 2) % 4, 16 * ((j - 2) // 4))

            def x1_row(b, par, stored):
                dve.wait_ge(s_yg[par], stored["gathered"])
                for i in range(2):
                    t = b * 2 + i
                    v.scalar_tensor_tensor(out=half1[:, i], in0=yg[:, par, i, 0], scalar=stored["p"](0, t),
                                           in1=stored["xs"](t), op0=ALU.mult, op1=ALU.add).then_inc(s_half, 1)
                if stored["old"] is not None:
                    dve.wait_ge(s_x1p, stored["old"])
                    dve.wait_ge(s_x1st, stored["old"] * 16)
                for i in range(2):
                    t = b * 2 + i
                    dve.wait_ge(s_half, b * 2 + i + 1)
                    ins = v.scalar_tensor_tensor(out=x1t[:, par, i], in0=yg[:, par, i, 1], scalar=stored["p"](1, t),
                                                 in1=half1[:, i], op0=ALU.mult, op1=ALU.add)
                    ins.then_inc(s_x1h, 1)
                dve.wait_ge(s_x1h, b * 2 + 2)
                dve.sem_inc(s_x1, 1)

            def row_args(b, gathered, old):
                if isinstance(b, int):
                    return dict(gathered=gathered, old=old, p=lambda k, t: pk[:, k, t:t + 1], xs=lambda t: xs[:, t])
                return dict(gathered=gathered, old=old, p=lambda k, t: pk[:, k, bass.ds(t, 1)],
                            xs=lambda t: xs[:, bass.ds(t, 1), :].rearrange("p a d -> p (a d)"))

            def gemma_hid(b, hh, ring):
                k = hh // 2
                dve.wait_ge(s_gl, b * 6 + (hh + 1))
                if ring:
                    dve.wait_ge(s_dn, b * 6 + (hh - 1))
                if k < 2:
                    w = cwt[:, k, b:b + 1] if isinstance(b, int) else cwt[:, k, bass.ds(b, 1)]
                    ins = v.scalar_tensor_tensor(out=hb[:, hh % 2], in0=gl[:, hh % 2], scalar=w,
                                                 in1=bank[2 + hh % 2][:], op0=ALU.mult, op1=ALU.mult)
                else:
                    ins = v.tensor_tensor(hb[:, hh % 2], gl[:, hh % 2], bank[2 + hh % 2][:], ALU.mult)
                ins.then_inc(s_m1, 1)

            def dve_row(b, par, gathered, old, first=False, last=False):
                for hh in range(6):
                    gemma_hid(b, hh, not (first and hh < 2))
                    if hh == 2 and not last:
                        x1_row(b + 1, 1 - par, row_args(b, gathered, old))

            dve.wait_ge(s_xs, NB)
            x1_row(0, 0, row_args(0, 64, None))
            dve.wait_ge(s_cp, 1)
            v.tensor_tensor(c_rep[:], bank[5][:, 0:E].unsqueeze(1).broadcast_to([P, G, E]),
                            b2T[:].unsqueeze(1).broadcast_to([P, G, E]), ALU.add).then_inc(s_c8, 1)
            dve_row(0, 0, 64, None, first=True)
            dve_row(1, 1, 128, 1)
            with dve.Fori(1, B // 2 - 1) as bp:
                dve_row(bp * 2, 0, bp * 64 + 64, bp * 2)
                dve_row(bp * 2 + 1, 1, bp * 64 + 128, bp * 2 + 1)
            dve_row(B - 2, 0, 64 * (B // 2), B - 2)
            dve_row(B - 1, 1, None, None, last=True)

            dve.wait_ge(s_attw, 80)
            v.tensor_scalar(bq_s[:], bqkv[:, 0:1], HD ** -0.5, None, ALU.mult).then_inc(s_bq, 1)
            for blk in range(NB):
                dve.wait_ge(s_qkp, blk + 1)
                dve.wait_ge(s_kz0, G)
                for h in range(2, 4):
                    a = HD * h
                    v.tensor_scalar(
                        kz[a:a + HD, BLK * blk:BLK * blk + BLK, h, :],
                        bank[2 * (blk % 2) + 1][a:a + HD, :].rearrange("p (g k) -> p g k", g=BLK),
                        bqkv[a:a + HD, 1:2], None, ALU.add).then_inc(s_kk, 1)
                dve.wait_ge(s_V, blk + 1)
                v.tensor_tensor(vv[:, BLK * blk:BLK * blk + BLK], bank[4 + blk % 2][:].rearrange("p (t d) -> p t d", t=BLK),
                                row(bv_bc, BLK), ALU.add).then_inc(s_vv, 1)
            for i in range(G + 7):
                g = i
                if g < G:
                    dve.wait_ge(s_S, g + 1)
                    if g >= 2:
                        dve.wait_ge(s_pr, H * (g - 1))
                    v.tensor_reduce(nmax[:, g % 2], bank[g % 2][:].rearrange("p (h k) -> p h k", h=H), AX.X, ALU.max,
                                    negate=True).then_inc(s_nm, 1)
                g = i - 1
                if 0 <= g < G:
                    dve.wait_ge(s_pr, H * (g + 1))
                    if g >= 2:
                        dve.wait_ge(s_att, g - 1)
                    v.reciprocal(rden[:, g % 2], den[:, g % 2]).then_inc(s_rd, 1)
                    dve.wait_ge(s_PT, g + 1)
                    if g >= 2:
                        dve.wait_ge(s_O, g - 1)
                    v.tensor_copy(prT[:, g % 2], bank[2 + g % 2][:]).then_inc(s_pe, 1)
                g = i - 2
                if 0 <= g < G:
                    dve.wait_ge(s_O, g + 1)
                    dve.wait_ge(s_rd, g + 1)
                    if g >= 2 * BLK:
                        dve.wait_ge(s_AT, g // BLK - 1)
                    v.tensor_tensor(att[:, (g // BLK) % 2, g % BLK].rearrange("p (h d) -> p h d", h=H),
                                    bank[4][:, 0:P].rearrange("p (h d) -> p h d", h=H),
                                    col(rden[:, g % 2], HD), ALU.mult).then_inc(s_att, 1)
                if i % BLK == 3 and i >= 7:
                    q = (i - 7) // BLK
                    dve.wait_ge(s_Y, q + 1)
                    if q >= 2:
                        dve.wait_ge(s_y1, q - 1)
                    link(v.tensor_tensor(res[:, q % 2], bank[6][:].rearrange("p (g d) -> p g d", g=BLK),
                                         row(bo_bc, BLK), ALU.add))
                    dve.sem_inc(s_res, 1)
                    if q < NB - 1:
                        moments(res, q).then_inc(s_seed, 1)
                    else:
                        link(moments(res, q))
                        last_scale_and_shift(q).then_inc(s_rs1v, 1)
                if i % BLK == 2 and i >= 10:
                    q = (i - 10) // BLK
                    dve.wait_ge(s_l1, q + 1)
                    v.tensor_copy(lg1[:, BLK * q:BLK * q + BLK], bank[7][:, 0:BLK * E].rearrange(
                        "p (g e) -> p g e", g=BLK)).then_inc(s_lgc, 1)

            dve.wait_ge(s_lgc, NB)
            link(v.tensor_reduce(sm1[:, 0], lg1[:], AX.X, ALU.max))
            v.tensor_tensor(t8[:], lg1[:], col(sm1[:, 0]), ALU.subtract).then_inc(s_gap1, 1)
            dve.wait_ge(s_e1, 1)
            first_max(e1[:], G, sm1[:, 1], sm1[:, 2], oh1[:], Q[:])
            link(v.tensor_copy(oh1b[:], oh1[:]))
            by_e = oh1[:].rearrange("p g e -> p e g")
            link(v.tensor_copy(tot[:], by_e))
            link(v.tensor_tensor_scan(incl[:].rearrange("p e t -> p (e t)"), K("restart"),
                                      tot[:].rearrange("p e t -> p (e t)"), 0.0, ALU.mult, ALU.add))
            link(v.tensor_tensor(exb[:].rearrange("p g e -> p e g"), incl[:], tot[:], ALU.subtract))
            link(v.tensor_copy(tsum_b[:], row(incl[:, :, G - 1], G)))
            dve.sem_inc(s_oh1, 1)
            link(v.tensor_reduce(sm1[:, 3], e1[:], AX.X, ALU.add))
            link(v.reciprocal(sm1[:, 4], sm1[:, 3]))
            link(v.tensor_tensor(sm1[:, 4], sm1[:, 4], sm1[:, 1], ALU.mult))
            dve.wait_ge(s_loc, 1)
            link(v.tensor_tensor(t8[:], bank[6][:, 0:P].rearrange("p (g e) -> p g e", g=G), oh1[:], ALU.mult))
            link(v.tensor_reduce(sm1[:, 5], t8[:], AX.X, ALU.add))
            link(v.tensor_scalar(sm1[:, 5], sm1[:, 5], float(CAP), None, ALU.is_lt))
            link(v.tensor_tensor(sm1[:, 4], sm1[:, 4], sm1[:, 5], ALU.mult))
            v.tensor_tensor(gk[:], oh1[:], col(sm1[:, 4]), ALU.mult).then_inc(s_gk, 1)
            dve.wait_ge(s_y1, NB)
            for blk in range(NB):
                dve.wait_ge(s_bp, blk + 1)
                v.tensor_tensor(base[:, BLK * blk:BLK * blk + BLK], bank[4 + blk][:].rearrange("p (g d) -> p g d", g=BLK),
                                y1[:, BLK * blk:BLK * blk + BLK], ALU.add).then_inc(s_base, 1)
            dve.wait_ge(s_gk, 1)
            dve.wait_ge(s_base, NB)
            for p in range(G // 2):
                q = p // 2
                dve.wait_ge(s_ym, 2 * p + 2)
                if q >= 2 and p % 2 == 0:
                    dve.wait_ge(s_nr2, BLK * (q - 1))
                for e in range(E // 2):
                    for g in (2 * p, 2 * p + 1):
                        if e > 0:
                            dve.wait_ge(s_dve, chain[0] - 1)
                        acc = macc[:, q % 2, g % BLK]
                        ins = v.scalar_tensor_tensor(
                            out=acc, in0=bank[2 * (g % 4)][:, D * e:D * e + D], scalar=gk[:, g, e:e + 1],
                            in1=base[:, g] if e == 0 else acc, op0=ALU.mult, op1=ALU.add)
                        chain[0] += 1
                        ins.then_inc(s_dve, 1)
                dve.wait_ge(s_psum, 2 * p + 2)
                for g in (2 * p, 2 * p + 1):
                    dve.wait_ge(s_dve, chain[0] - 1 + g % 2)
                    acc = macc[:, q % 2, g % BLK]
                    v.tensor_tensor(acc, acc, part[:, g % 4, 0], ALU.add).then_inc(s_acc, 1)
                if p % 2:
                    dve.wait_ge(s_acc, 2 * p + 2)
                    if q < NB - 1:
                        moments(macc, q).then_inc(s_seed2, 1)
            link(moments(macc, NB - 1))
            last_scale_and_shift(NB - 1).then_inc(s_rs2v, 1)
            q = NB - 1
            dve.wait_ge(s_nr2, BLK * NB)
            link(v.tensor_tensor(nrg2[:, q % 2], nrm2[:, q % 2], row(g2_bc, BLK), ALU.mult))
            dve.wait_ge(s_fst[q % 2], 16 * BLK * (q // 2))
            dve.wait_ge(s_xb, 1)
            v.tensor_tensor(fin[:, q % 2], nrg2[:, q % 2], x1g[:, BLK * q:BLK * q + BLK], ALU.add).then_inc(s_fov, 1)


def kernel(**a):
    import concourse.bacc as bacc
    from concourse.bass_utils import run_bass_kernel_spmd

    a = {k: np.asarray(v) for k, v in a.items()}
    x = a["x"].reshape(T, D)

    def chunked(w, p=P):
        w = w.reshape(*w.shape[:-2], w.shape[-2] // p, p, w.shape[-1])
        return np.moveaxis(w, -2, 0)

    wd = np.zeros((P, E, 3, D), np.float32)
    wd[:, :, 0:2] = chunked(a["L0_ffn_Wd"][:, 0:2 * P])
    wd[0:F0 - 2 * P, :, 2] = np.moveaxis(a["L0_ffn_Wd"][:, 2 * P:], 1, 0)

    def gemma(gate, up, down):
        d = np.moveaxis(down.reshape(-1, C1, P, D), 2, 1).reshape(-1, P, C1 * D)
        return np.concatenate([gate.reshape(-1, D, F1), up.reshape(-1, D, F1), d], axis=2)

    c = {k[3:]: v for k, v in a.items() if k.startswith("L1_")}
    ins = {
        "xT": x.T,
        "x_rows": x,
        "cond": a["cond_8"],
        "cw": a["L0_cond_weight"].transpose(2, 0, 1),
        "cmask": a["L0_cond_mask"].T,
        "cbias": a["L0_cond_bias"].reshape(D, 1),
        "vecs": np.stack([a["L0_cond_bias"], c["ffn_in_proj_b"][2 * D:], c["ffn_out_proj_b"], c["ffn_ln1_g"],
                          c["ffn_ln1_b"], c["ffn_ln2_g"], c["ffn_ln2_b"]]),
        "consts": shape_constants(),
        "gate_w": a["L0_ffn_gate_w"],
        "wgu": np.moveaxis(np.concatenate([a["L0_ffn_Wg"], a["L0_ffn_Wu"]], axis=2), 1, 0).reshape(D, E * 2 * F0),
        "wd": wd,
        "sgu": np.concatenate([a["L0_ffn_Sg"], a["L0_ffn_Su"]], axis=1),
        "sd": chunked(a["L0_ffn_Sd"], SC),
        "wexp": gemma(c["cond_skill_gate"], c["cond_skill_up"], c["cond_skill_down"]),
        "wsh": gemma(c["cond_shared_gate"], c["cond_shared_up"], c["cond_shared_down"])[0],
        "w1": chunked(c["ffn_w1"].transpose(0, 2, 1)),
        "w2": chunked(c["ffn_w2"]),
        "b1": c["ffn_b1"].reshape(E, C2, P).transpose(2, 0, 1),
        "b2": c["ffn_b2"].T,
        "wqkv": c["ffn_in_proj_w"].T,
        "wo": c["ffn_out_proj_w"].T,
        "bqkv": c["ffn_in_proj_b"].reshape(3, D).T,
        "wg": c["ffn_wg"],
        "cols1": np.stack([c["ffn_ln1_g"], c["ffn_ln1_b"]], axis=1),
    }
    nc = bacc.Bacc("TRN2", target_bir_lowering=False, num_devices=1)
    arrays, args = {}, []
    for name, v in ins.items():
        v = np.ascontiguousarray(v)
        arrays[f"in_{name}"] = v
        args.append(nc.dram_tensor(f"in_{name}", v.shape, mybir.dt.from_np(v.dtype), kind="ExternalInput").ap())
    args.append(nc.dram_tensor("out", [B, N, D], F32, kind="ExternalOutput").ap())
    block_kernel(nc, *args)
    r = run_bass_kernel_spmd(nc, [arrays], core_ids=[0])
    return r.results[0]["out"]
```

```python
from contextlib import ExitStack

import concourse.bass as bass
from concourse import mybir
import numpy as np

ALU = mybir.AluOpType
ACT = mybir.ActivationFunctionType
AX = mybir.AxisListType
F32 = mybir.dt.float32
F32R = mybir.dt.float32r
F16 = mybir.dt.float16
BF16 = mybir.dt.bfloat16
I32 = mybir.dt.int32
U32 = mybir.dt.uint32

P = 128
B, N, D = 8, 256, 128
T = B * N
NT = T // P
E = 8
F0 = 352
FS = 176
SC = FS // 2
F1 = 512
C1 = F1 // P
C2 = 512 // P
H, HD = 4, 32
G, GN = 16, 16
CAP = T // E
SLOT_TILES = 2 * T // P + E - 1
ROUNDS = -(-SLOT_TILES // 4)
BIG = 3.0e38
EPS = 1e-5
SKILL_SCALE = 1.0 / 12.0
BLK = 4
NB = NT // BLK

CONST = {}
_at = 0
for _name, _width in (("ident", P), ("iota", P), ("before", P), ("row_before", P), ("row_same", P),
                      ("row_same_before", P), ("mask", P), ("token", NT), ("tile_start", SLOT_TILES),
                      ("restart", E * G), ("ones", P), ("eye8", E * E), ("own_group", G), ("repeat8", P)):
    CONST[_name] = (_at, _at + _width)
    _at += _width
CONST_W = _at


def shape_constants():
    k = np.arange(P)[:, None]
    m = np.arange(P)[None, :]
    c = np.zeros((P, CONST_W), np.float32)

    def put(name, a):
        c[:, CONST[name][0]:CONST[name][1]] = a

    put("ident", k == m)
    put("iota", m + 0 * k)
    put("before", k < m)
    put("row_before", k // GN < m // GN)
    put("row_same", k // GN == m // GN)
    put("row_same_before", (k // GN == m // GN) & (k < m))
    put("mask", np.where((k - m) % GN == 0, 0.0, -1.0e30))
    put("token", k + P * np.arange(NT)[None, :])
    put("tile_start", P * np.arange(SLOT_TILES)[None, :] + 0 * k)
    put("restart", (np.arange(E * G)[None, :] % G != 0) + 0 * k)
    put("ones", 1.0)
    put("eye8", np.eye(E).reshape(1, -1) + 0 * k)
    put("own_group", k // E == np.arange(G)[None, :])
    put("repeat8", (k < E) & (m % E == k))
    return c


def block_kernel(nc, xT_d, x_d, cond_d, cw_d, cmask_d, cbias_d, vecs_d, const_d, gate_d, wgu_d, wd_d,
                 sgu_d, sd_d, wexp_d, wsh_d, w1_d, w2_d, b1_d, b2_d, wqkv_d, wo_d, bqkv_d, wg_d, cols1_d, out_d):
    with ExitStack() as ctx:
        def sb(name, shape, dt=F32):
            return ctx.enter_context(nc.sbuf_tensor(name, shape, dt))

        def sem(name):
            return ctx.enter_context(nc.semaphore(name))

        bank = [ctx.enter_context(nc.psum_tensor(f"bank{i}", [P, 512], F32)) for i in range(8)]

        row_bank = [bank[i] for i in (2, 3, 6, 7)]

        h0_rows = nc.dram_tensor("h0_rows", [T, D], F32, kind="Internal").ap()
        y_rows = nc.dram_tensor("y_rows", [SLOT_TILES * P, D], F32, kind="Internal").ap()
        x1_rows = nc.dram_tensor("x1_rows", [T, D], F32, kind="Internal").ap()

        xT = sb("xT", [P, T])
        y_bc = sb("y_bc", [P, B * E])
        cw = sb("cw", [P, 2, E, P])
        cmask = sb("cmask", [P, P])
        cbias = sb("cbias", [P, 1])
        vecs = sb("vecs", [P, 5, P])
        cbias_bc, bv_bc, bo_bc, g2_bc, n2_bc = (vecs[:, i, :] for i in range(5))
        const = sb("const", [P, CONST_W])
        gate_w = sb("gate_w", [P, E])
        sgu = sb("sgu", [P, 2 * FS])
        sd = sb("sd", [SC, 2, D])
        wk = [sb(f"wk{k}", [P, 3 * F1]) for k in range(2)]
        wsh = sb("wsh", [P, 3 * F1])
        w12in = sb("w12in", [P, 2, E, C2, P])
        b1 = sb("b1", [P, E, C2])
        b2 = sb("b2", [E, D])
        wqkv = sb("wqkv", [P, 3 * D])
        wo = sb("wo", [P, D])
        bqkv = sb("bqkv", [P, 3])
        wg = sb("wg", [P, E])

        def K(name):
            return const[:, CONST[name][0]:CONST[name][1]]

        wbt = sb("wbt", [P, B, P])
        h0T = sb("h0T", [P, T])
        h0r = sb("h0r", [P, NT, D])
        xs = sb("xs", [P, NT, D])
        lg = sb("lg", [P, NT, E])
        lgb = sb("lgb", [P, NT, E])
        oh = [sb(f"oh{k}", [P, NT, E]) for k in range(2)]
        mtop = [sb(f"mtop{k}", [P, NT]) for k in range(2)]
        itop = [sb(f"itop{k}", [P, NT]) for k in range(2)]
        t8 = sb("t8", [P, NT, E])
        taken = sb("taken", [P, NT, E], BF16)
        before_b = sb("before_b", [P, P], BF16)
        ones_b = sb("ones_b", [P, P], BF16)
        dlt = sb("dlt", [P, NT])
        edl = sb("edl", [P, NT])
        sdl = sb("sdl", [P, NT])
        pk = sb("pk", [P, 2, NT])
        tot = sb("tot", [P, E, NT])
        incl = sb("incl", [P, E, NT])
        excl = sb("excl", [P, E, NT])
        cnt = sb("cnt", [P, 6, E])
        Q = sb("Q", [P, NT, E])
        pos = sb("pos", [P, 2, NT])
        lo = sb("lo", [P, 2 * NT])
        hi = sb("hi", [P, 2 * NT])
        lo_i = sb("lo_i", [P, 2 * NT], U32)
        hi_i = sb("hi_i", [P, 2 * NT], U32)
        cnt_i = sb("cnt_i", [P, E], I32)
        pos_u = sb("pos_u", [P, 2, NT], U32)
        prod = sb("prod", [P, 2, E, D])
        ohlo = prod[:].rearrange("p a e d -> p (a e d)").bitcast(F16).rearrange("p (i s) -> p i s", s=P)
        slot_tok = sb("slot_tok", [P, SLOT_TILES], U32)
        cmp = sb("cmp", [P, SLOT_TILES, E])
        ecnt = sb("ecnt", [P, SLOT_TILES])
        eslot = sb("eslot", [P, SLOT_TILES], I32)
        words = sb("words", [P, ROUNDS - 1])
        words_i = sb("words_i", [P, ROUNDS - 1], I32)
        sul = cw[0:SC, 0].rearrange("p e d -> p (e d)").rearrange("p (a n) -> p a n", a=2)
        sdn = h0r[:, 0:2 * BLK]
        acts = sb("acts", [P, 4, 512])
        sact = acts[0:SC].rearrange("p (a c) n -> p a c n", a=2)
        xgT = sb("xgT", [P, 2, P])
        hidT = prod[:].rearrange("p a e d -> p (a e d)")[:, 0:6 * P].rearrange("p (a n) -> p a n", a=2)
        slu = prod[:].rearrange("p a e d -> p (a e d)")[:, 6 * P:6 * P + 2 * F0].rearrange("p (a n) -> p a n", a=2)
        yg = sb("yg", [P, 2, 2, 2, D])
        cd = sb("cd", [P, B, E])
        ce = sb("ce", [P, B, E])
        rw = sb("rw", [P, B, E])
        rwb = sb("rwb", [P, B, E])
        c8 = sb("c8", [P, B, E])
        coh = sb("coh", [P, B, E])
        cs = sb("cs", [P, 8, B])
        cwt = sb("cwt", [P, 2, B])
        cix = sb("cix", [P, 2, B], I32)
        cols1 = sb("cols1", [P, 2])
        half1 = sb("half1", [P, 2, D])
        x1t = sb("x1t", [P, 2, 2, D])
        gl = acts[:, 0:2]
        hb = acts[:, 2:4]
        zT = xT
        W12 = wbt[:].rearrange("p b d -> p (b d)")
        b1w2 = acts[:, 0:2].rearrange("p a (e d) -> p (a e) d", e=E // 2)
        c_e = sb("c_e", [E, D])
        c_ge = sb("c_ge", [P, D])
        qT = h0T
        bq_s = sb("bq_s", [P, 1])
        kz = w12in[:, :, :, :, :].rearrange("p a e c d -> p (a e c d)").rearrange(
            "p (g h k) -> p g h k", g=G, h=H)
        mask_b = sb("mask_b", [P, H, P], BF16)
        ident_b = sb("ident_b", [P, P], BF16)
        nmax = sb("nmax", [P, 2, H])
        pr = gl.rearrange("p a (h k) -> p a h k", h=H)
        den = sb("den", [P, 2, H])
        rden = sb("rden", [P, 2, H])
        prT = hb
        vv = xs

        def batches(buffer):
            return buffer.rearrange("p (a j d) -> p a j d", a=2, j=BLK)

        att = batches(wk[0][:, 0:1024])
        attT = wk[1][:, 0:1024].rearrange("p (a n) -> p a n", a=2)
        res = batches(wsh[:, 0:1024])
        prod_flat = prod[:].rearrange("p a e d -> p (a e d)")
        nrm = batches(prod_flat[:, 0:1024])
        part = prod_flat.rearrange("p (a e d) -> p a e d", a=4, e=E // 2)
        st1 = sb("st1", [P, 2, BLK, 6])
        mv1 = sb("mv1", [P, 2, BLK, 2])
        var_e = sb("var_e", [P, 2, BLK])
        rs1 = sb("rs1", [P, 2, BLK])
        newton = sb("newton", [P, 2, BLK])
        half_var = sb("half_var", [P, 2, BLK])
        warm = sb("warm", [P, 1])
        shift1 = sb("shift1", [P, 2, BLK])
        y1T = cw[:, :, :, :].rearrange("p a e d -> p (a e) d")
        lg1 = lg
        e1 = lgb
        oh1 = oh[0]
        oh1b = sb("oh1b", [P, G, E], BF16)
        rowm = {n: sb(n + "_b", [P, P], BF16) for n in ("row_before", "row_same", "row_same_before")}
        tsum = sb("tsum", [P, E])
        tsum_b = sb("tsum_b", [P, G, E], BF16)
        exb = sb("exb", [P, G, E], BF16)
        gk = sb("gk", [P, G, E])
        sm1 = sb("sm1", [P, 6, G])
        gkT = sb("gkT", [P, P])
        base = xs
        macc = batches(acts[:, 0:2].rearrange("p a n -> p (a n)"))
        fin = batches(acts[:, 2:4].rearrange("p a n -> p (a n)"))
        nrm2 = att
        nrg2 = batches(wk[1][:, 0:1024])

        with ExitStack() as tiles_ctx:
            wgu, wd, sgl, ohhi, xg, hid, ysb = (
                tiles_ctx.enter_context(nc.sbuf_tensor(name, shape, dt)) for name, shape, dt in (
                    ("wgu", [P, E * 2 * F0], F32), ("wd", [P, E, 3, D], F32), ("sgl", [SC, 2, 512], F32),
                    ("ohhi", [P, 2 * NT, SLOT_TILES], F16), ("xg", [P, 4, D], F32), ("hid", [P, 2, 3 * P], F32),
                    ("ysb", [P, 4, D], F32)))
        with ExitStack() as gemma_ctx:
            w_hi, w_lo = ([gemma_ctx.enter_context(nc.sbuf_tensor(f"w_{part}{k}", [P, 2 * F1], F32R)) for k in range(3)]
                          for part in ("hi", "lo"))
            d_hi, d_lo = ([gemma_ctx.enter_context(nc.sbuf_tensor(f"d_{part}{k}", [P, F1], F32R)) for k in range(3)]
                          for part in ("hi", "lo"))
            x1T_hi, x1T_lo = (gemma_ctx.enter_context(nc.sbuf_tensor(f"x1T_{part}", [P, 2, N], F32R))
                              for part in ("hi", "lo"))
            hb_hi, hb_lo = (gemma_ctx.enter_context(nc.sbuf_tensor(f"hb_{part}", [P, 2, 512], F32R))
                            for part in ("hi", "lo"))
        x1g = sb("x1g", [P, G, D])
        cblk = sb("cblk", [P, G, D])

        s_xT, s_cond, s_const, s_gate, s_sh, s_exp0, s_fold, s_wsh, s_attw = (
            sem(n) for n in ("xT_in", "cond_in", "const_in", "gate_in", "shared_in", "experts_in",
                             "fold_in", "gemma_shared_in", "attention_in"))
        s_dve = sem("dve_chain")
        s_wb, s_h0p, s_r0p, s_h0, s_h0r, s_h0st, s_lgp = (
            sem(n) for n in ("cond_weights", "h0T_product", "h0_rows_product", "h0T_ready",
                             "h0_rows_ready", "h0_rows_stored", "logits_product"))
        s_ssu, s_sde = sem("shared_up_copied"), sem("shared_down_copied")
        s_pool = sem("pool_chain")
        s_castb, s_taken, s_pre, s_dlt, s_edl, s_onehot, s_tab, s_slots, s_pos = (
            sem(n) for n in ("constants_cast", "taken_ready", "prefix_product", "gap_ready",
                             "gap_exp", "onehots_ready", "slot_table_product", "slots_ready",
                             "positions_ready"))
        s_cd, s_ce, s_cr = sem("cond_gap_ready"), sem("cond_exp"), sem("cond_router_ready")
        s_w12p, s_w12, s_cp, s_c8, s_c2p, s_cge = (
            sem(n) for n in ("w12_product", "w12_ready", "c_product", "c_ready",
                             "c_repeat_product", "c_repeat_ready"))
        s_sgp, s_ssl, s_sact, s_sdp, s_xs = (
            sem(n) for n in ("shared_gu", "shared_silu", "shared_act", "shared_down", "xs_ready"))
        s_hpad = sem("hid_padding")
        s_xg = [sem(f"xg_in{i}") for i in range(4)]
        s_X, s_xe, s_G, s_sl, s_hm, s_H, s_he, s_D, s_ye = (
            sem(n) for n in ("xg_turned", "xgT_ready", "gu_product", "silu_ready", "hid_ready",
                             "hid_turned", "hidT_ready", "down_product", "y_ready"))
        s_yst = [sem(f"y_stored{i}") for i in range(4)]
        s_yg = [sem(f"yg_in{i}") for i in range(2)]
        s_half, s_x1, s_x1st, s_x1p, s_x1T = (
            sem(n) for n in ("x1_half", "x1_ready", "x1_stored", "x1_turned", "x1T_ready"))
        s_x1h = sem("x1_half_rows")
        s_wk = [sem(f"skill_gate_up_in{k}") for k in range(2)]
        s_wd = [sem(f"skill_down_in{k}") for k in range(2)]
        s_whi = [sem(f"gate_up_hi{k}") for k in range(3)]
        s_wlo = [sem(f"gate_up_lo{k}") for k in range(2)]
        s_dhi = [sem(f"down_hi{k}") for k in range(3)]
        s_dlo = [sem(f"down_lo{k}") for k in range(2)]
        s_lo0, s_hhi, s_hlo = sem("first_lo"), sem("gemma_hid_hi"), sem("gemma_hid_lo")
        s_x1lo, s_b1w2, s_words = sem("x1T_lo_ready"), sem("b1_w2_terms"), sem("expert_words")
        s_gu1, s_gl, s_m1, s_dn, s_z = (
            sem(n) for n in ("gemma_gu", "gelu_ready", "gemma_hid", "gemma_down", "z_ready"))
        s_kz0, s_bq, s_qkp, s_qk, s_kk, s_ka = (
            sem(n) for n in ("kz_zeroed", "bq_scaled", "qk_product", "q_ready", "keys_ready_vector", "keys_ready_scalar"))
        s_S, s_V, s_nm, s_vv, s_pr, s_rd, s_PT, s_pe, s_O, s_att = (
            sem(n) for n in ("scores_product", "v_product", "score_max", "v_ready", "probs_ready",
                             "rden_ready", "probs_turned", "probsT_ready", "o_product", "att_ready"))
        s_AT, s_ae, s_Y, s_res, s_YT, s_yT = (
            sem(n) for n in ("att_turned", "attT_ready", "proj_product", "residual_ready",
                             "y1_turned", "y1T_ready"))
        s_seed, s_rs1, s_nr1, s_nr1v, s_xb, s_acc, s_seed2, s_rs2, s_nr2, s_fov = (
            sem(n) for n in ("norm1_seed", "norm1_scale_ready", "norm1_scaled", "norm1_last_scaled",
                             "x1_plus_bias", "moe_accumulated", "norm2_seed", "norm2_scale_ready",
                             "norm2_scaled", "last_final_ready"))
        s_l1, s_gap1, s_e1, s_oh1, s_loc, s_gk, s_gkp, s_gkT, s_bp, s_base = (
            sem(n) for n in ("moe_logits", "moe_gap", "moe_exp", "moe_onehot", "moe_location",
                             "moe_gates", "gates_turned", "gatesT_ready", "bias_product",
                             "base_ready"))
        s_x1g, s_cblk, s_ym, s_fo, s_lgc, s_part, s_psum = (
            sem(n) for n in ("x1_grouped_in", "cblk_ready", "moe_product", "final_ready",
                             "moe_logits_copied", "moe_parts_ready", "moe_parts_summed"))
        s_fsta = sem("out_stored_by_scalar")
        s_fst = [sem(f"out_stored{i}") for i in range(2)]

        group = lambda ap, g: ap[:, P * g:P * g + P]

        block = ctx.enter_context(nc.Block())

        def store_out(engine, batches_of_groups, members, stored):
            for q in batches_of_groups:
                if q < NB - 1:
                    engine.wait_ge(s_fo, q + 1)
                for j in members:
                    g = BLK * q + j
                    if q == NB - 1:
                        engine.wait_ge(s_fov, j + 1)
                    engine.dma_start(out_d[:, GN * g:GN * g + GN, :], fin[:, q % 2, j, :]).then_inc(stored[q % 2], 16)

        @block.sync
        def _(sp):
            sp.dma_start(y_bc[:], cond_d.rearrange("b e -> (b e)").partition_broadcast(P)).then_inc(s_cond, 16)
            sp.dma_start(cw[:, 0], cw_d).then_inc(s_cond, 16)
            sp.dma_start(cmask[:], cmask_d).then_inc(s_cond, 16)
            sp.dma_start(cbias[:], cbias_d).then_inc(s_cond, 16)
            sp.dma_start(vecs[:], vecs_d.partition_broadcast(P)).then_inc(s_cond, 16)
            sp.dma_start(xT[:], xT_d).then_inc(s_xT, 16)
            sp.dma_start(gate_w[:], gate_d).then_inc(s_gate, 16)
            sp.dma_start(const[:], const_d).then_inc(s_const, 16)
            sp.dma_start(sgu[:], sgu_d).then_inc(s_sh, 16)
            sp.dma_start(sd[:], sd_d).then_inc(s_sh, 16)
            sp.dma_start(xs[:], x_d.rearrange("(t p) d -> p t d", p=P)).then_inc(s_sh, 16)
            sp.dma_start(wgu[:], wgu_d).then_inc(s_exp0, 16)
            sp.dma_start(wd[:], wd_d).then_inc(s_exp0, 16)
            for blk in range(NB):
                sp.wait_ge(s_h0r, blk + 1)
                sp.dma_start(h0_rows[512 * blk:512 * blk + 512, :].rearrange("(t p) d -> p t d", p=P),
                             h0r[:, BLK * blk:BLK * blk + BLK, :]).then_inc(s_h0st, 16)
            sp.dma_start(w12in[:, 0], w1_d).then_inc(s_fold, 16)
            sp.dma_start(w12in[:, 1], w2_d).then_inc(s_fold, 16)
            sp.dma_start(b1[:], b1_d).then_inc(s_fold, 16)
            sp.dma_start(b2[:], b2_d).then_inc(s_fold, 16)
            sp.dma_start(wsh[:], wsh_d).then_inc(s_wsh, 16)
            sp.dma_start(wqkv[:], wqkv_d).then_inc(s_attw, 16)
            sp.dma_start(wo[:], wo_d).then_inc(s_attw, 16)
            sp.dma_start(bqkv[:], bqkv_d).then_inc(s_attw, 16)
            sp.dma_start(wg[:], wg_d).then_inc(s_attw, 16)
            sp.dma_start(cols1[:], cols1_d).then_inc(s_attw, 16)
            gate_up_part, down_part = slice(0, 2 * F1), slice(2 * F1, 3 * F1)

            def load_skill(e, k, part, loaded):
                sp.dma_start(wk[k][:, part], wexp_d[bass.ds(e, 1), :, part].rearrange("a p n -> (a p) n")).then_inc(loaded, 16)

            sp.wait_ge(s_cr, 1)
            for k in range(2):
                e = sp.value_load(cix[0:1, k, 0:1], min_val=0, max_val=E - 1)
                load_skill(e, k, gate_up_part, s_wk[k])
                load_skill(e, k, down_part, s_wd[k])
            with sp.Fori(0, ROUNDS - 1) as jj:
                for r in range(4):
                    sp.wait_ge(s_ye, jj * 4 + r + 1)
                    sp.dma_start(y_rows[bass.ds((jj * 4 + r) * P, P), :], ysb[:, r, :]).then_inc(s_yst[r], 16)
            for j in range(4 * (ROUNDS - 1), SLOT_TILES):
                sp.wait_ge(s_ye, j + 1)
                sp.dma_start(y_rows[j * P:j * P + P, :], ysb[:, j % 4, :]).then_inc(s_yst[j % 4], 16)

            def store_x1(b, par):
                sp.wait_ge(s_x1, b + 1)
                sp.dma_start(x1_rows[bass.ds(b * N, N), :].rearrange("(t p) d -> p t d", p=P),
                             x1t[:, par]).then_inc(s_x1st, 16)

            def load_gate_up(b, k):
                e = sp.value_load(cix[0:1, k, bass.ds(b, 1)], min_val=0, max_val=E - 1)
                sp.wait_ge(s_gu1, b * 6 - 6 + (2 * k + 1))
                load_skill(e, k, gate_up_part, s_wk[k])

            def load_down(b, k):
                e = sp.value_load(cix[0:1, k, bass.ds(b, 1)], min_val=0, max_val=E - 1)
                sp.wait_ge(s_dn, b * 6 - 6 + (2 * k + 1))
                load_skill(e, k, down_part, s_wd[k])

            def row_traffic(b, par):
                load_gate_up(b, 0)
                load_down(b, 0)
                load_gate_up(b, 1)
                store_x1(b, par)
                load_down(b, 1)

            store_x1(0, 0)
            with sp.Fori(0, B // 2 - 1) as bp:
                for u in range(2):
                    row_traffic(bp * 2 + u + 1, (u + 1) % 2)
            row_traffic(B - 1, 1)
            sp.wait_ge(s_x1st, 16 * B)
            sp.wait_ge(s_dn, 6 * B)
            for l in range(B):
                sp.dma_start(x1g[GN * l:GN * l + GN, :, :],
                             x1_rows[N * l:N * l + N, :].rearrange("(g n) d -> n g d", n=GN)).then_inc(s_x1g, 16)
            store_out(sp, range(0, NB - 2), range(BLK), s_fst)
            store_out(sp, (NB - 1, NB - 2), range(0, BLK // 2), s_fst)
            for r in range(2):
                sp.wait_ge(s_fst[r], 16 * (BLK * (NB // 2 - 1) + BLK // 2))

        @block.gpsimd
        def _(pool):
            nc.gpsimd.memset(hid[:], 0.0).then_inc(s_hpad, 1)
            pool.wait_ge(s_const, 16)
            nc.gpsimd.tensor_copy(before_b[:], K("before")).then_inc(s_castb, 1)
            nc.gpsimd.tensor_copy(ones_b[:], K("ones")).then_inc(s_castb, 1)
            nc.gpsimd.tensor_copy(ident_b[:], K("ident")).then_inc(s_castb, 1)
            nc.gpsimd.tensor_copy(mask_b[:], K("mask").unsqueeze(1).broadcast_to([P, H, P])).then_inc(s_castb, 1)
            for n in rowm:
                nc.gpsimd.tensor_copy(rowm[n][:], K(n)).then_inc(s_castb, 1)
            pool.wait_ge(s_sh, 48)

            def shared_xs(blk):
                pool.wait_ge(s_sde, blk + 1)
                t = xs[:, BLK * blk:BLK * blk + BLK]
                nc.gpsimd.tensor_tensor(t, sdn[:, BLK * (blk % 2):BLK * (blk % 2) + BLK], t, ALU.add).then_inc(s_xs, 1)

            for n in range(2 * NB):
                pool.wait_ge(s_ssl, n + 1)
                pool.wait_ge(s_ssu, n + 1)
                if n >= 4:
                    pool.wait_ge(s_sdp, n // 2 - 1)
                nc.gpsimd.tensor_tensor(sact[:, (n // 2) % 2, n % 2], sgl[:, n % 2], sul[:, n % 2], ALU.mult).then_inc(s_sact, 1)
                if n in (3, 5):
                    shared_xs(n // 2 - 1)
            pool.wait_ge(s_h0st, 16 * NB)
            pool.wait_ge(s_slots, 1)
            for j in range(SLOT_TILES):
                if j >= 4:
                    pool.wait_ge(s_X, j - 3)
                nc.gpsimd.indirect_dma_start(
                    out=xg[:, j % 4, :], out_offset=None, in_=h0_rows,
                    in_offset=bass.IndirectOffsetOnAxis(ap=slot_tok[:, j:j + 1], axis=0)).then_inc(s_xg[j % 4], 16)
                if j in (3, 5):
                    shared_xs(NB - 2 if j == 3 else NB - 1)
            for r in range(4):
                pool.wait_ge(s_yst[r], 16 * len(range(r, SLOT_TILES, 4)))
            pool.wait_ge(s_pos, 1)
            def gather_results(b):
                if b >= 2:
                    pool.wait_ge(s_x1, b - 1)
                for i in range(2):
                    for k in range(2):
                        nc.gpsimd.indirect_dma_start(
                            out=yg[:, b % 2, i, k, :], out_offset=None, in_=y_rows,
                            in_offset=bass.IndirectOffsetOnAxis(ap=pos_u[:, k, 2 * b + i:2 * b + i + 1], axis=0)
                        ).then_inc(s_yg[b % 2], 16)

            def split_lo(b, k, which, hi, lo, hi_ready, lo_ready):
                pool.wait_ge(hi_ready[k], b + 1)
                nc.gpsimd.tensor_tensor(lo[k][:], wk[k][:, which], hi[k][:].bitcast(F32), ALU.subtract).then_inc(lo_ready[k], 1)

            for b in range(3):
                gather_results(b)
            pool.wait_ge(s_w12p, 1)
            pool.wait_ge(s_cp, 1)
            for b in range(1, B):
                split_lo(b, 1, slice(0, 2 * F1), w_hi, w_lo, s_whi, s_wlo)
                for k in range(2):
                    split_lo(b, k, slice(2 * F1, 3 * F1), d_hi, d_lo, s_dhi, s_dlo)
                if b + 2 < B:
                    gather_results(b + 2)
                for g in range((b - 1) * G // (B - 1), b * G // (B - 1)):
                    nc.gpsimd.memset(kz[:, g], 0.0).then_inc(s_kz0, 1)
            pool.wait_ge(s_cge, 1)
            pool.wait_ge(s_dn, 6 * B)
            nc.gpsimd.tensor_tensor(cblk[:], c_ge[:].unsqueeze(1).broadcast_to([P, G, D]),
                                    K("own_group").unsqueeze(2).broadcast_to([P, G, D]), ALU.mult).then_inc(s_cblk, 1)
            chain = [0]

            def link(ins):
                chain[0] += 1
                ins.then_inc(s_pool, 1)
                pool.wait_ge(s_pool, chain[0])

            def newton_steps(q):
                w, z, v = rs1[:, q % 2], newton[:, q % 2], var_e[:, q % 2]
                for _ in range(3):
                    link(nc.gpsimd.tensor_tensor(z, w, w, ALU.mult))
                    link(nc.gpsimd.tensor_tensor(z, z, v, ALU.mult))
                    link(nc.gpsimd.tensor_scalar(z, z, -0.5, 1.5, ALU.mult, ALU.add))
                    link(nc.gpsimd.tensor_tensor(w, w, z, ALU.mult))

            def rows(vec):
                return vec.unsqueeze(1).broadcast_to([P, BLK, D])

            def scale_and_shift(q):
                newton_steps(q)
                link(nc.gpsimd.tensor_tensor(shift1[:, q % 2], mv1[:, q % 2, :, 0], rs1[:, q % 2], ALU.mult))
                return nc.gpsimd.tensor_scalar(shift1[:, q % 2], shift1[:, q % 2], -1.0, None, ALU.mult)

            for q in range(NB - 1):
                pool.wait_ge(s_seed, q + 1)
                scale_and_shift(q).then_inc(s_rs1, 1)
                if q == 0:
                    pool.wait_ge(s_x1g, 16 * B)
                    nc.gpsimd.tensor_tensor(x1g[:], x1g[:], n2_bc.unsqueeze(1).broadcast_to([P, G, D]), ALU.add).then_inc(s_xb, 1)
            for g in range(1, G, 2):
                pool.wait_ge(s_part, E // 2 * (g + 1))
                t = part[:, g % 4 - 1:g % 4 + 1]
                link(nc.gpsimd.tensor_tensor(t[:, :, 0:2], t[:, :, 0:2], t[:, :, 2:4], ALU.add))
                nc.gpsimd.tensor_tensor(t[:, :, 0], t[:, :, 0], t[:, :, 1], ALU.add).then_inc(s_psum, 1)
                if g in (BLK + 1, 2 * BLK + 1, G - 1):
                    q = min(g // BLK - 1, NB - 2)
                    pool.wait_ge(s_seed2, q + 1)
                    scale_and_shift(q).then_inc(s_rs2, 1)
                if g % BLK == 3 and g > BLK:
                    q = g // BLK - 1
                    pool.wait_ge(s_nr2, BLK * (q + 1))
                    link(nc.gpsimd.tensor_tensor(nrg2[:, q % 2], nrm2[:, q % 2], rows(g2_bc), ALU.mult))
                    if q == 0:
                        pool.wait_ge(s_xb, 1)
                    if q >= 2:
                        pool.wait_ge(s_fst[q % 2], 16 * BLK * (q // 2))
                    nc.gpsimd.tensor_tensor(fin[:, q % 2], nrg2[:, q % 2], x1g[:, BLK * q:BLK * q + BLK], ALU.add).then_inc(s_fo, 1)

        @block.scalar
        def _(act):
            act.wait_ge(s_cond, 80)
            for blk in range(NB):
                act.wait_ge(s_h0p, blk + 1)
                nc.scalar.activation(h0T[:, 512 * blk:512 * blk + 512], bank[blk % 2][:], ACT.Identity,
                                     bias=cbias[:]).then_inc(s_h0, 1)
            act.wait_ge(s_cd, 1)
            nc.scalar.activation(ce[:], cd[:], ACT.Exp).then_inc(s_ce, 1)
            def shared_down_copy(blk):
                act.wait_ge(s_sdp, blk + 1)
                if blk >= 2:
                    act.wait_ge(s_xs, blk - 1)
                nc.scalar.activation(sdn[:, BLK * (blk % 2):BLK * (blk % 2) + BLK],
                                     bank[5][:].rearrange("p (t d) -> p t d", t=BLK), ACT.Copy).then_inc(s_sde, 1)

            for n in range(2 * NB):
                act.wait_ge(s_sgp, n + 1)
                if n >= 2:
                    act.wait_ge(s_sact, n - 1)
                nc.scalar.activation(sgl[:, n % 2], bank[n % 2][0:SC, :], ACT.Silu).then_inc(s_ssl, 1)
                nc.scalar.activation(sul[:, n % 2], bank[2 + n % 2][0:SC, :], ACT.Copy).then_inc(s_ssu, 1)
                if n == 3:
                    act.wait_ge(s_h0st, 16 * NB)
                if n % 2 and n > 1:
                    shared_down_copy(n // 2 - 1)
            act.wait_ge(s_dlt, 1)
            nc.scalar.activation(edl[:], dlt[:], ACT.Exp).then_inc(s_edl, 1)
            shared_down_copy(NB - 1)
            nc.scalar.activation(warm[:], cbias[:], ACT.Silu)

            def silu(j, r, ring):
                act.wait_ge(s_G, j + 1)
                if ring:
                    act.wait_ge(s_hm, j - 1)
                nc.scalar.activation(slu[:, r], bank[2 * r][:, 0:F0], ACT.Silu).then_inc(s_sl, 1)

            def hidT_copy(j, r, ring):
                act.wait_ge(s_H, j + 1)
                if ring:
                    act.wait_ge(s_D, j - 1)
                nc.scalar.activation(hidT[:, r], bank[4 + r][:, 0:3 * P], ACT.Copy).then_inc(s_he, 1)

            silu(0, 0, False)
            silu(1, 1, False)
            hidT_copy(0, 0, False)
            silu(2, 0, True)
            hidT_copy(1, 1, False)
            silu(3, 1, True)
            hidT_copy(2, 0, True)
            with act.Fori(1, ROUNDS - 1) as jj:
                for u in range(4):
                    silu(jj * 4 + u, u % 2, True)
                    hidT_copy(jj * 4 + (u - 1), (u + 1) % 2, True)
            for j in range(4 * (ROUNDS - 1), SLOT_TILES):
                silu(j, j % 2, True)
                hidT_copy(j - 1, (j - 1) % 2, True)
            hidT_copy(SLOT_TILES - 1, (SLOT_TILES - 1) % 2, True)

            def x1T_copy(b, par):
                act.wait_ge(s_x1p, b + 1)
                nc.scalar.activation(x1T_hi[:, par], bank[6 + par][:, 0:N], ACT.Copy).then_inc(s_x1T, 1)

            def split_hi(b, k, raw, first=False):
                act.wait_ge(s_wk[k] if k < 2 else s_wsh, 16 * b + 16)
                if not first:
                    act.wait_ge(s_gu1, b * 6 - 6 + 2 * (k + 1))
                nc.scalar.activation(w_hi[k][:], raw[:, 0:2 * F1], ACT.Copy).then_inc(s_whi[k], 1)

            def gelu(b, hh, ring):
                act.wait_ge(s_gu1, b * 6 + (hh + 1))
                if ring:
                    act.wait_ge(s_m1, b * 6 + (hh - 1))
                nc.scalar.activation(gl[:, hh % 2], bank[hh % 2][:], ACT.Gelu_apprx_tanh).then_inc(s_gl, 1)

            def z_copy(b):
                act.wait_ge(s_dn, b * 6 + 6)
                nc.scalar.activation(zT[:].rearrange("p (g l n) -> p g l n", g=G, l=B)[:, :, bass.ds(b, 1), :].rearrange("p g a n -> p g (a n)"),
                                     bank[4][:, 0:N].rearrange("p (g n) -> p g n", g=G), ACT.Copy).then_inc(s_z, 1)

            def split_down_hi(b, k, raw, first=False):
                act.wait_ge(s_wd[k] if k < 2 else s_wsh, 16 * b + 16)
                if not first:
                    act.wait_ge(s_dn, b * 6 - 6 + 2 * (k + 1))
                nc.scalar.activation(d_hi[k][:], raw[:, 2 * F1:], ACT.Copy).then_inc(s_dhi[k], 1)

            def hid_hi(b, hh, ring):
                act.wait_ge(s_m1, b * 6 + (hh + 1))
                if ring:
                    act.wait_ge(s_dn, b * 6 + (hh - 1))
                nc.scalar.activation(hb_hi[:, hh % 2], hb[:, hh % 2], ACT.Copy).then_inc(s_hhi, 1)

            def act_row(b, par, first=False, last=False):
                for hh in range(6):
                    if hh == 2 and not first:
                        z_copy(b - 1)
                    if hh > 0:
                        hid_hi(b, hh - 1, not (first and hh <= 2))
                    elif not first:
                        hid_hi(b - 1, 5, True)
                    gelu(b, hh, not (first and hh < 2))
                    if hh < 2 and not first:
                        split_down_hi(b, hh, wk[hh])
                    if hh == 3 and not last:
                        split_hi(b + 1, 0, wk[0])
                    if hh == 4 and not last:
                        x1T_copy(b + 1, 1 - par)
                    if hh == 5 and not last:
                        split_hi(b + 1, 1, wk[1])

            act.wait_ge(s_D, SLOT_TILES)
            for k, raw in enumerate((*wk, wsh)):
                split_hi(0, k, raw, first=True)
                split_down_hi(0, k, raw, first=True)
            nc.scalar.activation(warm[:], cbias[:], ACT.Gelu_apprx_tanh)
            act.wait_ge(s_w12p, 1)
            for i in range(2):
                nc.scalar.activation(W12[:, 512 * i:512 * i + 512], bank[2 + i][:], ACT.Copy).then_inc(s_w12, 1)
            x1T_copy(0, 0)
            act.wait_ge(s_c2p, 1)
            nc.scalar.activation(c_ge[:], bank[5][:, 0:P], ACT.Copy).then_inc(s_cge, 1)
            act_row(0, 0, first=True)
            act_row(1, 1)
            with act.Fori(1, B // 2 - 1) as bp:
                for u in range(2):
                    act_row(bp * 2 + u, u)
            act_row(B - 2, 0)
            act_row(B - 1, 1, last=True)
            hid_hi(B - 1, 5, True)
            z_copy(B - 1)

            act.wait_ge(s_attw, 80)
            act.wait_ge(s_bq, 1)
            for blk in range(NB):
                act.wait_ge(s_qkp, blk + 1)
                nc.scalar.activation(qT[:, 512 * blk:512 * blk + 512], bank[2 * (blk % 2)][:], ACT.Identity,
                                     bias=bq_s[:], scale=HD ** -0.5).then_inc(s_qk, 1)
                act.wait_ge(s_kz0, G)
                for h in range(2):
                    a = HD * h
                    nc.scalar.activation(
                        kz[a:a + HD, BLK * blk:BLK * blk + BLK, h, :],
                        bank[2 * (blk % 2) + 1][a:a + HD, :].rearrange("p (g k) -> p g k", g=BLK),
                        ACT.Identity, bias=bqkv[a:a + HD, 1:2]).then_inc(s_ka, 1)
            for i in range(G + 10):
                if i < G:
                    act.wait_ge(s_nm, i + 1)
                    if i >= 2:
                        act.wait_ge(s_PT, i - 1)
                        act.wait_ge(s_rd, i - 1)
                    for h in range(H):
                        nc.scalar.activation(pr[:, i % 2, h], bank[i % 2][:, P * h:P * h + P], ACT.Exp,
                                             bias=nmax[:, i % 2, h:h + 1],
                                             accum_out=den[:, i % 2, h:h + 1]).then_inc(s_pr, 1)
                if i % BLK == 2 and i >= 6 and (i - 6) // BLK < NB:
                    q = (i - 6) // BLK
                    act.wait_ge(s_AT, q + 1)
                    if q >= 2:
                        act.wait_ge(s_Y, q - 1)
                    nc.scalar.activation(attT[:, q % 2], bank[5][:], ACT.Copy).then_inc(s_ae, 1)
                if i % BLK == 3 and i >= 11:
                    q = (i - 11) // BLK
                    if q < NB - 1:
                        act.wait_ge(s_rs1, q + 1)
                    if q >= 2:
                        act.wait_ge(s_YT, q - 1)
                    for j in range(BLK if q < NB - 1 else 0):
                        nc.scalar.activation(nrm[:, q % 2, j], res[:, q % 2, j], ACT.Identity,
                                             bias=shift1[:, q % 2, j:j + 1], scale=rs1[:, q % 2, j:j + 1]).then_inc(s_nr1, 1)
                if i % BLK == 0 and i >= 12:
                    q = (i - 12) // BLK
                    act.wait_ge(s_YT, q + 1)
                    nc.scalar.activation(y1T[:, BLK * q:BLK * q + BLK], bank[7][:].rearrange("p (g k) -> p g k", g=BLK),
                                         ACT.Identity, bias=cols1[:, 1:2], scale=cols1[:, 0:1]).then_inc(s_yT, 1)
            act.wait_ge(s_gap1, 1)
            nc.scalar.activation(e1[:], t8[:], ACT.Exp).then_inc(s_e1, 1)
            act.wait_ge(s_gkp, 1)
            nc.scalar.activation(gkT[:], bank[3][:, 0:P], ACT.Copy).then_inc(s_gkT, 1)

            def normalise2(q):
                act.wait_ge(s_rs2, q + 1)
                if q >= 2:
                    act.wait_ge(s_fo, q - 1)
                for j in range(BLK):
                    nc.scalar.activation(nrm2[:, q % 2, j], macc[:, q % 2, j], ACT.Identity,
                                         bias=shift1[:, q % 2, j:j + 1], scale=rs1[:, q % 2, j:j + 1]).then_inc(s_nr2, 1)

            def base_copy(blk):
                act.wait_ge(s_bp, blk + 1)
                nc.scalar.activation(base[:, BLK * blk:BLK * blk + BLK],
                                     bank[4 + blk][:].rearrange("p (g d) -> p g d", g=BLK), ACT.Copy).then_inc(s_base, 1)

            base_copy(0)
            act.wait_ge(s_gk, 1)
            for g in range(G):
                act.wait_ge(s_ym, g + 1)
                if g >= 4:
                    act.wait_ge(s_acc, g - 3)
                for e in range(E // 2):
                    nc.scalar.activation(part[:, g % 4, e], bank[2 * (g % 4) + 1][:, D * e:D * e + D], ACT.Copy,
                                         scale=gk[:, g, E // 2 + e:E // 2 + e + 1]).then_inc(s_part, 1)
                if g == 0:
                    base_copy(1)
                if g == 1:
                    base_copy(2)
                    base_copy(3)
                if g % BLK == 3 and g > BLK:
                    normalise2(g // BLK - 1)
            store_out(act, (NB - 1, NB - 2), range(BLK // 2, BLK), [s_fsta, s_fsta])
            act.wait_ge(s_fsta, 16 * BLK)

        @block.tensor
        def _(pe):
            ident = K("ident")
            mm = nc.tensor.matmul
            pe.wait_ge(s_xT, 16)

            def logits(blk):
                pe.wait_ge(s_h0, blk + 1)
                for t in range(BLK * blk, BLK * blk + BLK):
                    last = mm(bank[4][:, E * t:E * t + E], h0T[:, P * t:P * t + P], gate_w[:], start=True, stop=True)
                last.then_inc(s_lgp, 1)

            def keep_warm(count, target, source):
                for _ in range(count):
                    mm(target[:], source[:, 0:P], source[:, 0:BLK * P], start=True, stop=True)

            mask_flat = mask_b[:].rearrange("p h k -> p (h k)")

            cw_flat = cw[:, 0].rearrange("p e d -> p (e d)")

            def h0_columns(blk):
                pe.wait_ge(s_wb, blk + 1)
                if blk >= 2:
                    pe.wait_ge(s_h0, blk - 1)
                for b in (2 * blk, 2 * blk + 1):
                    last = mm(bank[blk % 2][:, N * (b % 2):N * (b % 2) + N], wbt[:, b, :], xT[:, N * b:N * b + N],
                              start=True, stop=True)
                last.then_inc(s_h0p, 1)

            def h0_of_tiles(blk):
                for i in range(BLK):
                    t = BLK * blk + i
                    last = mm(row_bank[blk][:, P * i:P * i + P], xT[:, P * t:P * t + P], wbt[:, t // 2, :],
                              start=True, stop=True)
                last.then_inc(s_r0p, 1)

            pe.wait_ge(s_cond, 80)
            keep_warm(3, bank[5], cw_flat)
            h0_columns(0)
            h0_of_tiles(0)
            keep_warm(1, bank[5], cw_flat)
            h0_columns(1)
            pe.wait_ge(s_gate, 16)
            logits(0)
            h0_of_tiles(1)
            keep_warm(1, bank[5], cw_flat)
            h0_columns(2)
            logits(1)
            keep_warm(2, bank[5], cw_flat)
            h0_columns(3)
            logits(2)
            h0_of_tiles(2)
            logits(3)
            h0_of_tiles(3)

            def prefixes():
                pe.wait_ge(s_castb, 4 + len(rowm))
                pe.wait_ge(s_taken, 1)
                mm(bank[4][:, 128:256], before_b[:], taken[:].rearrange("p t e -> p (t e)"), start=True, stop=True)
                mm(bank[4][:, 256:384], ones_b[:], taken[:].rearrange("p t e -> p (t e)"),
                   start=True, stop=True).then_inc(s_pre, 1)

            def shared_gu(n):
                blk, c = n // 2, n % 2
                if n >= 2:
                    pe.wait_ge(s_ssl, n - 1)
                    pe.wait_ge(s_ssu, n - 1)
                for i in range(2):
                    last = mm(bank[2 * i + c][0:SC, :], sgu[:, FS * i + SC * c:FS * i + SC * c + SC],
                              h0T[:, 512 * blk:512 * blk + 512], start=True, stop=True)
                last.then_inc(s_sgp, 1)

            def shared_down(blk):
                pe.wait_ge(s_sact, 2 * blk + 2)
                if blk >= 1:
                    pe.wait_ge(s_sde, blk)
                for i in range(BLK):
                    for c in range(2):
                        last = mm(bank[5][:, P * i:P * i + P], sact[:, blk % 2, c, P * i:P * i + P],
                                  sd[:, c], start=(c == 0), stop=(c == 1))
                last.then_inc(s_sdp, 1)

            def slot_table():
                pe.wait_ge(s_onehot, 1)
                for i in range(2 * NT):
                    last = mm(bank[4][:, 384:384 + SLOT_TILES], ohlo[:, i, :], ohhi[:, i], start=(i == 0), stop=(i == 2 * NT - 1))
                last.then_inc(s_tab, 1)

            pe.wait_ge(s_sh, 48)
            pe.wait_ge(s_h0r, 2)
            for n in range(2 * NB):
                shared_gu(n)
                if n == 0:
                    prefixes()
                if n == 6:
                    slot_table()
                if n % 2 and n > 1:
                    shared_down(n // 2 - 1)
            shared_down(NB - 1)

            def turn_x(j, r4, ring, gathers):
                pe.wait_ge(s_xg[r4], gathers * 16)
                if ring:
                    pe.wait_ge(s_xe, j)
                pe.transpose(bank[6][:, 0:P], xg[:, r4], ident).then_inc(s_X, 1)

            def expert_of(j):
                return pe.value_load(eslot[0:1, j:j + 1] if isinstance(j, int) else eslot[0:1, bass.ds(j, 1)],
                                     min_val=0, max_val=E - 1)

            def gate_up(j, r, ring, e):
                pe.wait_ge(s_xe, j + 1)
                if ring:
                    pe.wait_ge(s_hm, j - 1)
                mm(bank[2 * r][:, 0:F0], xgT[:, r], wgu[:, bass.ds(e * (2 * F0), F0)], start=True, stop=True)
                mm(bank[2 * r + 1][:, 0:F0], xgT[:, r], wgu[:, bass.ds(e * (2 * F0) + F0, F0)],
                   start=True, stop=True).then_inc(s_G, 1)

            def turn_hid(j, r, ring):
                pe.wait_ge(s_hm, j + 1)
                if ring:
                    pe.wait_ge(s_he, j - 1)
                for c in range(3):
                    last = pe.transpose(bank[4 + r][:, P * c:P * c + P], hid[:, r, P * c:P * c + P], ident)
                last.then_inc(s_H, 1)

            def down(j, r, ring, e):
                pe.wait_ge(s_he, j + 1)
                if ring:
                    pe.wait_ge(s_ye, j)
                for c in range(3):
                    last = mm(bank[7][:, 0:P], hidT[:, r, P * c:P * c + P],
                              wd[:, bass.ds(e, 1), c, :].rearrange("p a d -> p (a d)"), start=(c == 0), stop=(c == 2))
                last.then_inc(s_D, 1)

            pe.wait_ge(s_h0r, NB)
            keep_warm(1, bank[7], const)
            pe.wait_ge(s_exp0, 32)
            pe.wait_ge(s_slots, 1)
            turn_x(0, 0, False, 1)
            for j in range(4):
                e = expert_of(j)
                d = expert_of(j - 3) if j >= 3 else None
                if j == 2:
                    pe.wait_ge(s_sde, NB)
                if j >= 2:
                    turn_hid(j - 2, j % 2, False)
                if j >= 3:
                    down(j - 3, (j - 3) % 2, False, d)
                gate_up(j, j % 2, j >= 2, e)
                turn_x(j + 1, (j + 1) % 4, True, (j + 1) // 4 + 1)
            pe.wait_ge(s_words, 1)
            with pe.Fori(1, ROUNDS - 1) as jj:
                for u in range(4):
                    j = jj * 4 + u
                    turn_hid(jj * 4 + (u - 2), u % 2, True)
                    if u == 0:
                        word = pe.value_load(words_i[0:1, bass.ds(jj, 1)], min_val=0, max_val=E ** 7 - 1)
                    expert = lambda i: ((word >> (3 * i)) & (E - 1))
                    down(jj * 4 + (u - 3), (u + 1) % 2, True, expert(u))
                    gate_up(j, u % 2, True, expert(u + 3))
                    turn_x(j + 1, (u + 1) % 4, True, jj + (2 if u == 3 else 1))
            for j in range(4 * (ROUNDS - 1), SLOT_TILES + 3):
                e = expert_of(j) if j < SLOT_TILES else None
                d = expert_of(j - 3)
                if j - 2 < SLOT_TILES:
                    turn_hid(j - 2, j % 2, True)
                down(j - 3, (j - 3) % 2, True, d)
                if j < SLOT_TILES:
                    gate_up(j, j % 2, True, e)
                if j + 1 < SLOT_TILES:
                    turn_x(j + 1, (j + 1) % 4, True, (j + 1) // 4 + 1)

            pe.wait_ge(s_fold, 64)
            for e in range(E):
                for c in range(C2):
                    last = mm(bank[2 + e // 4][:, P * (e % 4):P * (e % 4) + P], w12in[:, 0, e, c],
                              w12in[:, 1, e, c], start=(c == 0), stop=(c == C2 - 1))
            last.then_inc(s_w12p, 1)
            pe.wait_ge(s_b1w2, E * C2)
            for e in range(E):
                last = mm(bank[5][0:E, 0:D], K("eye8")[:, E * e:E * e + E], b1w2[:, e], start=(e == 0), stop=(e == E - 1))
            last.then_inc(s_cp, 1)

            def turn_x1(b, par):
                pe.wait_ge(s_x1, b + 1)
                for i in range(2):
                    last = pe.transpose(bank[6 + par][:, P * i:P * i + P], x1t[:, par, i], ident)
                last.then_inc(s_x1p, 1)

            def gemma_gu(b, par, hh, ring, first):
                k, q = hh // 2, hh % 2
                if q == 0 and k < 2 and not first:
                    pe.wait_ge(s_wlo[k], b)
                if hh == 0:
                    pe.wait_ge(s_x1lo, b + 1)
                if ring:
                    pe.wait_ge(s_m1, b * 6 + (hh - 1))
                for i in range(2):
                    for c in range(2):
                        a = F1 * i + P * (2 * q + c)
                        o = bank[2 * i + hh % 2][:, N * c:N * c + N]
                        mm(o, w_hi[k][:, a:a + P], x1T_hi[:, par], start=True, stop=False)
                        mm(o, w_hi[k][:, a:a + P], x1T_lo[:, par], start=False, stop=False)
                        last = mm(o, w_lo[k][:, a:a + P], x1T_hi[:, par], start=False, stop=True)
                last.then_inc(s_gu1, 1)

            def gemma_down(b, hh, first):
                k, q = hh // 2, hh % 2
                pe.wait_ge(s_hlo, b * 6 + (hh + 1))
                if q == 0 and k < 2 and not first:
                    pe.wait_ge(s_dlo[k], b)
                if hh == 0 and not first:
                    pe.wait_ge(s_z, b)
                for c in range(2):
                    a = P * (2 * q + c)
                    n = slice(N * c, N * c + N)
                    o = bank[4][:, 0:N]
                    mm(o, d_hi[k][:, a:a + P], hb_hi[:, hh % 2, n], start=(hh == 0 and c == 0), stop=False,
                       skip_group_check=True)
                    mm(o, d_hi[k][:, a:a + P], hb_lo[:, hh % 2, n], start=False, stop=False, skip_group_check=True)
                    last = mm(o, d_lo[k][:, a:a + P], hb_hi[:, hh % 2, n], start=False,
                              stop=(hh == 5 and c == 1), skip_group_check=True)
                last.then_inc(s_dn, 1)

            def pe_row(b, par, first=False, last=False):
                for hh in range(6):
                    gemma_gu(b, par, hh, not (first and hh < 2), first)
                    if hh > 1:
                        gemma_down(b, hh - 2, first)
                    elif not first:
                        gemma_down(b - 1, hh + 4, False)
                    if hh == 4 and not last:
                        turn_x1(b + 1, 1 - par)

            pe.wait_ge(s_lo0, 6)
            turn_x1(0, 0)
            pe.wait_ge(s_c8, 1)
            mm(bank[5][:, 0:D], K("repeat8")[0:E], c_e[:], start=True, stop=True).then_inc(s_c2p, 1)
            pe.wait_ge(s_w12, 2)
            pe_row(0, 0, first=True)
            pe_row(1, 1)
            with pe.Fori(1, B // 2 - 1) as bp:
                for u in range(2):
                    pe_row(bp * 2 + u, u)
            pe_row(B - 2, 0)
            pe_row(B - 1, 1, last=True)
            gemma_down(B - 1, 4, False)
            gemma_down(B - 1, 5, False)

            pe.wait_ge(s_attw, 80)
            pe.wait_ge(s_z, B)
            for blk in range(NB):
                if blk >= 2:
                    pe.wait_ge(s_qk, blk - 1)
                    pe.wait_ge(s_kk, 2 * (blk - 1))
                    pe.wait_ge(s_ka, 2 * (blk - 1))
                    pe.wait_ge(s_vv, blk - 1)
                for i in range(2):
                    last = mm(bank[2 * (blk % 2) + i][:], wqkv[:, D * i:D * i + D], zT[:, 512 * blk:512 * blk + 512],
                              start=True, stop=True)
                last.then_inc(s_qkp, 1)
                for j in range(BLK):
                    last = mm(bank[4 + blk % 2][:, P * j:P * j + P], group(zT, BLK * blk + j), wqkv[:, 2 * D:3 * D],
                              start=True, stop=True)
                last.then_inc(s_V, 1)
            pe.wait_ge(s_qk, NB)
            pe.wait_ge(s_kk, 2 * NB)
            pe.wait_ge(s_ka, 2 * NB)
            pe.wait_ge(s_vv, NB)
            for i in range(G + 10):
                g = i
                if g < G:
                    if g >= 2:
                        pe.wait_ge(s_pr, H * (g - 1))
                    mm(bank[g % 2][:], group(qT, g), kz[:, g].rearrange("p h k -> p (h k)"), start=True, stop=False)
                    mm(bank[g % 2][:], ident_b[:], mask_b[:].rearrange("p h k -> p (h k)"),
                       start=False, stop=True).then_inc(s_S, 1)
                g = i - 1
                if 0 <= g < G:
                    pe.wait_ge(s_pr, H * (g + 1))
                    if g >= 2:
                        pe.wait_ge(s_pe, g - 1)
                    for h in range(H):
                        last = pe.transpose(bank[2 + g % 2][:, P * h:P * h + P], pr[:, g % 2, h], ident)
                    last.then_inc(s_PT, 1)
                g = i - 2
                if 0 <= g < G:
                    pe.wait_ge(s_pe, g + 1)
                    if g >= 1:
                        pe.wait_ge(s_att, g)
                    for h in range(H):
                        last = mm(bank[4][:, HD * h:HD * h + HD], prT[:, g % 2, P * h:P * h + P], vv[:, g, HD * h:HD * h + HD],
                                  start=True, stop=True)
                    last.then_inc(s_O, 1)
                if i % BLK == 2 and i >= 6 and (i - 6) // BLK < NB:
                    q = (i - 6) // BLK
                    pe.wait_ge(s_att, BLK * (q + 1))
                    if q >= 1:
                        pe.wait_ge(s_ae, q)
                    for j in range(BLK):
                        last = pe.transpose(bank[5][:, P * j:P * j + P], att[:, q % 2, j], ident)
                    last.then_inc(s_AT, 1)
                if i % BLK == 3 and i >= 7 and (i - 7) // BLK < NB:
                    q = (i - 7) // BLK
                    if q >= 1:
                        pe.wait_ge(s_res, q)
                    for j in range(BLK):
                        mm(bank[6][:, P * j:P * j + P], group(zT, BLK * q + j), ident, start=(j == 0), stop=False,
                           skip_group_check=True)
                    if q == NB - 1:
                        keep_warm(2, bank[0], mask_flat)
                    pe.wait_ge(s_ae, q + 1)
                    for j in range(BLK):
                        last = mm(bank[6][:, P * j:P * j + P], attT[:, q % 2, P * j:P * j + P], wo[:], start=False,
                                  stop=True, skip_group_check=True)
                    last.then_inc(s_Y, 1)
                if i % BLK == 0 and i >= 12:
                    q = (i - 12) // BLK
                    if q < NB - 1:
                        pe.wait_ge(s_nr1, BLK * (q + 1))
                    else:
                        keep_warm(12, bank[0], mask_flat)
                        pe.wait_ge(s_nr1v, 1)
                    if q >= 1:
                        pe.wait_ge(s_lgc, q)
                    for j in range(BLK):
                        last = pe.transpose(bank[7][:, P * j:P * j + P], nrm[:, q % 2, j], ident)
                    last.then_inc(s_YT, 1)
                if i % BLK == 1 and i >= 13:
                    q = (i - 13) // BLK
                    if q == NB - 1:
                        keep_warm(3, bank[0], mask_flat)
                    pe.wait_ge(s_yT, q + 1)
                    for g in range(BLK * q, BLK * q + BLK):
                        last = mm(bank[7][:, E * (g % BLK):E * (g % BLK) + E], y1T[:, g], wg[:], start=True, stop=True)
                    last.then_inc(s_l1, 1)

            def moe_product(g):
                for i in range(2):
                    last = mm(bank[2 * (g % 4) + i][:], y1T[:, g], W12[:, 512 * i:512 * i + 512], start=True, stop=True)
                last.then_inc(s_ym, 1)

            moe_product(0)
            for g in range(G):
                if g == G - BLK:
                    pe.wait_ge(s_lgc, NB)
                mm(bank[4 + g // BLK][:, P * (g % BLK):P * (g % BLK) + P], y1T[:, g], ident, start=(g % BLK == 0), stop=False,
                   skip_group_check=True)
            pe.wait_ge(s_oh1, 1)
            flat = lambda t: t[:].rearrange("p g e -> p (g e)")
            mm(bank[2][:, 0:P], rowm["row_before"][:], flat(tsum_b), start=True, stop=False)
            mm(bank[2][:, 0:P], rowm["row_same"][:], flat(exb), start=False, stop=False)
            mm(bank[2][:, 0:P], rowm["row_same_before"][:], flat(oh1b), start=False, stop=True).then_inc(s_loc, 1)
            keep_warm(3, bank[3], mask_flat)
            pe.wait_ge(s_gk, 1)
            pe.transpose(bank[3][:, 0:P], flat(gk), ident).then_inc(s_gkp, 1)
            pe.wait_ge(s_gkT, 1)
            pe.wait_ge(s_cblk, 1)
            for blk in range(NB):
                for j in range(BLK):
                    last = mm(bank[4 + blk][:, P * j:P * j + P], gkT[:], cblk[:, BLK * blk + j], start=False, stop=True,
                              skip_group_check=True)
                last.then_inc(s_bp, 1)
                if blk == 0:
                    moe_product(1)
            for g in range(2, G):
                if g < 4:
                    pe.wait_ge(s_base, 2 * g - 2)
                if g >= 4:
                    pe.wait_ge(s_acc, g - 3)
                    pe.wait_ge(s_part, E // 2 * (g - 3))
                moe_product(g)

        @block.vector
        def _(dve):
            v = nc.vector
            chain = [0]

            def link(ins):
                chain[0] += 1
                ins.then_inc(s_dve, 1)
                dve.wait_ge(s_dve, chain[0])

            def row(ap, n):
                return ap.unsqueeze(1).broadcast_to([P, n, ap.shape[-1]])

            def col(ap, n=E):
                return ap.unsqueeze(2).broadcast_to([P, ap.shape[-1], n])

            def first_max(vals, n, top, index, onehot, tmp):
                link(v.tensor_reduce(top, vals, AX.X, ALU.max))
                link(v.tensor_tensor(tmp, vals, col(top), ALU.is_lt))
                link(v.scalar_tensor_tensor(out=tmp, in0=tmp, scalar=float(E), in1=row(K("iota")[:, 0:E], n),
                                            op0=ALU.mult, op1=ALU.add))
                link(v.tensor_reduce(index, tmp, AX.X, ALU.min))
                link(v.tensor_tensor(onehot, row(K("iota")[:, 0:E], n), col(index), ALU.is_equal))

            def row_stats(src, q):
                for j in range(BLK):
                    chain[0] += 1
                    v.bn_stats(st1[:, q % 2, j], src[:, q % 2, j]).then_inc(s_dve, 1)
                return chain[0]

            def row_moments(q, stats):
                dve.wait_ge(s_dve, stats)
                for j in range(BLK):
                    ins = v.bn_aggr(mv1[:, q % 2, j], st1[:, q % 2, j])
                link(ins)
                chain[0] += 1
                v.tensor_scalar(var_e[:, q % 2], mv1[:, q % 2, :, 1], EPS, None, ALU.add).then_inc(s_dve, 1)
                return chain[0]

            def first_guess(q, variances):
                dve.wait_ge(s_dve, variances)
                w = rs1[:, q % 2]
                link(v.tensor_scalar(w.bitcast(I32), var_e[:, q % 2].bitcast(I32), 1, None, ALU.logical_shift_right))
                return v.tensor_scalar(w.bitcast(I32), w.bitcast(I32), -1.0, float(0x5f3759df), ALU.mult, ALU.add)

            def moments(src, q):
                return first_guess(q, row_moments(q, row_stats(src, q)))

            def last_normalise(src, out, q):
                w, z, h = rs1[:, q % 2], newton[:, q % 2], half_var[:, q % 2]
                link(v.tensor_scalar(h, var_e[:, q % 2], -0.5, None, ALU.mult))
                for _ in range(3):
                    link(v.tensor_tensor(z, w, w, ALU.mult))
                    link(v.tensor_tensor(z, z, h, ALU.mult))
                    link(v.scalar_tensor_tensor(out=w, in0=z, scalar=1.5, in1=w, op0=ALU.add, op1=ALU.mult))
                for j in range(BLK):
                    ins = v.tensor_scalar(out[:, q % 2, j], src[:, q % 2, j], mv1[:, q % 2, j, 0:1],
                                          rs1[:, q % 2, j:j + 1], ALU.subtract, ALU.mult)
                return ins

            dve.wait_ge(s_cond, 80)
            def masked(half):
                a, z = E // 2 * half, E // 2 * (half + 1)
                chain[0] += 1
                v.tensor_tensor(cw[:, 1, a:z], cw[:, 0, a:z], row(cmask[:], E // 2), ALU.mult).then_inc(s_dve, 1)

            masked(0)
            dve.wait_ge(s_dve, chain[0])
            for blk in range(NB):
                for e in range(E):
                    if blk == 0 and e == 2:
                        masked(1)
                    for b in (2 * blk, 2 * blk + 1):
                        y = y_bc[:, E * b + e:E * b + e + 1]
                        if e == 0:
                            ins = v.tensor_scalar(wbt[:, b], cw[:, 1, e], y, None, ALU.mult)
                        else:
                            dve.wait_ge(s_dve, chain[0] - 1)
                            ins = v.scalar_tensor_tensor(out=wbt[:, b], in0=cw[:, 1, e], scalar=y, in1=wbt[:, b],
                                                         op0=ALU.mult, op1=ALU.add)
                        chain[0] += 1
                        ins.then_inc(s_dve, 1)
                dve.wait_ge(s_dve, chain[0])
                dve.sem_inc(s_wb, 1)
            yv = y_bc[:].rearrange("p (b e) -> p b e", b=B)
            link(v.tensor_reduce(cs[:, 0], yv, AX.X, ALU.max))
            v.tensor_tensor(cd[:], yv, col(cs[:, 0]), ALU.subtract).then_inc(s_cd, 1)

            def h0_rows_out(blk):
                dve.wait_ge(s_r0p, blk + 1)
                v.tensor_tensor(h0r[:, BLK * blk:BLK * blk + BLK], row_bank[blk][:].rearrange("p (t d) -> p t d", t=BLK),
                                row(cbias_bc, BLK), ALU.add).then_inc(s_h0r, 1)

            h0_rows_out(0)
            h0_rows_out(1)
            dve.wait_ge(s_lgp, NB)
            dve.wait_ge(s_const, 16)
            link(v.tensor_copy(lg[:], bank[4][:, 0:NT * E].rearrange("p (t e) -> p t e", t=NT)))
            first_max(lg[:], NT, mtop[0][:], itop[0][:], oh[0][:], t8[:])
            link(v.scalar_tensor_tensor(out=lgb[:], in0=oh[0][:], scalar=-BIG, in1=lg[:], op0=ALU.mult, op1=ALU.add))
            first_max(lgb[:], NT, mtop[1][:], itop[1][:], oh[1][:], t8[:])
            v.tensor_tensor(taken[:], oh[0][:], oh[1][:], ALU.add).then_inc(s_taken, 1)
            v.tensor_tensor(dlt[:], mtop[1][:], mtop[0][:], ALU.subtract).then_inc(s_dlt, 1)
            h0_rows_out(2)
            h0_rows_out(3)
            dve.wait_ge(s_pre, 1)
            link(v.tensor_copy(tot[:].rearrange("p e t -> p t e"), bank[4][:, 256:384].rearrange("p (t e) -> p t e", t=NT)))
            link(v.tensor_tensor_scan(incl[:].rearrange("p e t -> p (e t)"), K("restart"),
                                      tot[:].rearrange("p e t -> p (e t)"), 0.0, ALU.mult, ALU.add))
            link(v.tensor_scalar(cnt[:, 0], incl[:, :, NT - 1], float(P - 1), None, ALU.add))
            link(v.tensor_copy(cnt_i[:], cnt[:, 0]))
            link(v.tensor_scalar(cnt_i[:], cnt_i[:], -P, None, ALU.bitwise_and))
            link(v.tensor_copy(cnt[:, 2], cnt_i[:]))
            link(v.tensor_tensor_scan(cnt[:, 3], K("ones")[:, 0:E], cnt[:, 2], 0.0, ALU.mult, ALU.add))
            link(v.tensor_tensor(cnt[:, 4], cnt[:, 3], cnt[:, 2], ALU.subtract))
            link(v.tensor_tensor(excl[:], incl[:], tot[:], ALU.subtract))
            link(v.tensor_tensor(Q[:], bank[4][:, 128:256].rearrange("p (t e) -> p t e", t=NT),
                                 excl[:].rearrange("p e t -> p t e"), ALU.add))
            link(v.tensor_tensor(Q[:], Q[:], row(cnt[:, 4], NT), ALU.add))
            for k in range(2):
                link(v.tensor_tensor(t8[:], oh[k][:], Q[:], ALU.mult))
                link(v.tensor_reduce(pos[:, k], t8[:], AX.X, ALU.add))
            link(v.tensor_copy(pos_u[:], pos[:]))
            flat_pos = pos_u[:].rearrange("p k t -> p (k t)")
            v.tensor_scalar(lo_i[:], flat_pos, P - 1, None, ALU.bitwise_and)
            link(v.tensor_scalar(hi_i[:], flat_pos, P.bit_length() - 1, None, ALU.logical_shift_right))
            v.tensor_copy(lo[:], lo_i[:])
            link(v.tensor_copy(hi[:], hi_i[:]))
            v.tensor_tensor(ohlo, row(K("iota"), 2 * NT), col(lo[:], P), ALU.is_equal)
            link(v.tensor_tensor(ohhi[:], row(K("iota")[:, 0:SLOT_TILES], 2 * NT), col(hi[:], SLOT_TILES), ALU.is_equal))
            link(v.tensor_tensor(ohhi[:].rearrange("p (k t) s -> p k t s", k=2), ohhi[:].rearrange("p (k t) s -> p k t s", k=2),
                                 K("token").unsqueeze(1).unsqueeze(3).broadcast_to([P, 2, NT, SLOT_TILES]), ALU.mult))
            dve.sem_inc(s_onehot, 1)
            dve.sem_inc(s_pos, 1)
            link(v.tensor_tensor(cmp[:], row(cnt[:, 3], SLOT_TILES), col(K("tile_start")), ALU.is_le))
            link(v.tensor_reduce(ecnt[:], cmp[:], AX.X, ALU.add))
            link(v.tensor_scalar(ecnt[:], ecnt[:], float(E - 1), None, ALU.min))
            link(v.tensor_copy(eslot[:], ecnt[:]))
            dve.wait_ge(s_tab, 1)
            v.tensor_copy(slot_tok[:], bank[4][:, 384:384 + SLOT_TILES]).then_inc(s_slots, 1)

            def token_weights():
                dve.wait_ge(s_edl, 1)
                link(v.tensor_scalar(sdl[:], edl[:], 1.0, None, ALU.add))
                link(v.reciprocal(pk[:, 0], sdl[:]))
                link(v.tensor_tensor(pk[:, 1], edl[:], pk[:, 0], ALU.mult))

            def row_softmax():
                dve.wait_ge(s_ce, 1)
                link(v.tensor_reduce(cs[:, 1], ce[:], AX.X, ALU.add))
                link(v.reciprocal(cs[:, 2], cs[:, 1]))
                link(v.tensor_tensor(rw[:], ce[:], col(cs[:, 2]), ALU.mult))

            def row_first_expert():
                first_max(rw[:], B, cs[:, 3], cs[:, 4], coh[:], c8[:])
                link(v.tensor_copy(cix[:, 0], cs[:, 4]))
                link(v.scalar_tensor_tensor(out=rwb[:], in0=coh[:], scalar=-BIG, in1=rw[:], op0=ALU.mult, op1=ALU.add))

            def row_second_expert():
                first_max(rwb[:], B, cs[:, 5], cs[:, 4], coh[:], c8[:])
                link(v.tensor_copy(cix[:, 1], cs[:, 4]))
                dve.sem_inc(s_cr, 1)

            def row_weights():
                link(v.tensor_tensor(cs[:, 6], cs[:, 3], cs[:, 5], ALU.add))
                link(v.reciprocal(cs[:, 7], cs[:, 6]))
                for k, m in enumerate((3, 5)):
                    link(v.tensor_tensor(cs[:, m], cs[:, m], cs[:, 7], ALU.mult))
                    link(v.tensor_scalar(cs[:, 6], cs[:, m], SKILL_SCALE, None, ALU.mult))
                    link(v.scalar_tensor_tensor(out=cwt[:, k], in0=cs[:, m], scalar=1.0 - SKILL_SCALE, in1=cs[:, 6],
                                                op0=ALU.mult, op1=ALU.add))

            def xgT_copy(j, r, ring):
                dve.wait_ge(s_X, j + 1)
                if ring:
                    dve.wait_ge(s_G, j - 1)
                v.tensor_copy(xgT[:, r], bank[6][:, 0:P]).then_inc(s_xe, 1)

            def hidden(j, r, ring):
                dve.wait_ge(s_sl, j + 1)
                if ring:
                    dve.wait_ge(s_H, j - 1)
                v.tensor_tensor(hid[:, r, 0:F0], slu[:, r], bank[2 * r + 1][:, 0:F0], ALU.mult).then_inc(s_hm, 1)

            def y_copy(j, r4, stored):
                dve.wait_ge(s_D, j + 1)
                if stored is not None:
                    dve.wait_ge(s_yst[r4], stored)
                v.tensor_copy(ysb[:, r4], bank[7][:, 0:P]).then_inc(s_ye, 1)

            steps = ROUNDS - 2
            experts_at = lambda i: ecnt[:, bass.ds(1 + i, steps, step=4)]
            link(v.scalar_tensor_tensor(out=words[:, 1:], in0=experts_at(6), scalar=float(E), in1=experts_at(5),
                                        op0=ALU.mult, op1=ALU.add))
            for i in reversed(range(5)):
                link(v.scalar_tensor_tensor(out=words[:, 1:], in0=words[:, 1:], scalar=float(E), in1=experts_at(i),
                                            op0=ALU.mult, op1=ALU.add))
            v.tensor_copy(words_i[:, 1:], words[:, 1:]).then_inc(s_words, 1)
            row_softmax()

            def b1_by_w2(e, c):
                b1_col = b1[:, bass.ds(e, 1), c]
                out = b1w2[:, bass.ds(e, 1), :].rearrange("p a d -> p (a d)")
                w2_rows = w12in[:, 1, bass.ds(e, 1), c, :].rearrange("p a d -> p (a d)")
                if c == 0:
                    ins = v.tensor_scalar(out, w2_rows, b1_col, None, ALU.mult)
                else:
                    dve.wait_ge(s_b1w2, e * C2 + c)
                    ins = v.scalar_tensor_tensor(out=out, in0=w2_rows, scalar=b1_col, in1=out, op0=ALU.mult, op1=ALU.add)
                ins.then_inc(s_b1w2, 1)

            dve.wait_ge(s_fold, 64)
            dve.wait_ge(s_hpad, 1)
            xgT_copy(0, 0, False)
            for j in range(4):
                xgT_copy(j + 1, (j + 1) % 2, j >= 1)
                hidden(j, j % 2, j >= 2)
                if j >= 2:
                    y_copy(j - 2, j - 2, None)
                (row_first_expert, row_second_expert, row_weights, token_weights)[j]()
            for j in range(4, 6):
                xgT_copy(j + 1, (j + 1) % 2, True)
                hidden(j, j % 2, True)
                y_copy(j - 2, j - 2, None)
            with dve.Fori(1, ROUNDS - 1) as jj:
                for u in range(4):
                    j = jj * 4 + (u + 2)
                    xgT_copy(j + 1, (u + 1) % 2, True)
                    hidden(j, u % 2, True)
                    y_copy(j - 2, u, jj * 16)
                    b1_by_w2(jj - 1, u)
            for j in range(4 * (ROUNDS - 1) + 2, SLOT_TILES + 2):
                if j + 1 < SLOT_TILES:
                    xgT_copy(j + 1, (j + 1) % 2, True)
                if j < SLOT_TILES:
                    hidden(j, j % 2, True)
                y_copy(j - 2, (j - 2) % 4, 16 * ((j - 2) // 4))

            def x1_row(b, par, stored):
                dve.wait_ge(s_yg[par], stored["gathered"])
                for i in range(2):
                    t = b * 2 + i
                    v.scalar_tensor_tensor(out=half1[:, i], in0=yg[:, par, i, 0], scalar=stored["p"](0, t),
                                           in1=stored["xs"](t), op0=ALU.mult, op1=ALU.add).then_inc(s_half, 1)
                if stored["old"] is not None:
                    dve.wait_ge(s_x1p, stored["old"])
                    dve.wait_ge(s_x1st, stored["old"] * 16)
                for i in range(2):
                    t = b * 2 + i
                    dve.wait_ge(s_half, b * 2 + i + 1)
                    ins = v.scalar_tensor_tensor(out=x1t[:, par, i], in0=yg[:, par, i, 1], scalar=stored["p"](1, t),
                                                 in1=half1[:, i], op0=ALU.mult, op1=ALU.add)
                    ins.then_inc(s_x1h, 1)
                dve.wait_ge(s_x1h, b * 2 + 2)
                dve.sem_inc(s_x1, 1)

            def x1_lo(b, par):
                dve.wait_ge(s_x1T, b + 1)
                v.tensor_tensor(x1T_lo[:, par], bank[6 + par][:, 0:N], x1T_hi[:, par].bitcast(F32),
                                ALU.subtract).then_inc(s_x1lo, 1)

            def split_lo(b, k, raw, done):
                dve.wait_ge(s_whi[k], b + 1)
                v.tensor_tensor(w_lo[k][:], raw[:, 0:2 * F1], w_hi[k][:].bitcast(F32), ALU.subtract).then_inc(done, 1)

            def hid_lo(b, hh, ring):
                dve.wait_ge(s_hhi, b * 6 + (hh + 1))
                if ring:
                    dve.wait_ge(s_dn, b * 6 + (hh - 1))
                v.tensor_tensor(hb_lo[:, hh % 2], hb[:, hh % 2], hb_hi[:, hh % 2].bitcast(F32),
                                ALU.subtract).then_inc(s_hlo, 1)

            def row_args(b, gathered, old):
                if isinstance(b, int):
                    return dict(gathered=gathered, old=old, p=lambda k, t: pk[:, k, t:t + 1], xs=lambda t: xs[:, t])
                return dict(gathered=gathered, old=old, p=lambda k, t: pk[:, k, bass.ds(t, 1)],
                            xs=lambda t: xs[:, bass.ds(t, 1), :].rearrange("p a d -> p (a d)"))

            def gemma_hid(b, hh, ring):
                k = hh // 2
                dve.wait_ge(s_gl, b * 6 + (hh + 1))
                if ring:
                    dve.wait_ge(s_hlo, b * 6 + (hh - 1))
                if k < 2:
                    w = cwt[:, k, b:b + 1] if isinstance(b, int) else cwt[:, k, bass.ds(b, 1)]
                    ins = v.scalar_tensor_tensor(out=hb[:, hh % 2], in0=gl[:, hh % 2], scalar=w,
                                                 in1=bank[2 + hh % 2][:], op0=ALU.mult, op1=ALU.mult)
                else:
                    ins = v.tensor_tensor(hb[:, hh % 2], gl[:, hh % 2], bank[2 + hh % 2][:], ALU.mult)
                ins.then_inc(s_m1, 1)

            def dve_row(b, par, gathered, old, first=False, last=False):
                for hh in range(6):
                    if hh > 0:
                        hid_lo(b, hh - 1, not (first and hh <= 2))
                    elif not first:
                        hid_lo(b - 1, 5, True)
                    gemma_hid(b, hh, not (first and hh < 2))
                    if hh == 2 and not last:
                        x1_row(b + 1, 1 - par, row_args(b, gathered, old))
                    if hh == 3 and not last:
                        split_lo(b + 1, 0, wk[0], s_wlo[0])
                    if hh == 4 and not last:
                        x1_lo(b + 1, 1 - par)

            for k, raw in enumerate((*wk, wsh)):
                split_lo(0, k, raw, s_lo0)
                dve.wait_ge(s_dhi[k], 1)
                v.tensor_tensor(d_lo[k][:], raw[:, 2 * F1:], d_hi[k][:].bitcast(F32), ALU.subtract).then_inc(s_lo0, 1)
            dve.wait_ge(s_xs, NB)
            x1_row(0, 0, row_args(0, 64, None))
            dve.wait_ge(s_cp, 1)
            v.tensor_tensor(c_e[:], bank[5][0:E, 0:D], b2[:], ALU.add).then_inc(s_c8, 1)
            x1_lo(0, 0)
            dve_row(0, 0, 64, None, first=True)
            dve_row(1, 1, 128, 1)
            with dve.Fori(1, B // 2 - 1) as bp:
                dve_row(bp * 2, 0, bp * 64 + 64, bp * 2)
                dve_row(bp * 2 + 1, 1, bp * 64 + 128, bp * 2 + 1)
            dve_row(B - 2, 0, 64 * (B // 2), B - 2)
            dve_row(B - 1, 1, None, None, last=True)
            hid_lo(B - 1, 5, True)

            dve.wait_ge(s_attw, 80)
            v.tensor_scalar(bq_s[:], bqkv[:, 0:1], HD ** -0.5, None, ALU.mult).then_inc(s_bq, 1)
            for blk in range(NB):
                dve.wait_ge(s_qkp, blk + 1)
                dve.wait_ge(s_kz0, G)
                for h in range(2, 4):
                    a = HD * h
                    v.tensor_scalar(
                        kz[a:a + HD, BLK * blk:BLK * blk + BLK, h, :],
                        bank[2 * (blk % 2) + 1][a:a + HD, :].rearrange("p (g k) -> p g k", g=BLK),
                        bqkv[a:a + HD, 1:2], None, ALU.add).then_inc(s_kk, 1)
                dve.wait_ge(s_V, blk + 1)
                v.tensor_tensor(vv[:, BLK * blk:BLK * blk + BLK], bank[4 + blk % 2][:].rearrange("p (t d) -> p t d", t=BLK),
                                row(bv_bc, BLK), ALU.add).then_inc(s_vv, 1)
            for i in range(G + 10):
                g = i
                if g < G:
                    dve.wait_ge(s_S, g + 1)
                    if g >= 2:
                        dve.wait_ge(s_pr, H * (g - 1))
                    v.tensor_reduce(nmax[:, g % 2], bank[g % 2][:].rearrange("p (h k) -> p h k", h=H), AX.X, ALU.max,
                                    negate=True).then_inc(s_nm, 1)
                g = i - 1
                if 0 <= g < G:
                    dve.wait_ge(s_pr, H * (g + 1))
                    if g >= 2:
                        dve.wait_ge(s_att, g - 1)
                    v.reciprocal(rden[:, g % 2], den[:, g % 2]).then_inc(s_rd, 1)
                    dve.wait_ge(s_PT, g + 1)
                    if g >= 2:
                        dve.wait_ge(s_O, g - 1)
                    v.tensor_copy(prT[:, g % 2], bank[2 + g % 2][:]).then_inc(s_pe, 1)
                if i % BLK == 0 and 8 <= i < G + BLK:
                    stats = row_stats(res, (i - 8) // BLK)
                g = i - 2
                if 0 <= g < G:
                    dve.wait_ge(s_O, g + 1)
                    dve.wait_ge(s_rd, g + 1)
                    if g >= 2 * BLK:
                        dve.wait_ge(s_AT, g // BLK - 1)
                    v.tensor_tensor(att[:, (g // BLK) % 2, g % BLK].rearrange("p (h d) -> p h d", h=H),
                                    bank[4][:, 0:P].rearrange("p (h d) -> p h d", h=H),
                                    col(rden[:, g % 2], HD), ALU.mult).then_inc(s_att, 1)
                if i % BLK == 0 and 8 <= i < G + BLK:
                    variances = row_moments((i - 8) // BLK, stats)
                    first_guess((i - 8) // BLK, variances).then_inc(s_seed, 1)
                if i % BLK == 3 and i >= 7 and (i - 7) // BLK < NB:
                    q = (i - 7) // BLK
                    dve.wait_ge(s_Y, q + 1)
                    if q >= 2:
                        dve.wait_ge(s_nr1, BLK * (q - 1))
                    link(v.tensor_tensor(res[:, q % 2], bank[6][:].rearrange("p (g d) -> p g d", g=BLK),
                                         row(bo_bc, BLK), ALU.add))
                    dve.sem_inc(s_res, 1)
                    if q == NB - 1:
                        link(moments(res, q))
                        last_normalise(res, nrm, q).then_inc(s_nr1v, 1)
                if i % BLK == 1 and i >= 13:
                    q = (i - 13) // BLK
                    dve.wait_ge(s_l1, q + 1)
                    v.tensor_copy(lg1[:, BLK * q:BLK * q + BLK], bank[7][:, 0:BLK * E].rearrange(
                        "p (g e) -> p g e", g=BLK)).then_inc(s_lgc, 1)

            dve.wait_ge(s_lgc, NB)
            link(v.tensor_reduce(sm1[:, 0], lg1[:], AX.X, ALU.max))
            v.tensor_tensor(t8[:], lg1[:], col(sm1[:, 0]), ALU.subtract).then_inc(s_gap1, 1)
            dve.wait_ge(s_e1, 1)
            first_max(e1[:], G, sm1[:, 1], sm1[:, 2], oh1[:], Q[:])
            link(v.tensor_copy(oh1b[:], oh1[:]))
            by_e = oh1[:].rearrange("p g e -> p e g")
            link(v.tensor_copy(tot[:], by_e))
            link(v.tensor_tensor_scan(incl[:].rearrange("p e t -> p (e t)"), K("restart"),
                                      tot[:].rearrange("p e t -> p (e t)"), 0.0, ALU.mult, ALU.add))
            link(v.tensor_tensor(exb[:].rearrange("p g e -> p e g"), incl[:], tot[:], ALU.subtract))
            link(v.tensor_copy(tsum_b[:], row(incl[:, :, G - 1], G)))
            dve.sem_inc(s_oh1, 1)
            link(v.tensor_reduce(sm1[:, 3], e1[:], AX.X, ALU.add))
            link(v.reciprocal(sm1[:, 4], sm1[:, 3]))
            link(v.tensor_tensor(sm1[:, 4], sm1[:, 4], sm1[:, 1], ALU.mult))
            dve.wait_ge(s_loc, 1)
            link(v.tensor_tensor(t8[:], bank[2][:, 0:P].rearrange("p (g e) -> p g e", g=G), oh1[:], ALU.mult))
            link(v.tensor_reduce(sm1[:, 5], t8[:], AX.X, ALU.add))
            link(v.tensor_scalar(sm1[:, 5], sm1[:, 5], float(CAP), None, ALU.is_lt))
            link(v.tensor_tensor(sm1[:, 4], sm1[:, 4], sm1[:, 5], ALU.mult))
            v.tensor_tensor(gk[:], oh1[:], col(sm1[:, 4]), ALU.mult).then_inc(s_gk, 1)
            dve.wait_ge(s_gk, 1)
            for p in range(G // 2):
                q = p // 2
                dve.wait_ge(s_base, q + 1)
                dve.wait_ge(s_ym, 2 * p + 2)
                if q >= 2 and p % 2 == 0:
                    dve.wait_ge(s_nr2, BLK * (q - 1))
                for e in range(E // 2):
                    for g in (2 * p, 2 * p + 1):
                        if e > 0:
                            dve.wait_ge(s_dve, chain[0] - 1)
                        acc = macc[:, q % 2, g % BLK]
                        ins = v.scalar_tensor_tensor(
                            out=acc, in0=bank[2 * (g % 4)][:, D * e:D * e + D], scalar=gk[:, g, e:e + 1],
                            in1=base[:, g] if e == 0 else acc, op0=ALU.mult, op1=ALU.add)
                        chain[0] += 1
                        ins.then_inc(s_dve, 1)
                dve.wait_ge(s_psum, p + 1)
                for g in (2 * p, 2 * p + 1):
                    dve.wait_ge(s_dve, chain[0] - 1 + g % 2)
                    acc = macc[:, q % 2, g % BLK]
                    v.tensor_tensor(acc, acc, part[:, g % 4, 0], ALU.add).then_inc(s_acc, 1)
                if p % 2:
                    dve.wait_ge(s_acc, 2 * p + 2)
                    if q < NB - 1:
                        moments(macc, q).then_inc(s_seed2, 1)
            link(moments(macc, NB - 1))
            q = NB - 1
            dve.wait_ge(s_fo, q - 1)
            link(last_normalise(macc, nrm2, q))
            dve.wait_ge(s_fst[q % 2], 16 * BLK * (q // 2))
            dve.wait_ge(s_xb, 1)
            for j in range(BLK):
                v.tensor_tensor(nrg2[:, q % 2, j], nrm2[:, q % 2, j], g2_bc, ALU.mult).then_inc(s_dve, 1)
                chain[0] += 1
            for j in range(BLK):
                dve.wait_ge(s_dve, chain[0] - BLK + 1 + j)
                v.tensor_tensor(fin[:, q % 2, j], nrg2[:, q % 2, j], x1g[:, BLK * q + j], ALU.add).then_inc(s_fov, 1)


def kernel(**a):
    import concourse.bacc as bacc
    from concourse.bass_utils import run_bass_kernel_spmd

    a = {k: np.asarray(v) for k, v in a.items()}
    x = a["x"].reshape(T, D)

    def chunked(w, p=P):
        w = w.reshape(*w.shape[:-2], w.shape[-2] // p, p, w.shape[-1])
        return np.moveaxis(w, -2, 0)

    wd = np.zeros((P, E, 3, D), np.float32)
    wd[:, :, 0:2] = chunked(a["L0_ffn_Wd"][:, 0:2 * P])
    wd[0:F0 - 2 * P, :, 2] = np.moveaxis(a["L0_ffn_Wd"][:, 2 * P:], 1, 0)

    def gemma(gate, up, down):
        d = np.moveaxis(down.reshape(-1, C1, P, D), 2, 1).reshape(-1, P, C1 * D)
        return np.concatenate([gate.reshape(-1, D, F1), up.reshape(-1, D, F1), d], axis=2)

    c = {k[3:]: v for k, v in a.items() if k.startswith("L1_")}
    ins = {
        "xT": x.T,
        "x_rows": x,
        "cond": a["cond_8"],
        "cw": a["L0_cond_weight"].transpose(2, 0, 1),
        "cmask": a["L0_cond_mask"].T,
        "cbias": a["L0_cond_bias"].reshape(D, 1),
        "vecs": np.stack([a["L0_cond_bias"], c["ffn_in_proj_b"][2 * D:], c["ffn_out_proj_b"], c["ffn_ln2_g"],
                          c["ffn_ln2_b"]]),
        "consts": shape_constants(),
        "gate_w": a["L0_ffn_gate_w"],
        "wgu": np.moveaxis(np.concatenate([a["L0_ffn_Wg"], a["L0_ffn_Wu"]], axis=2), 1, 0).reshape(D, E * 2 * F0),
        "wd": wd,
        "sgu": np.concatenate([a["L0_ffn_Sg"], a["L0_ffn_Su"]], axis=1),
        "sd": chunked(a["L0_ffn_Sd"], SC),
        "wexp": gemma(c["cond_skill_gate"], c["cond_skill_up"], c["cond_skill_down"]),
        "wsh": gemma(c["cond_shared_gate"], c["cond_shared_up"], c["cond_shared_down"])[0],
        "w1": chunked(c["ffn_w1"].transpose(0, 2, 1)),
        "w2": chunked(c["ffn_w2"]),
        "b1": c["ffn_b1"].reshape(E, C2, P).transpose(2, 0, 1),
        "b2": c["ffn_b2"],
        "wqkv": c["ffn_in_proj_w"].T,
        "wo": c["ffn_out_proj_w"].T,
        "bqkv": c["ffn_in_proj_b"].reshape(3, D).T,
        "wg": c["ffn_wg"],
        "cols1": np.stack([c["ffn_ln1_g"], c["ffn_ln1_b"]], axis=1),
    }
    nc = bacc.Bacc("TRN2", target_bir_lowering=False, num_devices=1)
    arrays, args = {}, []
    for name, v in ins.items():
        v = np.ascontiguousarray(v)
        arrays[f"in_{name}"] = v
        args.append(nc.dram_tensor(f"in_{name}", v.shape, mybir.dt.from_np(v.dtype), kind="ExternalInput").ap())
    args.append(nc.dram_tensor("out", [B, N, D], F32, kind="ExternalOutput").ap())
    block_kernel(nc, *args)
    r = run_bass_kernel_spmd(nc, [arrays], core_ids=[0])
    return r.results[0]["out"]
```
